# Optimizing a Trainium2 kernel written in Bass

```python
import numpy as np
import jax
import jax.numpy as jnp

def _softmax(x, axis=-1):
    return jax.nn.softmax(x, axis=axis)

def _gelu(x):
    return jax.nn.gelu(x, approximate=True)

def _silu(x):
    return jax.nn.silu(x)

def _sigmoid(x):
    return jax.nn.sigmoid(x)

def _layernorm(x, axis=-1, eps=1e-05):
    m = jnp.mean(x, axis=axis, keepdims=True)
    v = jnp.var(x, axis=axis, keepdims=True)
    return (x - m) / jnp.sqrt(v + eps)

def _scatter_add(tgt, idx, src, axis=0):
    return tgt.at[idx].add(src)

def _segment_sum(src, seg, n):
    return jax.ops.segment_sum(src, seg, n)
kernel_name = 'mk_gps_d2_gnn_r8_7fe35a'

def setup_inputs(seed: int=0):
    np.random.seed(seed)
    _w = jnp.asarray

    def _rec_inputs():
        import jax
        import jax.numpy as jnp
        _gk = jax.random.key(seed)
        x = -0.0006008 + 1.001 * jax.random.normal(jax.random.fold_in(_gk, 1), (6250, 256), jnp.float32)
        src = jax.random.randint(jax.random.fold_in(_gk, 2), (100000,), 0, 6250, jnp.int32)
        dst = jax.random.randint(jax.random.fold_in(_gk, 3), (100000,), 0, 6250, jnp.int32)
        _o = jnp.argsort(dst, stable=True)
        src = src[_o]
        dst = dst[_o]
        return (x, src, dst)
    x, src, dst = _rec_inputs()

    def _L0_gnn_setup():
        import jax, jax.numpy as jnp
        import numpy as np
        N = 1250
        E = 40000
        D = 256

        def gine_conv(x, edge_index, w1, b1, w2, b2):
            src, dst = (edge_index[0], edge_index[1])
            msg = jax.nn.relu(x[src])
            agg = jax.ops.segment_sum(msg, dst, num_segments=x.shape[0])
            h = x + agg
            h = jax.nn.relu(h @ w1 + b1)
            return h @ w2 + b2
        key = jax.random.key(seed)
        ks = jax.random.split(key, 10)
        s = 1.0 / np.sqrt(D)
        inp = {'x': jax.random.normal(ks[0], (N, D), dtype=jnp.float32), 'edge_index': jax.random.randint(ks[1], (2, E), 0, N, dtype=jnp.int64), 'w11': jax.random.uniform(ks[2], (D, D), jnp.float32, -s, s), 'b11': jnp.zeros((D,), jnp.float32), 'w12': jax.random.uniform(ks[3], (D, D), jnp.float32, -s, s), 'b12': jnp.zeros((D,), jnp.float32), 'w21': jax.random.uniform(ks[4], (D, D), jnp.float32, -s, s), 'b21': jnp.zeros((D,), jnp.float32), 'w22': jax.random.uniform(ks[5], (D, D), jnp.float32, -s, s), 'b22': jnp.zeros((D,), jnp.float32)}
        return inp
    _L0_gnn_all = _L0_gnn_setup()
    _L0_gnn_in = {k: v for k, v in _L0_gnn_all.items() if k in ('w11', 'b11', 'w12', 'b12', 'w21', 'b21', 'w22', 'b22')}
    del _L0_gnn_all

    def _L0_mix_setup():
        import jax, jax.numpy as jnp
        import numpy as np
        import math
        EMBED = 256
        HEADS = 4
        HEAD_DIM = EMBED // HEADS
        OUT_DIM = 256
        LN_EPS = 1e-05

        def _qkv_init(key):
            spread = math.sqrt(3.0 / EMBED)
            gain, delta = (0.01, 0.01)
            w = jax.random.uniform(key, (EMBED, EMBED), minval=-spread, maxval=spread) * gain
            return w + delta * jnp.eye(EMBED, dtype=w.dtype)

        def _layer_norm(x, g, b):
            mu = jnp.mean(x, axis=-1, keepdims=True)
            var = jnp.mean(jnp.square(x - mu), axis=-1, keepdims=True)
            return (x - mu) * jax.lax.rsqrt(var + LN_EPS) * g + b

        def _split_heads(x, B, S):
            return x.reshape(B, S, HEADS, HEAD_DIM).transpose(0, 2, 1, 3)
        key = jax.random.key(seed)
        ks = jax.random.split(key, 6)
        seq = jax.random.normal(ks[0], (4, 1024, EMBED), dtype=jnp.float32)
        wq = _qkv_init(ks[1])
        wk = _qkv_init(ks[2])
        wv = _qkv_init(ks[3])
        bound = 1.0 / math.sqrt(EMBED)
        wo = jax.random.uniform(ks[4], (OUT_DIM, EMBED), minval=-bound, maxval=bound)
        bo = jax.random.uniform(ks[5], (OUT_DIM,), minval=-bound, maxval=bound)
        ln_k_g = jnp.ones((HEAD_DIM,), jnp.float32)
        ln_k_b = jnp.zeros((HEAD_DIM,), jnp.float32)
        ln_v_g = jnp.ones((HEAD_DIM,), jnp.float32)
        ln_v_b = jnp.zeros((HEAD_DIM,), jnp.float32)
        return {'seq': seq, 'wq': wq, 'wk': wk, 'wv': wv, 'wo': wo, 'bo': bo, 'ln_k_g': ln_k_g, 'ln_k_b': ln_k_b, 'ln_v_g': ln_v_g, 'ln_v_b': ln_v_b}
    _L0_mix_all = _L0_mix_setup()
    _L0_mix_in = {k: v for k, v in _L0_mix_all.items() if k in ('wq', 'wk', 'wv', 'wo', 'bo', 'ln_k_g', 'ln_k_b', 'ln_v_g', 'ln_v_b')}
    del _L0_mix_all

    def _L0_ffn_setup():
        import jax, jax.numpy as jnp
        import numpy as np
        IN_CH = 256
        OUT_CH = 256
        key = jax.random.key(seed)
        kx, kw, kb = jax.random.split(key, 3)
        x = jax.random.normal(kx, (8, 512, IN_CH), dtype=jnp.float32)
        bound = 1.0 / np.sqrt(IN_CH)
        weight = jax.random.uniform(kw, (OUT_CH, IN_CH), dtype=jnp.float32, minval=-bound, maxval=bound)
        bias = jax.random.uniform(kb, (OUT_CH,), dtype=jnp.float32, minval=-bound, maxval=bound)
        return {'x': x, 'weight': weight, 'bias': bias}
    _L0_ffn_all = _L0_ffn_setup()
    _L0_ffn_in = {k: v for k, v in _L0_ffn_all.items() if k in ('weight', 'bias')}
    del _L0_ffn_all

    def _L1_gnn_setup():
        import jax, jax.numpy as jnp
        import numpy as np
        N_NODES = 6250
        N_EDGES = 200000
        IN_DIM, OUT_DIM, N_HEADS = (256, 64, 4)
        EPS = 1e-12
        key = jax.random.key(seed)
        k1, k2, k3, k4, k5 = jax.random.split(key, 5)
        h = jax.random.normal(k1, (N_NODES, IN_DIM), dtype=jnp.float32)
        edge_index = jax.random.randint(k2, (2, N_EDGES), 0, N_NODES, dtype=jnp.int32)
        W = jax.random.normal(k3, (IN_DIM, OUT_DIM), dtype=jnp.float32) * 0.05
        Wl = jax.random.normal(k4, (N_HEADS, OUT_DIM), dtype=jnp.float32) * 0.05
        Wr = jax.random.normal(k5, (N_HEADS, OUT_DIM), dtype=jnp.float32) * 0.05
        b = jnp.zeros((OUT_DIM,), dtype=jnp.float32)
        return {'h': h, 'W': W, 'Wl': Wl, 'Wr': Wr, 'b': b, 'edge_index': edge_index}
    _L1_gnn_all = _L1_gnn_setup()
    _L1_gnn_in = {k: v for k, v in _L1_gnn_all.items() if k in ('W', 'Wl', 'Wr', 'b')}
    del _L1_gnn_all

    def _L1_mix_setup():
        import jax, jax.numpy as jnp
        import numpy as np
        EPS_NORM = 1e-06
        EPS_ATTN = 1e-06
        HEADS = 8

        def rmsnorm(x, w):
            ms = jnp.mean(x * x, axis=-1, keepdims=True)
            return w * (x * jax.lax.rsqrt(ms + EPS_NORM))

        def linear_attention(x, w_qkv, w_out, b_out):
            B, N, D = x.shape
            hd = D // HEADS
            qkv = (x @ w_qkv).reshape(B, N, 3, HEADS, hd)
            q, k, v = (qkv[:, :, 0], qkv[:, :, 1], qkv[:, :, 2])
            q = jax.nn.elu(q) + 1.0
            k = jax.nn.elu(k) + 1.0
            kv = jnp.einsum('bnhd,bnhm->bhdm', k, v)
            z = 1.0 / (jnp.einsum('bnhd,bhd->bnh', q, k.sum(axis=1)) + EPS_ATTN)
            out = jnp.einsum('bnhd,bhdm,bnh->bnhm', q, kv, z)
            out = out.reshape(B, N, D)
            return out @ w_out + b_out
        key = jax.random.key(seed)
        ks = jax.random.split(key, 4)
        B, N, D = (16, 1024, 256)
        x = jax.random.normal(ks[0], (B, N, D), dtype=jnp.float32)
        w_norm1 = jnp.ones((D,), dtype=jnp.float32)
        w_qkv = jax.random.normal(ks[1], (D, 3 * D), dtype=jnp.float32) * 0.02
        w_out = jax.random.normal(ks[2], (D, D), dtype=jnp.float32) * 0.02
        b_out = jnp.zeros((D,), dtype=jnp.float32)
        w_norm2 = jnp.ones((D,), dtype=jnp.float32)
        return {'x': x, 'w_norm1': w_norm1, 'w_qkv': w_qkv, 'w_out': w_out, 'b_out': b_out, 'w_norm2': w_norm2}
    _L1_mix_all = _L1_mix_setup()
    _L1_mix_in = {k: v for k, v in _L1_mix_all.items() if k in ('w_norm1', 'w_qkv', 'w_out', 'b_out', 'w_norm2')}
    del _L1_mix_all

    def _L1_ffn_setup():
        import jax, jax.numpy as jnp
        import numpy as np
        E = 8
        K = 2
        D = 256
        H = 512
        DOUT = 256
        EPS = 1e-05
        key = jax.random.key(seed)
        ks = jax.random.split(key, 9)
        s = 0.02
        return {'x': jax.random.normal(ks[0], (4, 1024, D), jnp.float32), 'gamma': 1.0 + 0.05 * jax.random.normal(ks[1], (D,), jnp.float32), 'beta': 0.05 * jax.random.normal(ks[2], (D,), jnp.float32), 'Wr': 0.01 * jax.random.normal(ks[3], (D, E), jnp.float32), 'br': jnp.zeros((E,), jnp.float32), 'W1': s * jax.random.normal(ks[4], (E, D, H), jnp.float32), 'b1': s * jax.random.normal(ks[5], (E, H), jnp.float32), 'W2': s * jax.random.normal(ks[6], (E, H, DOUT), jnp.float32), 'b2': s * jax.random.normal(ks[7], (E, DOUT), jnp.float32)}
    _L1_ffn_all = _L1_ffn_setup()
    _L1_ffn_in = {k: v for k, v in _L1_ffn_all.items() if k in ('gamma', 'beta', 'Wr', 'br', 'W1', 'b1', 'W2', 'b2')}
    del _L1_ffn_all
    return {'x': x, 'src': src, 'dst': dst, 'L0_gnn_w11': _L0_gnn_in['w11'], 'L0_gnn_b11': _L0_gnn_in['b11'], 'L0_gnn_w12': _L0_gnn_in['w12'], 'L0_gnn_b12': _L0_gnn_in['b12'], 'L0_gnn_w21': _L0_gnn_in['w21'], 'L0_gnn_b21': _L0_gnn_in['b21'], 'L0_gnn_w22': _L0_gnn_in['w22'], 'L0_gnn_b22': _L0_gnn_in['b22'], 'L0_mix_wq': _L0_mix_in['wq'], 'L0_mix_wk': _L0_mix_in['wk'], 'L0_mix_wv': _L0_mix_in['wv'], 'L0_mix_wo': _L0_mix_in['wo'], 'L0_mix_bo': _L0_mix_in['bo'], 'L0_mix_ln_k_g': _L0_mix_in['ln_k_g'], 'L0_mix_ln_k_b': _L0_mix_in['ln_k_b'], 'L0_mix_ln_v_g': _L0_mix_in['ln_v_g'], 'L0_mix_ln_v_b': _L0_mix_in['ln_v_b'], 'L0_ffn_weight': _L0_ffn_in['weight'], 'L0_ffn_bias': _L0_ffn_in['bias'], 'L1_gnn_W': _L1_gnn_in['W'], 'L1_gnn_Wl': _L1_gnn_in['Wl'], 'L1_gnn_Wr': _L1_gnn_in['Wr'], 'L1_gnn_b': _L1_gnn_in['b'], 'L1_mix_w_norm1': _L1_mix_in['w_norm1'], 'L1_mix_w_qkv': _L1_mix_in['w_qkv'], 'L1_mix_w_out': _L1_mix_in['w_out'], 'L1_mix_b_out': _L1_mix_in['b_out'], 'L1_mix_w_norm2': _L1_mix_in['w_norm2'], 'L1_ffn_gamma': _L1_ffn_in['gamma'], 'L1_ffn_beta': _L1_ffn_in['beta'], 'L1_ffn_Wr': _L1_ffn_in['Wr'], 'L1_ffn_br': _L1_ffn_in['br'], 'L1_ffn_W1': _L1_ffn_in['W1'], 'L1_ffn_b1': _L1_ffn_in['b1'], 'L1_ffn_W2': _L1_ffn_in['W2'], 'L1_ffn_b2': _L1_ffn_in['b2']}

def reference(x, src, dst, L0_gnn_w11, L0_gnn_b11, L0_gnn_w12, L0_gnn_b12, L0_gnn_w21, L0_gnn_b21, L0_gnn_w22, L0_gnn_b22, L0_mix_wq, L0_mix_wk, L0_mix_wv, L0_mix_wo, L0_mix_bo, L0_mix_ln_k_g, L0_mix_ln_k_b, L0_mix_ln_v_g, L0_mix_ln_v_b, L0_ffn_weight, L0_ffn_bias, L1_gnn_W, L1_gnn_Wl, L1_gnn_Wr, L1_gnn_b, L1_mix_w_norm1, L1_mix_w_qkv, L1_mix_w_out, L1_mix_b_out, L1_mix_w_norm2, L1_ffn_gamma, L1_ffn_beta, L1_ffn_Wr, L1_ffn_br, L1_ffn_W1, L1_ffn_b1, L1_ffn_W2, L1_ffn_b2):
    import jax
    import jax.numpy as jnp

    def _L0_gnn_ref(x, edge_index, w11, b11, w12, b12, w21, b21, w22, b22):
        import jax, jax.numpy as jnp
        import numpy as np
        N = 1250
        E = 40000
        D = 256

        def gine_conv(x, edge_index, w1, b1, w2, b2):
            src, dst = (edge_index[0], edge_index[1])
            msg = jax.nn.relu(x[src])
            agg = jax.ops.segment_sum(msg, dst, num_segments=x.shape[0])
            h = x + agg
            h = jax.nn.relu(h @ w1 + b1)
            return h @ w2 + b2
        out = jax.nn.relu(gine_conv(x, edge_index, w11, b11, w12, b12))
        out = gine_conv(out, edge_index, w21, b21, w22, b22)
        out = out + out
        return jax.nn.relu(out)

    def _L0_mix_ref(seq, wq, wk, wv, wo, bo, ln_k_g, ln_k_b, ln_v_g, ln_v_b):
        import jax, jax.numpy as jnp
        import numpy as np
        import math
        EMBED = 256
        HEADS = 4
        HEAD_DIM = EMBED // HEADS
        OUT_DIM = 256
        LN_EPS = 1e-05

        def _qkv_init(key):
            spread = math.sqrt(3.0 / EMBED)
            gain, delta = (0.01, 0.01)
            w = jax.random.uniform(key, (EMBED, EMBED), minval=-spread, maxval=spread) * gain
            return w + delta * jnp.eye(EMBED, dtype=w.dtype)

        def _layer_norm(x, g, b):
            mu = jnp.mean(x, axis=-1, keepdims=True)
            var = jnp.mean(jnp.square(x - mu), axis=-1, keepdims=True)
            return (x - mu) * jax.lax.rsqrt(var + LN_EPS) * g + b

        def _split_heads(x, B, S):
            return x.reshape(B, S, HEADS, HEAD_DIM).transpose(0, 2, 1, 3)
        B, S, _ = seq.shape
        q = _split_heads(seq @ wq.T, B, S)
        k = _split_heads(seq @ wk.T, B, S)
        v = _split_heads(seq @ wv.T, B, S)
        k = _layer_norm(k, ln_k_g, ln_k_b)
        v = _layer_norm(v, ln_v_g, ln_v_b)
        kv = jnp.einsum('bhsd,bhse->bhde', k, v) / S
        ga = jnp.einsum('bhsd,bhde->bhse', q, kv)
        ga = ga.transpose(0, 2, 1, 3).reshape(B, S, EMBED)
        return ga @ wo.T + bo

    def _L0_ffn_ref(x, weight, bias):
        import jax, jax.numpy as jnp
        import numpy as np
        IN_CH = 256
        OUT_CH = 256
        return jnp.einsum('bsi,oi->bso', x, weight) + bias

    def _L1_gnn_ref(h, W, Wl, Wr, b, edge_index):
        import jax, jax.numpy as jnp
        import numpy as np
        N_NODES = 6250
        N_EDGES = 200000
        IN_DIM, OUT_DIM, N_HEADS = (256, 64, 4)
        EPS = 1e-12
        N = h.shape[0]
        H = Wl.shape[0]
        x = h @ W
        el = x @ Wl.T
        er = x @ Wr.T
        src, dst = (edge_index[0], edge_index[1])
        e = el[src] + er[dst]
        e = jnp.exp(jax.nn.leaky_relu(e, negative_slope=0.2))
        rowsum = jax.ops.segment_sum(e, src, num_segments=N)
        w = e / jnp.maximum(rowsum, EPS)[src]
        heads = [jax.ops.segment_sum(w[:, hd:hd + 1] * x[dst], src, num_segments=N) for hd in range(H)]
        out = jnp.stack(heads, axis=1)
        out = jax.nn.elu(out + b)
        return out.reshape(N, H * x.shape[1])

    def _L1_mix_ref(x, w_norm1, w_qkv, w_out, b_out, w_norm2):
        import jax, jax.numpy as jnp
        import numpy as np
        EPS_NORM = 1e-06
        EPS_ATTN = 1e-06
        HEADS = 8

        def rmsnorm(x, w):
            ms = jnp.mean(x * x, axis=-1, keepdims=True)
            return w * (x * jax.lax.rsqrt(ms + EPS_NORM))

        def linear_attention(x, w_qkv, w_out, b_out):
            B, N, D = x.shape
            hd = D // HEADS
            qkv = (x @ w_qkv).reshape(B, N, 3, HEADS, hd)
            q, k, v = (qkv[:, :, 0], qkv[:, :, 1], qkv[:, :, 2])
            q = jax.nn.elu(q) + 1.0
            k = jax.nn.elu(k) + 1.0
            kv = jnp.einsum('bnhd,bnhm->bhdm', k, v)
            z = 1.0 / (jnp.einsum('bnhd,bhd->bnh', q, k.sum(axis=1)) + EPS_ATTN)
            out = jnp.einsum('bnhd,bhdm,bnh->bnhm', q, kv, z)
            out = out.reshape(B, N, D)
            return out @ w_out + b_out
        h = x + linear_attention(rmsnorm(x, w_norm1), w_qkv, w_out, b_out)
        return h + rmsnorm(h, w_norm2)

    def _L1_ffn_ref(x, gamma, beta, Wr, br, W1, b1, W2, b2):
        import jax, jax.numpy as jnp
        import numpy as np
        E = 8
        K = 2
        D = 256
        H = 512
        DOUT = 256
        EPS = 1e-05
        mu = jnp.mean(x, axis=-1, keepdims=True)
        var = jnp.mean(jnp.square(x - mu), axis=-1, keepdims=True)
        xn = (x - mu) * jax.lax.rsqrt(var + EPS) * gamma + beta
        logits = jnp.einsum('bsd,de->bse', xn, Wr) + br
        top_vals, top_idx = jax.lax.top_k(logits, K)
        w = jax.nn.softmax(top_vals, axis=-1)
        w_full = jnp.einsum('bsk,bske->bse', w, jax.nn.one_hot(top_idx, E, dtype=w.dtype))
        y = jnp.zeros(x.shape[:-1] + (DOUT,), x.dtype)
        for e in range(E):
            h = jax.nn.gelu(jnp.einsum('bsd,dh->bsh', xn, W1[e]) + b1[e], approximate=False)
            y_e = jnp.einsum('bsh,hd->bsd', h, W2[e]) + b2[e]
            y = y + y_e * w_full[..., e, None]
        return y
    edge_index = jnp.stack([src, dst])
    xn = _layernorm(x, axis=-1)
    x = x + _L0_gnn_ref(xn, edge_index, L0_gnn_w11, L0_gnn_b11, L0_gnn_w12, L0_gnn_b12, L0_gnn_w21, L0_gnn_b21, L0_gnn_w22, L0_gnn_b22) + _L0_mix_ref(xn[None], L0_mix_wq, L0_mix_wk, L0_mix_wv, L0_mix_wo, L0_mix_bo, L0_mix_ln_k_g, L0_mix_ln_k_b, L0_mix_ln_v_g, L0_mix_ln_v_b)[0]
    x = x + _L0_ffn_ref(_layernorm(x, axis=-1)[None], L0_ffn_weight, L0_ffn_bias)[0]
    xn = _layernorm(x, axis=-1)
    x = x + _L1_gnn_ref(xn, L1_gnn_W, L1_gnn_Wl, L1_gnn_Wr, L1_gnn_b, edge_index) + _L1_mix_ref(xn[None], L1_mix_w_norm1, L1_mix_w_qkv, L1_mix_w_out, L1_mix_b_out, L1_mix_w_norm2)[0]
    x = x + _L1_ffn_ref(_layernorm(x, axis=-1)[None], L1_ffn_gamma, L1_ffn_beta, L1_ffn_Wr, L1_ffn_br, L1_ffn_W1, L1_ffn_b1, L1_ffn_W2, L1_ffn_b2)[0]
    return x

_drawn_inputs = setup_inputs


def setup_inputs(seed=0):
    import zlib

    import numpy as np

    out = dict(_drawn_inputs(seed))
    spreads = {'L0_gnn_b11': (0.0, 0.269),
     'L0_gnn_b12': (0.0, 0.1),
     'L0_gnn_b21': (0.0, 0.615),
     'L0_gnn_b22': (0.0, 0.1),
     'L0_mix_ln_k_g': (1.0, 0.6),
     'L0_mix_ln_k_b': (0.0, 0.8),
     'L0_mix_ln_v_g': (1.0, 0.6),
     'L0_mix_ln_v_b': (0.0, 0.8),
     'L1_gnn_b': (0.0, 0.603),
     'L1_mix_w_norm1': (1.0, 0.6),
     'L1_mix_b_out': (0.0, 0.281),
     'L1_mix_w_norm2': (1.0, 0.549),
     'L1_ffn_br': (0.0, 0.8)}
    factors = {'L0_mix_wq': 8.0,
     'L0_mix_wk': 8.0,
     'L0_mix_wv': 8.0,
     'L0_mix_wo': 8.0,
     'L0_mix_bo': 7.293,
     'L0_ffn_bias': 7.225,
     'L1_gnn_Wl': 26.442,
     'L1_gnn_Wr': 8.0,
     'L1_ffn_gamma': 8.0,
     'L1_ffn_beta': 8.0,
     'L1_ffn_Wr': 8.0,
     'L1_ffn_W1': 7.577,
     'L1_ffn_b1': 57.161,
     'L1_ffn_W2': 7.869,
     'L1_ffn_b2': 64.0}
    for name, (base, spread) in spreads.items():
        noise = np.random.default_rng([zlib.crc32(name.encode()), seed]).standard_normal(out[name].shape)
        drawn = base * np.exp(spread * noise) if base else spread * noise
        out[name] = jnp.asarray(drawn.astype(out[name].dtype))
    for name, factor in factors.items():
        out[name] = (out[name] * factor).astype(out[name].dtype)
    return out
```

```python
from contextlib import ExitStack

import concourse.bass as bass
from concourse import mybir

P = 128
N, D = 6250, 256
E = 100000
EDGE_ROOM = (E + 2 * P - 1) // P * P
TILES = (N + P - 1) // P
TAIL = N - (TILES - 1) * P
NPAD = TILES * P
LANES = 125
COLS = E // LANES
CH = 10
CT = CH * TILES
BITS = 13
NOWHERE = (1 << BITS) - 1
SLOT_TILES = ((E + TILES * (P - 1)) // P + 7) // 8 * 8
SC = (SLOT_TILES + P - 1) // P
AW = 260
GW = 68
EXPERTS, HID = 8, 512
EX_TILES = ((2 * N + EXPERTS * (P - 1)) // P + 1) // 2 * 2
RING = 8

F32 = mybir.dt.float32
I32 = mybir.dt.int32
BF16 = mybir.dt.bfloat16
ALU = mybir.AluOpType
ACT = mybir.ActivationFunctionType
X_AXIS = mybir.AxisListType.X


class Stage:

    def __init__(self, nc, name):
        self.nc, self.name, self.ctx, self.taken = nc, name, ExitStack(), []

    def __enter__(self):
        return self

    def __exit__(self, *a):
        self.ctx.__exit__(*a)
        self.nc.clear_and_free_semaphores(self.taken)
        self.nc.all_engine_barrier()

    def sb(self, name, shape, dt=F32):
        return self.ctx.enter_context(self.nc.sbuf_tensor(f"{self.name}_{name}", shape, dt))

    def ps(self, name, shape=(P, 512), dt=F32):
        return self.ctx.enter_context(self.nc.psum_tensor(f"{self.name}_{name}", list(shape), dt))

    def sem(self, name):
        self.taken.append(self.nc.alloc_semaphore(f"{self.name}_{name}"))
        return self.taken[-1]

    def sems(self, name, n=2):
        return [self.sem(f"{name}{k}") for k in range(n)]

    def block(self):
        return self.ctx.enter_context(self.nc.Block())


def in_twos(eng, count, body):
    body(0, 0)
    body(1, 1)
    with eng.Fori(1, count // 2) as q:
        body(q * 2, 0)
        body(q * 2 + 1, 1)


def over_tiles(eng, body):
    in_twos(eng, TILES - 1, lambda i, s: body(i, s, P))
    body(TILES - 1, 0, TAIL)


def reused(i):
    return not (isinstance(i, int) and i < 2)


def dma_count(i, s):
    return i * 8 + (16 - 8 * s)


def dma_count_before(i, s):
    return i * 8 - 8 * s


def held(eng, turns):
    eng.sem_inc(turns, 1)


def cols(t, start, width):
    return t[:, bass.ds(start, width)]


def row_to_all(ap, parts=P):
    return ap.partition_broadcast(parts)


def stage_load(nc, m):
    with Stage(nc, "load") as st:
        nat = [st.sb(f"nat{k}", [P, 2, D]) for k in range(4)]
        gWlr = st.sb("gWlr", [8, 64])
        gWT = st.sb("gWT", [64, D])
        gWlrT = st.sb("gWlrT", [64, 8])
        mw1p = st.sb("mw1p", [P, 2])
        small = st.sb("small", [1, 8], I32)
        ps = [st.ps(f"ps{k}") for k in range(4)]
        loaded, x_in, x_clear, consts, steps = (st.sem(s) for s in ("loaded", "x_in", "x_clear", "consts", "steps"))
        turned, copied = st.sem("turned"), st.sem("copied")
        pads, pads_out = st.sem("pads"), st.sem("pads_out")
        block = st.block()
        chunks = lambda w: w.rearrange("(c p) n -> p c n", p=P)
        count = [0]

        @block.sync
        def _(sp):
            def load(to, frm, **kw):
                sp.dma_start(to, frm, **kw).then_inc(loaded, 16)
                count[0] += 16

            load(m.src_i[:, :], m.src.rearrange("(p c) -> p c", p=LANES))
            load(m.dst_i[:, :], m.dst.rearrange("(p c) -> p c", p=LANES))
            for k, w in enumerate((m.wk, m.wv, m.wo, m.fw)):
                load(nat[k][:, :, :], chunks(w))
            load(gWlr[0:4, :], m.gWr)
            load(gWlr[4:8, :], m.gWl)
            load(m.gWs[:, :, :], chunks(m.gW))
            load(mw1p[:, :], m.mw1.rearrange("(c p) -> p c", p=P), allow_slow_non_contiguous=True)
            load(m.wqkvs[:, :, :], chunks(m.wqkv))
            for to, frm in ((m.wqs, m.wq), (m.w11s, m.w11), (m.w12s, m.w12), (m.w21s, m.w21), (m.w22s, m.w22),
                            (m.wouts, m.wout), (m.rWs, m.rW)):
                load(to[:, :, :], chunks(frm))
            for to, frm in ((m.b11s, m.b11), (m.b21s, m.b21)):
                load(to[:, :], frm.rearrange("(c p) -> p c", p=P), allow_slow_non_contiguous=True)
            for to, frm in ((m.b12r, m.b12), (m.b22r, m.b22), (m.bor, m.bo), (m.fbr, m.fb), (m.boutr, m.bout),
                            (m.mw2r, m.mw2), (m.gammar, m.gamma), (m.betar, m.beta), (m.gbr, m.gb), (m.rbr, m.rb)):
                load(to[:, :], row_to_all(frm))
            for half in range(2):
                lo = 64 * half
                load(m.kgp[lo:lo + 64, :], m.kg.rearrange("(p a) -> p a", a=1))
                load(m.kbp[lo:lo + 64, :], m.kb.rearrange("(p a) -> p a", a=1))
                load(m.vgr[:, lo:lo + 64], row_to_all(m.vg))
                load(m.vbr[:, lo:lo + 64], row_to_all(m.vb))
            whole = (TILES - 1) * P
            for g in range(4):
                sp.dma_start(m.X[:, g * 12 * D:(g + 1) * 12 * D].rearrange("p (i d) -> p i d", d=D),
                             m.x[g * 12 * P:(g + 1) * 12 * P, :].rearrange("(i p) d -> p i d", p=P)).then_inc(x_in, 16)
            sp.wait_ge(x_clear, 1)
            sp.dma_start(m.X[0:TAIL, (TILES - 1) * D:TILES * D], m.x[whole:N, :]).then_inc(x_in, 16)
            sp.wait_ge(x_in, 80)
            sp.wait_ge(pads, 1)
            sp.dma_start(m.edges[0][E:EDGE_ROOM].rearrange("(a b) -> a b", a=1), m.pad_dst[:, :]).then_inc(pads_out, 16)
            sp.dma_start(m.edges[1][E:EDGE_ROOM].rearrange("(a b) -> a b", a=1), m.pad_src[:, :]).then_inc(pads_out, 16)
            sp.wait_ge(pads_out, 32)
            sp.wait_ge(loaded, count[0])

        @block.gpsimd
        def _(pool):
            nc.gpsimd.memset(m.X[:, (TILES - 1) * D:TILES * D], 0.0).then_inc(x_clear, 1)
            for t, v in ((m.ident, 0.0), (m.tri, 1.0), (m.ones, 1.0), (m.zeros, 0.0), (m.mask64, 1.0), (m.mask32, 1.0)):
                nc.gpsimd.memset(t[:, :], v)
            nc.gpsimd.memset(m.pad_dst[:, :], NOWHERE)
            nc.gpsimd.memset(m.pad_src[:, :], NOWHERE << BITS)
            pool.drain().then_inc(pads, 1)
            nc.gpsimd.affine_select(out=m.ident[:, :], in_=m.ident[:, :], compare_op=ALU.not_equal, fill=1.0, base=0,
                                    pattern=[[-1, P]], channel_multiplier=1)
            nc.gpsimd.affine_select(out=m.tri[:, :], in_=m.tri[:, :], compare_op=ALU.is_ge, fill=0.0, base=-1,
                                    pattern=[[1, P]], channel_multiplier=-1)
            for t, w in ((m.mask64, 64), (m.mask32, 32)):
                v = t[:, :].rearrange("p (g j) -> p g j", j=w)
                nc.gpsimd.affine_select(out=v, in_=v, compare_op=ALU.is_ge, fill=0.0, base=0,
                                        pattern=[[-w, P // w], [0, w]], channel_multiplier=1)
                pool.drain()
                nc.gpsimd.affine_select(out=v, in_=v, compare_op=ALU.is_ge, fill=0.0, base=w - 1,
                                        pattern=[[w, P // w], [0, w]], channel_multiplier=-1)
            nc.gpsimd.iota(m.iota_row[:, :], [[1, P]], base=0, channel_multiplier=0, allow_small_or_imprecise_dtypes=True)
            nc.gpsimd.iota(m.slot_no[:, :], [[P, SC]], base=0, channel_multiplier=1, allow_small_or_imprecise_dtypes=True)
            pool.drain().then_inc(consts, 1)

        @block.tensor
        def _(pe):
            pe.wait_ge(consts, 1)
            pe.wait_ge(loaded, count[0])
            for k in range(4):
                for oc in range(2):
                    for kc in range(2):
                        nc.tensor.transpose(ps[k][:, kc * D + oc * P:kc * D + oc * P + P], nat[k][:, oc, kc * P:kc * P + P],
                                            m.ident[:, :])
            pe.drain().then_inc(turned, 1)
            pe.wait_ge(copied, 1)
            for kc in range(2):
                nc.tensor.transpose(ps[0][0:64, kc * P:kc * P + P], m.gWs[:, kc, :], m.ident[:, :])
            nc.tensor.transpose(ps[1][0:64, 0:8], gWlr[:, :], m.ident[0:8, 0:8])
            pe.drain().then_inc(turned, 1)
            pe.wait_ge(copied, 2)
            for kc in range(2):
                nc.tensor.matmul(ps[2][:, 8 * kc:8 * kc + 8], gWT[:, kc * P:kc * P + P], gWlrT[:, :], start=True, stop=True)
            pe.drain().then_inc(turned, 1)

        @block.scalar
        def _(act):
            act.wait_ge(consts, 1)
            nc.scalar.copy(m.tri_bf[:, :], m.tri[:, :])
            nc.scalar.copy(m.ones_bf[:, :], m.ones[:, :])
            nc.scalar.copy(m.zeros_bf[:, :], m.zeros[:, 0:512])
            nc.scalar.activation(m.rest_bf[:, :], m.tri[:, :], ACT.Copy, bias=1.0, scale=-1.0)
            act.wait_ge(turned, 1)
            for k, (t, at) in enumerate(((m.wkvT, 0), (m.wkvT, D), (m.woT, 0), (m.fT, 0))):
                nc.scalar.copy(t[:, :, at:at + D], ps[k][:, :].rearrange("p (c n) -> p c n", c=2))
            act.drain().then_inc(copied, 1)
            act.wait_ge(turned, 2)
            nc.scalar.copy(gWT[:, :], ps[0][0:64, 0:D])
            nc.scalar.copy(gWlrT[:, :], ps[1][0:64, 0:8])
            nc.scalar.copy(m.gcat[:, :, 0:64], m.gWs[:, :, :])
            act.drain().then_inc(copied, 1)
            act.wait_ge(turned, 3)
            nc.scalar.copy(m.gcat[:, :, 64:72], ps[2][:, 0:16].rearrange("p (c n) -> p c n", c=2))

        @block.vector
        def _(v):
            v.wait_ge(loaded, count[0])
            for kc in range(2):
                nc.vector.tensor_scalar(m.wqkvs[:, kc, :], m.wqkvs[:, kc, :], mw1p[:, kc:kc + 1], None, ALU.mult)
            nc.vector.tensor_scalar(m.packed[:, :], m.src_i[:, :], BITS, None, ALU.logical_shift_left)
            v.drain()
            nc.vector.tensor_tensor(m.packed[:, :], m.packed[:, :], m.dst_i[:, :], ALU.bitwise_or)


def stage_rank(nc, m, key_in, which):
    with Stage(nc, f"rank{which}") as st:
        key_i = st.sb("key_i", [LANES, COLS], I32)
        key = st.sb("key", [LANES, COLS])
        rank = st.sb("rank", [LANES, COLS])
        oh = [st.sb(f"oh{s}", [LANES, CH, TILES], BF16) for s in range(2)]
        base = st.sb("base", [P, CH, TILES])
        prod = [st.sb(f"prod{s}", [LANES, CH, TILES]) for s in range(2)]
        bin_f2 = st.sb("bin_f2", [P, SC])
        tot = st.sb("tot", [P, TILES])
        a, b, start, below = (st.sb(n, [P, TILES]) for n in ("a", "b", "start", "below"))
        ti = st.sb("ti", [P, TILES], I32)
        cmp = st.sb("cmp", [P, SC, TILES])
        off = st.sb("off", [P, SC])
        bin_f, bin_i, off_i = st.sb("bin_f", [P, SC]), st.sb("bin_i", [P, SC], I32), st.sb("off_i", [P, SC], I32)
        raw = st.sb("raw", [P, SC, P], I32)
        part = st.sb("part", [P, SC, P], I32)
        loc, nbr = st.sb("loc", [P, SC, P]), st.sb("nbr", [P, SC, P])
        lanes_idx, lanes_pay = st.sb("lanes_idx", [LANES, 2, 8], I32), st.sb("lanes_pay", [LANES, 2, 8], I32)
        hist, run = st.ps("hist"), st.ps("run")
        pt = [st.ps(f"pt{k}") for k in range(4)]
        cleared, keyed, oh_made, oh_used, hist_done = (st.sem(s) for s in
                                                       ("cleared", "keyed", "oh_made", "oh_used", "hist_done"))
        oh2_made, before, counted, after = (st.sem(s) for s in ("oh2_made", "before", "counted", "after"))
        ranked, batch, sent = st.sem("ranked"), st.sem("batch"), st.sems("sent", 2)
        off_ready, sorted_in, slots_ready, turned = (st.sem(s) for s in ("off_ready", "sorted_in", "slots_ready", "turned"))
        bin_out, bin_back = st.sem("bin_out"), st.sem("bin_back")
        t_v, t_p, t_t = st.sem("turns_v"), st.sem("turns_p"), st.sem("turns_t")
        block = st.block()
        edges = m.edges[which].rearrange("(r c) -> r c", c=P)

        def f2(t):
            return t[:, :, :].rearrange("p c b -> p (c b)")

        @block.vector
        def _(v):
            nc.vector.tensor_scalar(key_i[:, :], key_in[:, :], 7, None, ALU.logical_shift_right)
            v.drain()
            nc.vector.tensor_copy(key[:, :], key_i[:, :])
            v.drain()
            bins = m.iota_row[0:LANES, 0:TILES].unsqueeze(1).broadcast_to([LANES, CH, TILES])
            def one_hot(c, s):
                k = cols(key, c * CH, CH).unsqueeze(2).broadcast_to([LANES, CH, TILES])
                return nc.vector.tensor_tensor(oh[s][:, :, :], k, bins, ALU.is_equal)

            def count_chunk(c, s):
                if reused(c):
                    v.wait_ge(oh_used, c - 1)
                    held(v, t_v)
                one_hot(c, s).then_inc(oh_made, 1)

            in_twos(v, COLS // CH, count_chunk)
            v.wait_ge(hist_done, 1)
            nc.vector.tensor_copy(f2(base), hist[:, 0:CT])
            v.drain()
            nc.vector.tensor_reduce(tot[:, :], base[:, :, :].rearrange("p c b -> p b c"), X_AXIS, ALU.add)
            v.drain()

            def prefix(x, y):
                w = 1
                while w < TILES:
                    nc.vector.tensor_tensor(y[:, w:TILES], x[:, w:TILES], x[:, 0:TILES - w], ALU.add)
                    nc.vector.tensor_copy(y[:, 0:w], x[:, 0:w])
                    v.drain()
                    x, y, w = y, x, 2 * w
                return x, y

            nc.vector.tensor_copy(a[:, :], tot[:, :])
            v.drain()
            ends, spare = prefix(a, b)
            nc.vector.tensor_tensor(start[:, :], ends[:, :], tot[:, :], ALU.subtract)
            v.drain()
            nc.vector.tensor_copy(below[:, :], start[:, :])
            v.drain()
            for j in range(CH):
                nc.vector.tensor_copy(spare[:, :], base[:, j, :])
                v.drain()
                nc.vector.tensor_copy(base[:, j, :], below[:, :])
                v.drain()
                nc.vector.tensor_tensor(below[:, :], below[:, :], spare[:, :], ALU.add)
                v.drain()
            nc.vector.tensor_scalar(a[:, :], tot[:, :], float(P - 1), None, ALU.add)
            v.drain()
            nc.vector.tensor_copy(ti[:, :], a[:, :])
            v.drain()
            nc.vector.tensor_scalar(ti[:, :], ti[:, :], 7, None, ALU.logical_shift_right)
            v.drain()
            nc.vector.tensor_copy(a[:, :], ti[:, :])
            nc.vector.tensor_copy(tot[:, :], ti[:, :])
            v.drain()
            tile_ends, spare = prefix(a, b)
            nc.vector.tensor_tensor(tot[:, :], tile_ends[:, :], tot[:, :], ALU.subtract)
            v.drain()
            nc.vector.scalar_tensor_tensor(out=spare[:, :], in0=tot[:, :], scalar=-float(P), in1=start[:, :], op0=ALU.mult, op1=ALU.add)
            slots = m.slot_no[:, :].unsqueeze(2).broadcast_to([P, SC, TILES])
            over = lambda t: t.unsqueeze(1).broadcast_to([P, SC, TILES])
            nc.vector.tensor_tensor(cmp[:, :, :], over(tile_ends[:, :]), slots, ALU.is_le)
            v.drain()
            nc.vector.tensor_reduce(bin_f[:, :], cmp[:, :, :], X_AXIS, ALU.add)
            v.drain()
            nc.vector.tensor_tensor(cmp[:, :, :], over(m.iota_row[:, 0:TILES]),
                                    bin_f[:, :].unsqueeze(2).broadcast_to([P, SC, TILES]), ALU.is_equal)
            nc.vector.tensor_scalar(off[:, :], bin_f[:, :], float(TILES - 1), None, ALU.min)
            v.drain()
            nc.vector.tensor_copy(bin_i[:, :], off[:, :]).then_inc(bin_out, 1)
            nc.vector.tensor_tensor(cmp[:, :, :], cmp[:, :, :], over(spare[:, :]), ALU.mult)
            v.drain()
            nc.vector.tensor_reduce(off[:, :], cmp[:, :, :], X_AXIS, ALU.add)
            v.drain()
            nc.vector.scalar_tensor_tensor(out=off[:, :], in0=m.slot_no[:, :], scalar=float(P), in1=off[:, :],
                                           op0=ALU.mult, op1=ALU.add)
            v.drain()
            nc.vector.tensor_scalar(off[:, :], off[:, :], float(E), None, ALU.min)
            v.drain()
            nc.vector.tensor_copy(off_i[:, :], off[:, :])
            def rank_chunk(c, s):
                v.wait_ge(after, c + 1)
                held(v, t_v)
                one_hot(c, s).then_inc(oh2_made, 1)
                v.wait_ge(before, c + 1)
                held(v, t_v)
                nc.vector.tensor_tensor(f2(prod[0]), run[0:LANES, 0:CT], f2(base)[0:LANES, :], ALU.add)
                v.drain().then_inc(counted, 1)
                nc.vector.tensor_tensor(f2(prod[1]), f2(prod[0]), f2(oh[s]), ALU.mult)
                v.drain()
                nc.vector.tensor_reduce(cols(rank, c * CH, CH), prod[1][:, :, :], X_AXIS, ALU.add)

            in_twos(v, COLS // CH, rank_chunk)
            v.drain()
            nc.vector.tensor_copy(key_i[:, :], rank[:, :])
            v.drain()

            def batch_of_eight(c, s):
                if reused(c):
                    v.wait_ge(sent[s], (c - s) * 64)
                    held(v, t_v)
                nc.vector.tensor_copy(lanes_idx[:, s, :], cols(key_i, c * 8, 8))
                nc.vector.tensor_copy(lanes_pay[:, s, :], cols(m.packed, c * 8, 8))
                v.drain().then_inc(batch, 1)

            in_twos(v, COLS // 8, batch_of_eight)
            v.wait_ge(sorted_in, 16 * SC)
            shift, keep = (ALU.logical_shift_right, BITS), (ALU.bitwise_and, NOWHERE)
            own, other = (keep, shift) if which == 0 else (shift, keep)
            nc.vector.tensor_scalar(part[:, :, :], raw[:, :, :], own[1], None, own[0])
            v.drain()
            nc.vector.tensor_copy(loc[:, :, :], part[:, :, :])
            v.drain()
            for c4 in range(SC):
                nc.vector.tensor_scalar(bin_f2[:, c4:c4 + 1], bin_f[:, c4:c4 + 1], -float(P), None, ALU.mult)
            nc.vector.tensor_scalar(part[:, :, :], raw[:, :, :], other[1], None, other[0])
            v.drain()
            for c4 in range(SC):
                nc.vector.tensor_scalar(loc[:, c4, :], loc[:, c4, :], bin_f2[:, c4:c4 + 1], None, ALU.add)
            nc.vector.tensor_copy(nbr[:, :, :], part[:, :, :])
            v.drain().then_inc(slots_ready, 1)
            v.wait_ge(turned, 1)
            for k, t in enumerate((m.LOC, m.GI)):
                nc.vector.tensor_copy(t[:, 0:512], pt[2 * k][:, :])
                nc.vector.tensor_copy(t[:, 512:SC * P], pt[2 * k + 1][:, 0:SC * P - 512])

        @block.tensor
        def _(pe):
            for bank in (hist, run):
                nc.tensor.matmul(bank[:, 0:CT], m.ones_bf[0:LANES, :], m.zeros_bf[0:LANES, 0:CT], start=True, stop=False,
                                 skip_group_check=True)
            pe.drain().then_inc(after, 1)
            def count_chunk(c, s):
                pe.wait_ge(oh_made, c + 1)
                held(pe, t_t)
                nc.tensor.matmul(hist[:, 0:CT], m.ones_bf[0:LANES, :], f2(oh[s]), start=False, stop=False,
                                 skip_group_check=True).then_inc(oh_used, 1)

            in_twos(pe, COLS // CH, count_chunk)
            nc.tensor.matmul(hist[:, 0:CT], m.ones_bf[0:LANES, :], m.zeros_bf[0:LANES, 0:CT], start=False, stop=True,
                             skip_group_check=True).then_inc(hist_done, 1)
            def rank_chunk(c, s):
                pe.wait_ge(oh2_made, c + 1)
                held(pe, t_t)
                nc.tensor.matmul(run[:, 0:CT], m.tri_bf[0:LANES, :], f2(oh[s]), start=False, stop=False,
                                 skip_group_check=True).then_inc(before, 1)
                pe.wait_ge(counted, c + 1)
                held(pe, t_t)
                nc.tensor.matmul(run[:, 0:CT], m.rest_bf[0:LANES, :], f2(oh[s]), start=False, stop=False,
                                 skip_group_check=True).then_inc(after, 1)

            in_twos(pe, COLS // CH, rank_chunk)
            nc.tensor.matmul(run[:, 0:CT], m.ones_bf[0:LANES, :], m.zeros_bf[0:LANES, 0:CT], start=False, stop=True,
                             skip_group_check=True)
            pe.wait_ge(slots_ready, 1)
            for k, t in enumerate((loc, nbr)):
                for c in range(SC):
                    nc.tensor.transpose(pt[2 * k + c // 4][:, (c % 4) * P:(c % 4 + 1) * P], t[:, c, :], m.ident[:, :])
            pe.drain().then_inc(turned, 1)

        @block.gpsimd
        def _(pool):
            def batch_of_eight(c, s):
                pool.wait_ge(batch, c + 1)
                held(pool, t_p)
                for k in range(8):
                    pool.indirect_dma_start(m.edges[which].rearrange("(e a) -> e a", a=1),
                                            bass.IndirectOffsetOnAxis(ap=lanes_idx[:, s, k:k + 1], axis=0),
                                            lanes_pay[:, s, k:k + 1], None).then_inc(sent[s], 16)

            in_twos(pool, COLS // 8, batch_of_eight)
            for s in range(2):
                pool.wait_ge(sent[s], 16 * COLS // 2)
            for c in range(SC):
                pool.indirect_dma_start(raw[:, c, :], None, edges,
                                        bass.IndirectOffsetOnAxis(ap=off_i[:, c:c + 1], axis=1)).then_inc(sorted_in, 16)
            pool.wait_ge(sorted_in, 16 * SC)

        @block.sync
        def _(sp):
            sp.wait_ge(bin_out, 1)
            sp.dma_start(m.bin_dram[which].rearrange("(c p) -> p c", p=P), bin_i[:, :],
                         allow_slow_non_contiguous=True).then_inc(bin_back, 16)
            sp.wait_ge(bin_back, 16)
            sp.dma_start(m.bin_row[:, :], m.bin_dram[which].rearrange("(a c) -> a c", a=1)).then_inc(bin_back, 16)
            sp.wait_ge(bin_back, 32)


def stage_stats(nc, m, name, eps, with_rms=False):
    with Stage(nc, name) as st:
        parts = st.sb("parts", [P, TILES, 6])
        a, b = st.sb("a", [P, TILES]), st.sb("b", [P, TILES])
        var_done, root_done = st.sem("var_done"), st.sem("root_done")
        block = st.block()

        @block.vector
        def _(v):
            flat = parts[:, :, :].rearrange("p i s -> p (i s)")
            with v.Fori(0, TILES) as i:
                nc.vector.bn_stats(flat[:, bass.ds(i * 6, 6)], cols(m.X, i * D, D))
            v.drain()
            f = lambda k: parts[:, :, k]
            nc.vector.tensor_tensor(a[:, :], f(1), f(4), ALU.add)
            nc.vector.tensor_tensor(b[:, :], f(1), f(4), ALU.subtract)
            nc.vector.tensor_tensor(m.rms_out[:, :], f(2), f(5), ALU.add)
            v.drain()
            nc.vector.tensor_scalar(m.mean[:, :], a[:, :], 0.5, None, ALU.mult)
            nc.vector.scalar_tensor_tensor(out=b[:, :], in0=b[:, :], scalar=0.25, in1=b[:, :], op0=ALU.mult, op1=ALU.mult)
            v.drain()
            nc.vector.scalar_tensor_tensor(out=b[:, :], in0=m.rms_out[:, :], scalar=1.0 / D, in1=b[:, :],
                                           op0=ALU.mult, op1=ALU.add)
            v.drain()
            nc.vector.tensor_scalar(a[:, :], b[:, :], eps, None, ALU.add)
            v.drain().then_inc(var_done, 1)
            v.wait_ge(root_done, 1)
            nc.vector.reciprocal(m.rstd[:, :], m.rms_out[:, :])
            if with_rms:
                v.drain()
                nc.vector.tensor_tensor(a[:, :], m.rstd[:, :], m.rstd[:, :], ALU.mult)
                v.drain()
                nc.vector.tensor_tensor(a[:, :], a[:, :], b[:, :], ALU.mult)
                v.drain()
                nc.vector.tensor_scalar(a[:, :], a[:, :], 1e-6, None, ALU.add)
                v.drain().then_inc(var_done, 1)
                v.wait_ge(root_done, 2)
                nc.vector.reciprocal(b[:, :], m.rms_out[:, :])
                v.drain()
                nc.vector.tensor_tensor(m.rms_in[:, :], b[:, :], m.rstd[:, :], ALU.mult)

        @block.scalar
        def _(act):
            act.wait_ge(var_done, 1)
            nc.scalar.activation(m.rms_out[:, :], a[:, :], ACT.Sqrt).then_inc(root_done, 1)
            if with_rms:
                act.wait_ge(var_done, 2)
                nc.scalar.activation(m.rms_out[:, :], a[:, :], ACT.Sqrt).then_inc(root_done, 1)


def stage_norm_kv(nc, m):
    with Stage(nc, "nkv") as st:
        xn = [st.sb(f"xn{s}", [P, D]) for s in range(2)]
        rx = [st.sb(f"rx{s}", [P, D]) for s in range(2)]
        xt = [st.sb(f"xt{s}", [P, D]) for s in range(2)]
        sq = [st.sb(f"sq{s}", [P, 2 * D]) for s in range(2)]
        kn = [st.sb(f"kn{s}", [P, D]) for s in range(2)]
        vn = [st.sb(f"vn{s}", [P, 2, P + 1]) for s in range(2)]
        cen = st.sb("cen", [P, 2 * D])
        s1, s2, mu, va, rt = (st.sb(n, [P, 8]) for n in ("s1", "s2", "mu", "va", "rt"))
        kv_sum = st.sb("kv_sum", [P, 2 * (P + 1)])
        v_sum = st.sb("v_sum", [P, 2 * (P + 1)])
        w = [st.sb(f"w{k}", [P, P]) for k in range(3)]
        bd = st.sb("bd", [P, 2, P])
        kgs, kbs = st.sb("kgs", [P, 1]), st.sb("kbs", [P, 1])
        u = st.sb("u", [P, 2, D])
        pt = [st.ps(f"pt{s}") for s in range(2)]
        pkv = [st.ps(f"pkv{s}") for s in range(2)]
        psum_kv, psum_v = st.ps("kv"), st.ps("v")
        xn_made, xn_turned, xt_made, projected, squared, root_in, rooted, kn_made, kn_used = (
            st.sem(n) for n in ("xn_made", "xn_turned", "xt_made", "projected", "squared", "root_in", "rooted",
                                "kn_made", "kn_used"))
        xn_kept, rx_made = st.sem("xn_kept"), st.sem("rx_made")
        out_rx, out_xt = st.sems("out_rx"), st.sems("out_xt")
        vones, sums_done, bd_made, u_done, u_kept, m_done = (st.sem(n) for n in ("vones", "sums_done", "bd_made", "u_done", "u_kept", "m_done"))
        tv, ta, tt, tp, ts = (st.sem(n) for n in ("turns_v", "turns_a", "turns_t", "turns_p", "turns_s"))
        block = st.block()
        groups = lambda t: t.rearrange("p (g j) -> p g j", j=64)
        W2 = P + 1

        @block.vector
        def _(v):
            for s in range(2):
                nc.vector.memset(vn[s][:, :, :], 1.0)
            v.drain().then_inc(vones, 1)

            def norm(i, s, rows):
                if reused(i):
                    v.wait_ge(xn_turned, i - 1)
                    v.wait_ge(rx_made, i - 1)
                    v.wait_ge(xn_kept, i - 1)
                    held(v, tv)
                nc.vector.tensor_scalar(xn[s][:, :], cols(m.X, i * D, D), cols(m.mean, i, 1), cols(m.rstd, i, 1),
                                        ALU.subtract, ALU.mult).then_inc(xn_made, 1)
                v.wait_ge(squared, i + 1)
                held(v, tv)
                kv = groups(pkv[s][:, :])
                nc.vector.tensor_reduce(s1[:, :], kv, X_AXIS, ALU.add)
                nc.vector.tensor_reduce(s2[:, :], groups(sq[s][:, :]), X_AXIS, ALU.add)
                v.drain()
                nc.vector.tensor_scalar(mu[:, :], s1[:, :], 1.0 / 64, None, ALU.mult)
                v.drain()
                nc.vector.tensor_tensor(va[:, :], mu[:, :], mu[:, :], ALU.mult)
                bc = lambda t: t[:, :].unsqueeze(2).broadcast_to([P, 8, 64])
                nc.vector.tensor_tensor(groups(cen[:, :]), kv, bc(mu), ALU.subtract)
                v.drain()
                nc.vector.scalar_tensor_tensor(out=s2[:, :], in0=s2[:, :], scalar=1.0 / 64, in1=va[:, :],
                                               op0=ALU.mult, op1=ALU.subtract)
                v.drain()
                nc.vector.tensor_scalar(va[:, :], s2[:, :], 0.0, 1e-5, ALU.max, ALU.add)
                v.drain().then_inc(root_in, 1)
                v.wait_ge(rooted, i + 1)
                held(v, tv)
                nc.vector.reciprocal(s1[:, :], rt[:, :])
                v.drain()
                if reused(i):
                    v.wait_ge(kn_used, i - 1)
                    held(v, tv)
                r = s1[:, :].unsqueeze(2).broadcast_to([P, 8, 64])
                nc.vector.tensor_tensor(groups(kn[s][:, :]), groups(cen[:, 0:D]), r[:, 0:4, :], ALU.mult)
                for c in range(2):
                    nc.vector.tensor_tensor(groups(vn[s][:, c, 0:P]), groups(cen[:, D + c * P:D + c * P + P]),
                                            r[:, 4 + 2 * c:6 + 2 * c, :], ALU.mult)
                v.drain().then_inc(kn_made, 1)

            over_tiles(v, norm)
            v.wait_ge(sums_done, 1)
            nc.vector.tensor_copy(kv_sum[:, :], psum_kv[:, 0:2 * W2])
            nc.vector.tensor_copy(v_sum[:, :], psum_v[:, 0:2 * W2])
            nc.vector.tensor_scalar(kgs[:, :], m.kgp[:, :], 1.0 / N, None, ALU.mult)
            nc.vector.tensor_scalar(kbs[:, :], m.kbp[:, :], 1.0 / N, None, ALU.mult)
            v.drain()
            for c in range(2):
                lo = c * W2
                nc.vector.tensor_tensor(w[0][:, :], kv_sum[:, lo:lo + P], m.vgr[:, :], ALU.mult)
                nc.vector.tensor_tensor(w[1][:, :], v_sum[:, lo:lo + P], m.vgr[:, :], ALU.mult)
                v.drain()
                nc.vector.scalar_tensor_tensor(out=w[0][:, :], in0=m.vbr[:, :], scalar=kv_sum[:, lo + P:lo + P + 1],
                                               in1=w[0][:, :], op0=ALU.mult, op1=ALU.add)
                nc.vector.scalar_tensor_tensor(out=w[1][:, :], in0=m.vbr[:, :], scalar=float(N),
                                               in1=w[1][:, :], op0=ALU.mult, op1=ALU.add)
                v.drain()
                nc.vector.tensor_scalar(w[0][:, :], w[0][:, :], kgs[:, :], None, ALU.mult)
                v.drain()
                nc.vector.scalar_tensor_tensor(out=w[2][:, :], in0=w[1][:, :], scalar=kbs[:, :], in1=w[0][:, :],
                                               op0=ALU.mult, op1=ALU.add)
                v.drain()
                nc.vector.tensor_tensor(bd[:, c, :], w[2][:, :], m.mask64[:, :], ALU.mult)
            v.drain().then_inc(bd_made, 1)

        @block.tensor
        def _(pe):
            for bank in (psum_kv, psum_v):
                nc.tensor.matmul(bank[:, 0:2 * W2], m.ones[:, :], m.zeros[:, 0:2 * W2], start=True, stop=False,
                                 skip_group_check=True)

            def tile(i, s, rows):
                pe.wait_ge(xn_made, i + 1)
                if reused(i):
                    pe.wait_ge(xt_made, i - 1)
                held(pe, tt)
                for c in range(2):
                    nc.tensor.transpose(pt[s][:, c * P:c * P + P], xn[s][:, c * P:c * P + P], m.ident[:, :])
                pe.drain().then_inc(xn_turned, 1)
                pe.wait_ge(xt_made, i + 1)
                if reused(i):
                    pe.wait_ge(kn_made, i - 1)
                held(pe, tt)
                for c in range(2):
                    mm = nc.tensor.matmul(pkv[s][:, :], xt[s][:, c * P:c * P + P], m.wkvT[:, c, :], start=(c == 0), stop=(c == 1))
                mm.then_inc(projected, 1)
                pe.wait_ge(kn_made, i + 1)
                held(pe, tt)
                for c in range(2):
                    nc.tensor.matmul(psum_kv[:, c * W2:c * W2 + W2], kn[s][:, c * P:c * P + P], vn[s][:, c, :],
                                     start=False, stop=False, skip_group_check=True)
                nc.tensor.matmul(psum_v[:, 0:2 * W2], m.ones[:, :], vn[s][:, :, :].rearrange("p c n -> p (c n)"),
                                 start=False, stop=False, skip_group_check=True).then_inc(kn_used, 1)

            over_tiles(pe, tile)
            for bank in (psum_kv, psum_v):
                mm = nc.tensor.matmul(bank[:, 0:2 * W2], m.ones[:, :], m.zeros[:, 0:2 * W2], start=False, stop=True,
                                      skip_group_check=True)
            mm.then_inc(sums_done, 1)
            pe.wait_ge(bd_made, 1)
            for c in range(2):
                mm = nc.tensor.matmul(pkv[c][:, 0:D], bd[:, c, :], m.wqs[:, c, :], start=True, stop=True)
            mm.then_inc(u_done, 1)
            pe.wait_ge(u_kept, 1)
            for k in range(2):
                for c in range(2):
                    mm = nc.tensor.matmul(pt[k][:, 0:D], u[:, c, k * P:k * P + P], m.woT[:, c, :], start=(c == 0), stop=(c == 1))
            mm.then_inc(m_done, 1)

        @block.scalar
        def _(act):
            def tile(i, s, rows):
                act.wait_ge(xn_made, i + 1)
                if reused(i):
                    act.wait_ge(out_rx[s], dma_count_before(i, s))
                held(act, ta)
                nc.scalar.activation(rx[s][:, :], xn[s][:, :], ACT.Relu).then_inc(rx_made, 1)
                act.wait_ge(xn_turned, i + 1)
                if reused(i):
                    act.wait_ge(out_xt[s], dma_count_before(i, s))
                    act.wait_ge(projected, i - 1)
                held(act, ta)
                nc.scalar.copy(xt[s][:, :], pt[s][:, 0:D]).then_inc(xt_made, 1)
                act.wait_ge(projected, i + 1)
                held(act, ta)
                nc.scalar.activation(sq[s][:, :], pkv[s][:, :], ACT.Square).then_inc(squared, 1)
                act.wait_ge(root_in, i + 1)
                held(act, ta)
                nc.scalar.activation(rt[:, :], va[:, :], ACT.Sqrt).then_inc(rooted, 1)

            over_tiles(act, tile)
            act.wait_ge(u_done, 1)
            for c in range(2):
                cp = nc.scalar.copy(u[:, c, :], pkv[c][:, 0:D])
            act.drain().then_inc(u_kept, 1)
            act.wait_ge(m_done, 1)
            for k in range(2):
                nc.scalar.copy(m.mixM[:, k, :], pt[k][:, 0:D])

        @block.gpsimd
        def _(pool):
            def tile(i, s, rows):
                pool.wait_ge(xn_made, i + 1)
                held(pool, tp)
                nc.gpsimd.tensor_copy(cols(m.ACC, i * AW, D), xn[s][:, :]).then_inc(xn_kept, 1)

            over_tiles(pool, tile)

        @block.sync
        def _(sp):
            def tile(i, s, rows):
                sp.wait_ge(rx_made, i + 1)
                held(sp, ts)
                sp.dma_start(m.relu_xn_table[bass.ds(i * P, P), :], rx[s][:, :]).then_inc(out_rx[s], 16)
                sp.wait_ge(xt_made, i + 1)
                held(sp, ts)
                sp.dma_start(m.xnT[bass.ds(i * P, P), :], xt[s][:, :]).then_inc(out_xt[s], 16)

            over_tiles(sp, tile)
            for s in range(2):
                sp.wait_ge(out_rx[s], dma_count(TILES - 1 - s, s))
                sp.wait_ge(out_xt[s], dma_count(TILES - 1 - s, s))


def stage_conv(nc, m, name, table):
    with Stage(nc, name) as st:
        idx = st.sb("idx", [P, 2, RING], I32)
        msg = st.sb("msg", [P, 2 * RING, D])
        S = st.sb("S", [P, 4, P])
        ps = [st.ps(f"ps{k}") for k in range(4)]
        idx_ready, got = st.sem("idx_ready"), st.sems("got", 2 * RING)
        s_made, summed, added = st.sem("s_made"), st.sem("summed"), st.sem("added")
        tv, tt, tp, ta = (st.sem(n) for n in ("turns_v", "turns_t", "turns_p", "turns_a"))
        block = st.block()

        def rounds(eng, body):
            in_twos(eng, SLOT_TILES // RING, body)

        @block.gpsimd
        def _(pool):
            def gathers(r, h):
                pool.wait_ge(idx_ready, r + 1)
                held(pool, tp)
                for k in range(RING):
                    if reused(r):
                        pool.wait_ge(summed, (r - 2) * RING + k + 1)
                        held(pool, tp)
                    pool.indirect_dma_start(msg[:, h * RING + k, :], None, table,
                                            bass.IndirectOffsetOnAxis(ap=idx[:, h, k:k + 1], axis=0)
                                            ).then_inc(got[h * RING + k], 16)

            rounds(pool, gathers)

        @block.scalar
        def _(act):
            def indices(r, h):
                if reused(r):
                    act.wait_ge(summed, (r - 1) * RING)
                    held(act, ta)
                nc.scalar.copy(idx[:, h, :], cols(m.GI, r * RING, RING)).then_inc(idx_ready, 1)

            rounds(act, indices)

        @block.vector
        def _(v):
            def one_hots(r, h):
                for k in range(RING):
                    t = r * RING + k
                    if reused(r) or k >= 4:
                        v.wait_ge(summed, t - 3)
                        held(v, tv)
                    nc.vector.tensor_scalar(S[:, k % 4, :], m.iota_row[:, :], cols(m.LOC, t, 1), None,
                                            ALU.is_equal).then_inc(s_made, 1)
                    if k >= 1 or not (isinstance(r, int) and r == 0):
                        add(t - 1, (k - 1) % 4)

            def add(t, b):
                first = v.value_load(m.bin_row[0:1, bass.ds(t, 1)], min_val=0, max_val=TILES - 1)
                v.wait_ge(summed, t + 1)
                v.wait_ge(added, t + 0) if not isinstance(t, int) or t > 0 else None
                held(v, tv)
                acc = cols(m.ACC, first * AW, D)
                nc.vector.tensor_tensor(acc, acc, ps[b][:, 0:D], ALU.add).then_inc(added, 1)

            rounds(v, one_hots)
            add(SLOT_TILES - 1, (RING - 1) % 4)

        @block.tensor
        def _(pe):
            def sums(r, h):
                for k in range(RING):
                    t = r * RING + k
                    pe.wait_ge(got[h * RING + k], (r - h) * 8 + 16)
                    pe.wait_ge(s_made, t + 1)
                    if reused(r) or k >= 4:
                        pe.wait_ge(added, t - 3)
                    held(pe, tt)
                    nc.tensor.matmul(ps[k % 4][:, 0:D], S[:, k % 4, :], msg[:, h * RING + k, :], start=True,
                                     stop=True).then_inc(summed, 1)

            rounds(pe, sums)



def stage_mlp(nc, m, name, w1, b1, w2, b2, last):
    with Stage(nc, name) as st:
        two = lambda n, w: [st.sb(f"{n}{s}", [P, w]) for s in range(2)]
        hs, ht, h1, a, b, xt = two("hs", D), two("ht", D), two("h1", D), two("a", D), two("b", D), two("xt", D)
        pt, ph, po = ([st.ps(f"{n}{s}") for s in range(2)] for n in ("pt", "ph", "po"))
        copied, turned, ht_made, h1_ps, h1_made, out_ps, out_made, kept = (
            st.sem(n) for n in ("copied", "turned", "ht_made", "h1_ps", "h1_made", "out_ps", "out_made", "kept"))
        stored, xt_in = st.sems("stored"), st.sems("xt_in")
        tv, ta, tt, tp, ts = (st.sem(n) for n in ("turns_v", "turns_a", "turns_t", "turns_p", "turns_s"))
        block = st.block()

        @block.scalar
        def _(act):
            def first(i, s):
                if reused(i):
                    act.wait_ge(turned, i - 1)
                    held(act, ta)
                nc.scalar.copy(hs[s][:, :], cols(m.ACC, i * AW, D)).then_inc(copied, 1)

            def tile(i, s, rows):
                if isinstance(i, int) and i == 0:
                    first(0, 0)
                if not (isinstance(i, int) and i == TILES - 1):
                    first(i + 1, 1 - s)
                act.wait_ge(turned, i + 1)
                if reused(i):
                    act.wait_ge(h1_ps, i - 1)
                held(act, ta)
                nc.scalar.copy(ht[s][:, :], pt[s][:, 0:D]).then_inc(ht_made, 1)
                act.wait_ge(h1_ps, i + 1)
                if reused(i):
                    act.wait_ge(out_ps, i - 1)
                held(act, ta)
                for c in range(2):
                    nc.scalar.activation(h1[s][:, c * P:c * P + P], ph[s][:, c * P:c * P + P], ACT.Relu, bias=b1[:, c:c + 1])
                act.drain().then_inc(h1_made, 1)

            over_tiles(act, tile)

        @block.tensor
        def _(pe):
            def turn(i, s):
                pe.wait_ge(copied, i + 1)
                if reused(i):
                    pe.wait_ge(ht_made, i - 1)
                held(pe, tt)
                for c in range(2):
                    tr = nc.tensor.transpose(pt[s][:, c * P:c * P + P], hs[s][:, c * P:c * P + P], m.ident[:, :])
                tr.then_inc(turned, 1)

            def second(i, s):
                pe.wait_ge(h1_made, i + 1)
                if reused(i):
                    pe.wait_ge(out_made, i - 1)
                if last:
                    pe.wait_ge(xt_in[s], dma_count(i, s))
                held(pe, tt)
                if last:
                    for c in range(2):
                        nc.tensor.matmul(po[s][:, D:2 * D], xt[s][:, c * P:c * P + P], m.mixM[:, c, :],
                                         start=(c == 0), stop=(c == 1))
                for c in range(2):
                    mm = nc.tensor.matmul(po[s][:, 0:D], h1[s][:, c * P:c * P + P], w2[:, c, :], start=(c == 0), stop=(c == 1))
                mm.then_inc(out_ps, 1)

            def tile(i, s, rows):
                if isinstance(i, int) and i == 0:
                    turn(0, 0)
                pe.wait_ge(ht_made, i + 1)
                if reused(i):
                    pe.wait_ge(h1_made, i - 1)
                held(pe, tt)
                for k in range(2):
                    for c in range(2):
                        mm = nc.tensor.matmul(ph[s][:, k * P:k * P + P], w1[:, c, k * P:k * P + P], ht[s][:, c * P:c * P + P],
                                              start=(c == 0), stop=(c == 1))
                mm.then_inc(h1_ps, 1)
                if not (isinstance(i, int) and i == TILES - 1):
                    turn(i + 1, 1 - s)
                if not (isinstance(i, int) and i == 0):
                    second(i - 1, 1 - s)

            over_tiles(pe, tile)
            second(TILES - 1, 0)

        @block.vector
        def _(v):
            def tile(i, s, rows):
                v.wait_ge(out_ps, i + 1)
                if reused(i) and not last:
                    v.wait_ge(kept, i - 1)
                    v.wait_ge(stored[s], dma_count_before(i, s))
                held(v, tv)
                nc.vector.tensor_tensor(b[s][:, :], po[s][:, 0:D], b2[:, :], ALU.add)
                if not last:
                    v.drain()
                    nc.vector.tensor_scalar(a[s][:, :], b[s][:, :], 0.0, None, ALU.max).then_inc(out_made, 1)
                    return
                nc.vector.tensor_tensor(a[s][:, :], po[s][:, D:2 * D], m.bor[:, :], ALU.add)
                v.drain().then_inc(out_made, 1)
                x = cols(m.X, i * D, D)
                nc.vector.tensor_scalar(b[s][:, :], b[s][:, :], 0.0, 2.0, ALU.max, ALU.mult)
                nc.vector.tensor_tensor(x, x, a[s][:, :], ALU.add)
                v.drain()
                nc.vector.tensor_tensor(x, x, b[s][:, :], ALU.add)

            over_tiles(v, tile)

        @block.gpsimd
        def _(pool):
            if not last:
                def tile(i, s, rows):
                    pool.wait_ge(out_made, i + 1)
                    held(pool, tp)
                    nc.gpsimd.tensor_copy(cols(m.ACC, i * AW, D), a[s][:, :]).then_inc(kept, 1)

                over_tiles(pool, tile)

        @block.sync
        def _(sp):
            def store(i, s, rows):
                sp.wait_ge(out_made, i + 1)
                held(sp, ts)
                sp.dma_start(m.conv1_table[bass.ds(i * P, P), :], a[s][:, :]).then_inc(stored[s], 16)

            def load(i, s, rows):
                if reused(i):
                    sp.wait_ge(out_ps, i - 1)
                    held(sp, ts)
                sp.dma_start(xt[s][:, :], m.xnT[bass.ds(i * P, P), :]).then_inc(xt_in[s], 16)

            over_tiles(sp, load if last else store)
            for s in range(2):
                sp.wait_ge((xt_in if last else stored)[s], dma_count(TILES - 1 - s, s))


def stage_ffn(nc, m):
    with Stage(nc, "ffn") as st:
        two = lambda n, w: [st.sb(f"{n}{s}", [P, w]) for s in range(2)]
        xn, xt, a = two("xn", D), two("xt", D), two("a", D)
        pt, po = ([st.ps(f"{n}{s}") for s in range(2)] for n in ("pt", "po"))
        xn_made, turned, xt_made, out_ps, out_read = (st.sem(n) for n in ("xn_made", "turned", "xt_made", "out_ps", "out_read"))
        tv, ta, tt = (st.sem(n) for n in ("turns_v", "turns_a", "turns_t"))
        block = st.block()

        @block.vector
        def _(v):
            def norm(i, s):
                if reused(i):
                    v.wait_ge(turned, i - 1)
                    held(v, tv)
                nc.vector.tensor_scalar(xn[s][:, :], cols(m.X, i * D, D), cols(m.mean, i, 1), cols(m.rstd, i, 1),
                                        ALU.subtract, ALU.mult).then_inc(xn_made, 1)

            def tile(i, s, rows):
                if isinstance(i, int) and i == 0:
                    norm(0, 0)
                if not (isinstance(i, int) and i == TILES - 1):
                    norm(i + 1, 1 - s)
                v.wait_ge(out_ps, i + 1)
                held(v, tv)
                nc.vector.tensor_tensor(a[s][:, :], po[s][:, 0:D], m.fbr[:, :], ALU.add)
                v.drain().then_inc(out_read, 1)
                x = cols(m.X, i * D, D)
                nc.vector.tensor_tensor(x, x, a[s][:, :], ALU.add)

            over_tiles(v, tile)

        @block.scalar
        def _(act):
            def tile(i, s, rows):
                act.wait_ge(turned, i + 1)
                if reused(i):
                    act.wait_ge(out_ps, i - 1)
                held(act, ta)
                nc.scalar.copy(xt[s][:, :], pt[s][:, 0:D]).then_inc(xt_made, 1)

            over_tiles(act, tile)

        @block.tensor
        def _(pe):
            def turn(i, s):
                pe.wait_ge(xn_made, i + 1)
                if reused(i):
                    pe.wait_ge(xt_made, i - 1)
                held(pe, tt)
                for c in range(2):
                    tr = nc.tensor.transpose(pt[s][:, c * P:c * P + P], xn[s][:, c * P:c * P + P], m.ident[:, :])
                tr.then_inc(turned, 1)

            def tile(i, s, rows):
                if isinstance(i, int) and i == 0:
                    turn(0, 0)
                if not (isinstance(i, int) and i == TILES - 1):
                    turn(i + 1, 1 - s)
                pe.wait_ge(xt_made, i + 1)
                if reused(i):
                    pe.wait_ge(out_read, i - 1)
                held(pe, tt)
                for c in range(2):
                    mm = nc.tensor.matmul(po[s][:, 0:D], xt[s][:, c * P:c * P + P], m.fT[:, c, :], start=(c == 0), stop=(c == 1))
                mm.then_inc(out_ps, 1)

            over_tiles(pe, tile)


def stage_attn_kv(nc, m):
    W2 = P + 1
    with Stage(nc, "akv") as st:
        two = lambda n, w: [st.sb(f"{n}{s}", [P, w]) for s in range(2)]
        xr, xt, g, low, ex, kp = two("xr", D), two("xt", D), two("g", 72), two("low", D), two("ex", D), two("kp", D)
        vp = [st.sb(f"vp{s}", [P, 2, W2]) for s in range(2)]
        kv_sum = st.sb("kv_sum", [P, 2 * W2])
        pt, pk, pg = ([st.ps(f"{n}{s}") for s in range(2)] for n in ("pt", "pk", "pg"))
        psum_kv = st.ps("kv")
        xr_made, turned, xt_made, projected, low_made, ex_made, kp_made, vp_made, g_made, el_kept, used, vones, sums = (
            st.sem(n) for n in ("xr_made", "turned", "xt_made", "projected", "low_made", "ex_made", "kp_made", "vp_made",
                                "g_made", "el_kept", "used", "vones", "sums"))
        out_xt, out_g = st.sems("out_xt"), st.sems("out_g")
        tv, ta, tt, tp, ts = (st.sem(n) for n in ("turns_v", "turns_a", "turns_t", "turns_p", "turns_s"))
        block = st.block()

        @block.vector
        def _(v):
            for s in range(2):
                nc.vector.memset(vp[s][:, :, :], 1.0)
            v.drain().then_inc(vones, 1)

            def norm(i, s):
                if reused(i):
                    v.wait_ge(turned, i - 1)
                    held(v, tv)
                nc.vector.tensor_scalar(xr[s][:, :], cols(m.X, i * D, D), cols(m.mean, i, 1), cols(m.rms_in, i, 1),
                                        ALU.subtract, ALU.mult).then_inc(xr_made, 1)

            def tile(i, s, rows):
                if isinstance(i, int) and i == 0:
                    norm(0, 0)
                if not (isinstance(i, int) and i == TILES - 1):
                    norm(i + 1, 1 - s)
                v.wait_ge(projected, i + 1)
                if reused(i):
                    v.wait_ge(ex_made, i - 1)
                held(v, tv)
                nc.vector.tensor_scalar(low[s][:, :], pk[s][:, 0:D], 0.0, None, ALU.min).then_inc(low_made, 1)
                v.wait_ge(ex_made, i + 1)
                if reused(i):
                    v.wait_ge(used, i - 1)
                held(v, tv)
                nc.vector.scalar_tensor_tensor(out=kp[s][:, :], in0=pk[s][:, 0:D], scalar=0.0, in1=ex[s][:, :],
                                               op0=ALU.max, op1=ALU.add).then_inc(kp_made, 1)

            over_tiles(v, tile)
            v.wait_ge(sums, 1)
            nc.vector.tensor_copy(kv_sum[:, :], psum_kv[:, 0:2 * W2])
            v.drain()
            for c in range(2):
                lo = c * W2
                nc.vector.tensor_tensor(m.kvbd[:, c, 0:P], kv_sum[:, lo:lo + P], m.mask32[:, :], ALU.mult)
                nc.vector.tensor_scalar(m.kvbd[:, c, P:P + 4], m.mask32[:, 0:P:32], kv_sum[:, lo + P:lo + P + 1], None, ALU.mult)

        @block.scalar
        def _(act):
            act.wait_ge(vones, 1)

            def tile(i, s, rows):
                act.wait_ge(turned, i + 1)
                if reused(i):
                    act.wait_ge(projected, i - 1)
                    act.wait_ge(out_xt[s], dma_count_before(i, s))
                held(act, ta)
                nc.scalar.copy(xt[s][:, :], pt[s][:, 0:D]).then_inc(xt_made, 1)
                act.wait_ge(projected, i + 1)
                if reused(i):
                    act.wait_ge(el_kept, i - 1)
                    act.wait_ge(out_g[s], dma_count_before(i, s))
                    act.wait_ge(used, i - 1)
                held(act, ta)
                nc.scalar.activation(g[s][:, :], pg[s][:, 0:72], ACT.Copy, scale=cols(m.rms_out, i, 1)).then_inc(g_made, 1)
                nc.scalar.copy(vp[s][:, :, 0:P], pg[s][:, D:2 * D].rearrange("p (c n) -> p c n", c=2)).then_inc(vp_made, 1)
                act.wait_ge(low_made, i + 1)
                if reused(i):
                    act.wait_ge(kp_made, i - 1)
                held(act, ta)
                nc.scalar.activation(ex[s][:, :], low[s][:, :], ACT.Exp).then_inc(ex_made, 1)

            over_tiles(act, tile)

        @block.tensor
        def _(pe):
            nc.tensor.matmul(psum_kv[:, 0:2 * W2], m.ones[:, :], m.zeros[:, 0:2 * W2], start=True, stop=False, skip_group_check=True)

            def turn(i, s):
                pe.wait_ge(xr_made, i + 1)
                if reused(i):
                    pe.wait_ge(xt_made, i - 1)
                held(pe, tt)
                for c in range(2):
                    tr = nc.tensor.transpose(pt[s][:, c * P:c * P + P], xr[s][:, c * P:c * P + P], m.ident[:, :])
                tr.then_inc(turned, 1)

            def gather_sums(i, s, rows):
                pe.wait_ge(kp_made, i + 1)
                pe.wait_ge(vp_made, i + 1)
                held(pe, tt)
                for c in range(2):
                    mm = nc.tensor.matmul(psum_kv[:, c * W2:c * W2 + W2], kp[s][0:rows, c * P:c * P + P], vp[s][0:rows, c, :],
                                          start=False, stop=False, skip_group_check=True)
                mm.then_inc(used, 1)

            def tile(i, s, rows):
                if isinstance(i, int) and i == 0:
                    turn(0, 0)
                if not (isinstance(i, int) and i == TILES - 1):
                    turn(i + 1, 1 - s)
                pe.wait_ge(xt_made, i + 1)
                if reused(i):
                    pe.wait_ge(kp_made, i - 1)
                    pe.wait_ge(vp_made, i - 1)
                    pe.wait_ge(g_made, i - 1)
                held(pe, tt)
                for c in range(2):
                    nc.tensor.matmul(pg[s][:, 0:72], xt[s][:, c * P:c * P + P], m.gcat[:, c, :], start=(c == 0), stop=(c == 1))
                for c in range(2):
                    nc.tensor.matmul(pg[s][:, D:2 * D], xt[s][:, c * P:c * P + P], m.wqkvs[:, c, 2 * D:3 * D], start=(c == 0), stop=(c == 1))
                for c in range(2):
                    mm = nc.tensor.matmul(pk[s][:, 0:D], xt[s][:, c * P:c * P + P], m.wqkvs[:, c, D:2 * D], start=(c == 0), stop=(c == 1))
                mm.then_inc(projected, 1)
                if not (isinstance(i, int) and i == 0):
                    gather_sums(i - 1, 1 - s, P)

            over_tiles(pe, tile)
            gather_sums(TILES - 1, 0, TAIL)
            nc.tensor.matmul(psum_kv[:, 0:2 * W2], m.ones[:, :], m.zeros[:, 0:2 * W2], start=False, stop=True,
                             skip_group_check=True).then_inc(sums, 1)

        @block.gpsimd
        def _(pool):
            def tile(i, s, rows):
                pool.wait_ge(g_made, i + 1)
                held(pool, tp)
                nc.gpsimd.tensor_copy(cols(m.EL, i * 4, 4), g[s][:, 68:72]).then_inc(el_kept, 1)

            over_tiles(pool, tile)

        @block.sync
        def _(sp):
            def tile(i, s, rows):
                sp.wait_ge(xt_made, i + 1)
                held(sp, ts)
                sp.dma_start(m.xrT[bass.ds(i * P, P), :], xt[s][:, :]).then_inc(out_xt[s], 16)
                sp.wait_ge(g_made, i + 1)
                held(sp, ts)
                sp.dma_start(m.attn_table[bass.ds(i * P, P), :], g[s][:, 0:GW]).then_inc(out_g[s], 16)

            over_tiles(sp, tile)
            for s in range(2):
                sp.wait_ge(out_xt[s], dma_count(TILES - 1 - s, s))
                sp.wait_ge(out_g[s], dma_count(TILES - 1 - s, s))


def stage_attn_q(nc, m):
    with Stage(nc, "aq") as st:
        two = lambda n, w: [st.sb(f"{n}{s}", [P, w]) for s in range(2)]
        xt, low, ex, qp, o, ot, h = (two(n, D) for n in ("xt", "low", "ex", "qp", "o", "ot", "h"))
        den = st.sb("den", [P, 2, 4])
        z = st.sb("z", [P, 2, 4])
        pq, pn, pt, po = ([st.ps(f"{n}{s}") for s in range(2)] for n in ("pq", "pn", "pt", "po"))
        q_ps, low_made, ex_made, qp_made, n_ps, o_made, turned, ot_made, out_ps, h_made = (
            st.sem(n) for n in ("q_ps", "low_made", "ex_made", "qp_made", "n_ps", "o_made", "turned", "ot_made",
                                "out_ps", "h_made"))
        xt_in = st.sems("xt_in")
        tv, ta, tt, ts = (st.sem(n) for n in ("turns_v", "turns_a", "turns_t", "turns_s"))
        block = st.block()
        W = P + 4
        edge = lambda i, e: isinstance(i, int) and i == e

        @block.sync
        def _(sp):
            def load(i, s, rows):
                if reused(i):
                    sp.wait_ge(q_ps, i - 1)
                    held(sp, ts)
                sp.dma_start(xt[s][:, :], m.xrT[bass.ds(i * P, P), :]).then_inc(xt_in[s], 16)

            over_tiles(sp, load)

        @block.tensor
        def _(pe):
            def queries(i, s):
                pe.wait_ge(xt_in[s], dma_count(i, s))
                if reused(i):
                    pe.wait_ge(qp_made, i - 1)
                held(pe, tt)
                for k in range(2):
                    for c in range(2):
                        mm = nc.tensor.matmul(pq[s][:, k * P:k * P + P], m.wqkvs[:, c, k * P:k * P + P], xt[s][:, c * P:c * P + P],
                                              start=(c == 0), stop=(c == 1))
                mm.then_inc(q_ps, 1)

            def back(i, s):
                pe.wait_ge(o_made, i + 1)
                if reused(i):
                    pe.wait_ge(ot_made, i - 1)
                held(pe, tt)
                for c in range(2):
                    tr = nc.tensor.transpose(pt[s][:, c * P:c * P + P], o[s][:, c * P:c * P + P], m.ident[:, :])
                tr.then_inc(turned, 1)
                pe.wait_ge(ot_made, i + 1)
                if reused(i):
                    pe.wait_ge(h_made, i - 1)
                held(pe, tt)
                for c in range(2):
                    mm = nc.tensor.matmul(po[s][:, 0:D], ot[s][:, c * P:c * P + P], m.wouts[:, c, :], start=(c == 0), stop=(c == 1))
                mm.then_inc(out_ps, 1)

            def tile(i, s, rows):
                if edge(i, 0):
                    queries(0, 0)
                pe.wait_ge(qp_made, i + 1)
                if reused(i):
                    pe.wait_ge(o_made, i - 1)
                held(pe, tt)
                for c in range(2):
                    mm = nc.tensor.matmul(pn[s][:, c * W:c * W + W], qp[s][:, c * P:c * P + P], m.kvbd[:, c, :], start=True, stop=True)
                mm.then_inc(n_ps, 1)
                if not edge(i, TILES - 1):
                    queries(i + 1, 1 - s)
                back(i, s)

            over_tiles(pe, tile)

        @block.scalar
        def _(act):
            def exps(i, s):
                act.wait_ge(low_made, i + 1)
                if reused(i):
                    act.wait_ge(qp_made, i - 1)
                held(act, ta)
                nc.scalar.activation(ex[s][:, :], low[s][:, :], ACT.Exp).then_inc(ex_made, 1)

            def tile(i, s, rows):
                if edge(i, 0):
                    exps(0, 0)
                act.wait_ge(turned, i + 1)
                if reused(i):
                    act.wait_ge(out_ps, i - 1)
                held(act, ta)
                nc.scalar.copy(ot[s][:, :], pt[s][:, 0:D]).then_inc(ot_made, 1)
                if not edge(i, TILES - 1):
                    exps(i + 1, 1 - s)

            over_tiles(act, tile)

        @block.vector
        def _(v):
            def low_of(i, s):
                v.wait_ge(q_ps, i + 1)
                if reused(i):
                    v.wait_ge(ex_made, i - 1)
                held(v, tv)
                nc.vector.tensor_scalar(low[s][:, :], pq[s][:, 0:D], 0.0, None, ALU.min).then_inc(low_made, 1)

            def tile(i, s, rows):
                if edge(i, 0):
                    low_of(0, 0)
                v.wait_ge(ex_made, i + 1)
                if reused(i):
                    v.wait_ge(n_ps, i - 1)
                held(v, tv)
                nc.vector.scalar_tensor_tensor(out=qp[s][:, :], in0=pq[s][:, 0:D], scalar=0.0, in1=ex[s][:, :],
                                               op0=ALU.max, op1=ALU.add).then_inc(qp_made, 1)
                nc.vector.tensor_scalar(h[s][:, :], cols(m.X, i * D, D), cols(m.mean, i, 1), cols(m.rstd, i, 1),
                                        ALU.subtract, ALU.mult)
                v.drain()
                nc.vector.tensor_tensor(h[s][:, :], h[s][:, :], m.boutr[:, :], ALU.add)
                v.wait_ge(n_ps, i + 1)
                if reused(i):
                    v.wait_ge(turned, i - 1)
                held(v, tv)
                n3 = pn[s][:, 0:2 * W].rearrange("p (c n) -> p c n", c=2)
                nc.vector.tensor_scalar(den[:, :, :], n3[:, :, P:W], 1e-6, None, ALU.add)
                v.drain()
                nc.vector.reciprocal(z[:, :, :], den[:, :, :])
                v.drain()
                for c in range(2):
                    op = nc.vector.tensor_tensor(o[s][:, c * P:c * P + P].rearrange("p (g j) -> p g j", j=32),
                                                 n3[:, c, 0:P].rearrange("p (g j) -> p g j", j=32),
                                                 z[:, c, :].unsqueeze(2).broadcast_to([P, 4, 32]), ALU.mult)
                op.then_inc(o_made, 1)
                if not edge(i, TILES - 1):
                    low_of(i + 1, 1 - s)
                v.wait_ge(out_ps, i + 1)
                held(v, tv)
                nc.vector.tensor_tensor(cols(m.ACC, i * AW, D), po[s][:, 0:D], h[s][:, :], ALU.add).then_inc(h_made, 1)

            over_tiles(v, tile)


def stage_attn_add(nc, m):
    with Stage(nc, "aadd") as st:
        parts = st.sb("parts", [P, TILES * 6])
        a, b, r = (st.sb(n, [P, TILES]) for n in ("a", "b", "r"))
        t = [st.sb(f"t{s}", [P, D]) for s in range(2)]
        ready, rooted = st.sem("ready"), st.sem("rooted")
        block = st.block()

        @block.vector
        def _(v):
            with v.Fori(0, TILES) as i:
                nc.vector.bn_stats(parts[:, bass.ds(i * 6, 6)], cols(m.ACC, i * AW, D))
            v.drain()
            f = lambda k: parts[:, :].rearrange("p (i s) -> p i s", s=6)[:, :, k]
            nc.vector.tensor_tensor(r[:, :], f(2), f(5), ALU.add)
            nc.vector.tensor_tensor(a[:, :], f(1), f(1), ALU.mult)
            nc.vector.tensor_tensor(b[:, :], f(4), f(4), ALU.mult)
            v.drain()
            nc.vector.tensor_tensor(a[:, :], a[:, :], b[:, :], ALU.add)
            nc.vector.tensor_scalar(r[:, :], r[:, :], 1.0 / D, 1e-6, ALU.mult, ALU.add)
            v.drain()
            nc.vector.scalar_tensor_tensor(out=b[:, :], in0=a[:, :], scalar=0.5, in1=r[:, :], op0=ALU.mult, op1=ALU.add)
            v.drain().then_inc(ready, 1)
            v.wait_ge(rooted, 1)
            nc.vector.reciprocal(r[:, :], a[:, :])
            v.drain()

            def tile(i, s, rows):
                h, x = cols(m.ACC, i * AW, D), cols(m.X, i * D, D)
                nc.vector.tensor_tensor(t[s][:, :], h, m.mw2r[:, :], ALU.mult)
                v.drain()
                nc.vector.scalar_tensor_tensor(out=t[s][:, :], in0=t[s][:, :], scalar=cols(r, i, 1), in1=h, op0=ALU.mult, op1=ALU.add)
                v.drain()
                nc.vector.tensor_tensor(x, x, t[s][:, :], ALU.add)

            over_tiles(v, tile)

        @block.scalar
        def _(act):
            act.wait_ge(ready, 1)
            nc.scalar.activation(a[:, :], b[:, :], ACT.Sqrt).then_inc(rooted, 1)


def stage_gat(nc, m):
    with Stage(nc, "gat") as st:
        idx = st.sb("idx", [P, 2, RING], I32)
        msg = st.sb("msg", [P, 2 * RING, GW])
        S = st.sb("S", [P, 4, P])
        ST = st.sb("ST", [P, 4, P])
        M = st.sb("M", [P, 4, AW])
        zz = st.sb("zz", [P, 4, 4])
        lk = st.sb("lk", [P, 4, 4])
        rs, o, ex = ([st.sb(f"{n}{s}", [P, w]) for s in range(2)] for n, w in (("rs", 4), ("o", D), ("ex", D)))
        pst = [st.ps(f"pst{k}") for k in range(2)]
        pel = [st.ps(f"pel{k}") for k in range(2)]
        ps = [st.ps(f"ps{k}") for k in range(4)]
        idx_ready, got = st.sem("idx_ready"), st.sems("got", 2 * RING)
        s_made, turned, st_made, el_made, lk_made, e_made, m_made, summed, added = (
            st.sem(n) for n in ("s_made", "turned", "st_made", "el_made", "lk_made", "e_made", "m_made", "summed", "added"))
        low_made, ex_made = st.sem("low_made"), st.sem("ex_made")
        tv, tt, tp, ta = (st.sem(n) for n in ("turns_v", "turns_t", "turns_p", "turns_a"))
        block = st.block()
        early = lambda r, k, n: isinstance(r, int) and r * RING + k < n

        def rounds(eng, body):
            in_twos(eng, SLOT_TILES // RING, body)

        @block.gpsimd
        def _(pool):
            def gathers(r, h):
                pool.wait_ge(idx_ready, r + 1)
                held(pool, tp)
                for k in range(RING):
                    if reused(r):
                        pool.wait_ge(m_made, (r - 2) * RING + k + 1)
                        held(pool, tp)
                    pool.indirect_dma_start(msg[:, h * RING + k, :], None, m.attn_table,
                                            bass.IndirectOffsetOnAxis(ap=idx[:, h, k:k + 1], axis=0)
                                            ).then_inc(got[h * RING + k], 16)

            rounds(pool, gathers)

        @block.scalar
        def _(act):
            def exps(t, b):
                act.wait_ge(lk_made, t + 1)
                if not isinstance(t, int) or t >= 4:
                    act.wait_ge(summed, t - 3)
                held(act, ta)
                nc.scalar.activation(M[:, b, D:AW], lk[:, b, :], ACT.Exp).then_inc(e_made, 1)

            def tile(r, h):
                if reused(r):
                    act.wait_ge(m_made, (r - 1) * RING)
                    held(act, ta)
                nc.scalar.copy(idx[:, h, :], cols(m.GI, r * RING, RING)).then_inc(idx_ready, 1)
                for k in range(RING):
                    t = r * RING + k
                    act.wait_ge(turned, t + 1)
                    if not early(r, k, 4):
                        act.wait_ge(el_made, t - 3)
                    held(act, ta)
                    nc.scalar.copy(ST[:, k % 4, :], pst[k % 2][:, 0:P]).then_inc(st_made, 1)
                    if not early(r, k, 1):
                        exps(t - 1, (k - 1) % 4)

            rounds(act, tile)
            exps(SLOT_TILES - 1, 3)

            def exp_tile(i, s, rows):
                act.wait_ge(low_made, i + 1)
                held(act, ta)
                nc.scalar.activation(ex[s][:, :], ex[s][:, :], ACT.Exp).then_inc(ex_made, 1)

            over_tiles(act, exp_tile)

        @block.tensor
        def _(pe):
            def el_of(t, b):
                first = pe.value_load(m.bin_row[0:1, bass.ds(t, 1)], min_val=0, max_val=TILES - 1)
                pe.wait_ge(st_made, t + 1)
                if not isinstance(t, int) or t >= 2:
                    pe.wait_ge(lk_made, t - 1)
                held(pe, tt)
                nc.tensor.matmul(pel[b % 2][:, 0:4], ST[:, b, :], cols(m.EL, first * 4, 4), start=True,
                                 stop=True).then_inc(el_made, 1)

            def sums(t, b):
                pe.wait_ge(m_made, t + 1)
                if not isinstance(t, int) or t >= 4:
                    pe.wait_ge(added, t - 3)
                held(pe, tt)
                nc.tensor.matmul(ps[b][:, 0:AW], S[:, b, :], M[:, b, :], start=True, stop=True).then_inc(summed, 1)

            def tile(r, h):
                for k in range(RING):
                    t = r * RING + k
                    pe.wait_ge(s_made, t + 1)
                    if not early(r, k, 2):
                        pe.wait_ge(st_made, t - 1)
                    held(pe, tt)
                    nc.tensor.transpose(pst[k % 2][:, 0:P], S[:, k % 4, :], m.ident[:, :]).then_inc(turned, 1)
                    if not early(r, k, 1):
                        el_of(t - 1, (k - 1) % 4)
                    if not early(r, k, 3):
                        sums(t - 3, (k - 3) % 4)

            rounds(pe, tile)
            n = SLOT_TILES
            el_of(n - 1, 3)
            for t in (n - 3, n - 2, n - 1):
                sums(t, t % 4)

        @block.vector
        def _(v):
            nc.vector.memset(m.ACC[:, :], 0.0)
            v.drain()

            def leaky(t, b, q, g):
                v.wait_ge(el_made, t + 1)
                v.wait_ge(got[q], g)
                if not isinstance(t, int) or t >= 4:
                    v.wait_ge(e_made, t - 3)
                held(v, tv)
                nc.vector.tensor_tensor(zz[:, b, :], pel[b % 2][:, 0:4], msg[:, q, 64:GW], ALU.add)
                v.drain()
                nc.vector.scalar_tensor_tensor(out=lk[:, b, :], in0=zz[:, b, :], scalar=0.2, in1=zz[:, b, :],
                                               op0=ALU.mult, op1=ALU.max).then_inc(lk_made, 1)

            def weigh(t, b, q):
                v.wait_ge(e_made, t + 1)
                if not isinstance(t, int) or t >= 4:
                    v.wait_ge(summed, t - 3)
                held(v, tv)
                nc.vector.tensor_tensor(M[:, b, 0:D].rearrange("p (g j) -> p g j", j=64),
                                        msg[:, q, 0:64].unsqueeze(1).broadcast_to([P, 4, 64]),
                                        M[:, b, D:AW].unsqueeze(2).broadcast_to([P, 4, 64]), ALU.mult).then_inc(m_made, 1)

            def add(t, b):
                first = v.value_load(m.bin_row[0:1, bass.ds(t, 1)], min_val=0, max_val=TILES - 1)
                v.wait_ge(summed, t + 1)
                if not isinstance(t, int) or t > 0:
                    v.wait_ge(added, t)
                held(v, tv)
                acc = cols(m.ACC, first * AW, AW)
                nc.vector.tensor_tensor(acc, acc, ps[b][:, 0:AW], ALU.add).then_inc(added, 1)

            def tile(r, h):
                for k in range(RING):
                    t = r * RING + k
                    q = lambda n: (h * RING + k - n) % (2 * RING)
                    if not early(r, k, 4):
                        v.wait_ge(summed, t - 3)
                        held(v, tv)
                    nc.vector.tensor_scalar(S[:, k % 4, :], m.iota_row[:, :], cols(m.LOC, t, 1), None,
                                            ALU.is_equal).then_inc(s_made, 1)
                    if not early(r, k, 1):
                        g = (r - h) * 8 + 16 if h * RING + k >= 1 else (r - h) * 8
                        leaky(t - 1, (k - 1) % 4, q(1), g)
                    if not early(r, k, 2):
                        weigh(t - 2, (k - 2) % 4, q(2))
                    if not early(r, k, 4):
                        add(t - 4, k % 4)

            rounds(v, tile)
            n = SLOT_TILES
            leaky(n - 1, 3, (n - 1) % (2 * RING), (SLOT_TILES // RING) * 8)
            weigh(n - 2, 2, (n - 2) % (2 * RING))
            weigh(n - 1, 3, (n - 1) % (2 * RING))
            for t in range(n - 4, n):
                add(t, t % 4)
            v.drain()

            def heads(i, s):
                acc = cols(m.ACC, i * AW, D)
                nc.vector.tensor_scalar(rs[s][:, :], cols(m.ACC, i * AW + D, 4), 1e-12, None, ALU.max)
                v.drain()
                nc.vector.reciprocal(rs[s][:, :], rs[s][:, :])
                v.drain()
                o3 = o[s][:, :].rearrange("p (g j) -> p g j", j=64)
                nc.vector.tensor_tensor(o3, acc.rearrange("p (g j) -> p g j", j=64),
                                        rs[s][:, :].unsqueeze(2).broadcast_to([P, 4, 64]), ALU.mult)
                v.drain()
                nc.vector.tensor_tensor(o3, o3, m.gbr[:, :].unsqueeze(1).broadcast_to([P, 4, 64]), ALU.add)
                v.drain()
                nc.vector.tensor_scalar(ex[s][:, :], o[s][:, :], 0.0, None, ALU.min).then_inc(low_made, 1)

            def finish(i, s):
                v.wait_ge(ex_made, i + 1)
                held(v, tv)
                x = cols(m.X, i * D, D)
                nc.vector.scalar_tensor_tensor(out=o[s][:, :], in0=o[s][:, :], scalar=0.0, in1=ex[s][:, :], op0=ALU.max, op1=ALU.add)
                v.drain()
                nc.vector.scalar_tensor_tensor(out=x, in0=o[s][:, :], scalar=-1.0, in1=x, op0=ALU.add, op1=ALU.add)
                v.drain()

            def out_tile(i, s, rows):
                heads(i, s)
                if not (isinstance(i, int) and i == 0):
                    finish(i - 1, 1 - s)

            over_tiles(v, out_tile)
            finish(TILES - 1, 0)


def stage_router(nc, m):
    with Stage(nc, "router") as st:
        two = lambda n, w: [st.sb(f"{n}{s}", [P, w]) for s in range(2)]
        t, t2, xm, xt = (two(n, D) for n in ("t", "u", "xm", "xt"))
        pt, pl = ([st.ps(f"{n}{s}") for s in range(2)] for n in ("pt", "pl"))
        xm_made, turned, xt_made, l_ps, l_read, zeroed = (
            st.sem(n) for n in ("xm_made", "turned", "xt_made", "l_ps", "l_read", "zeroed"))
        out_xm, zero_out = st.sems("out_xm"), st.sem("zero_out")
        tv, ta, tt, ts = (st.sem(n) for n in ("turns_v", "turns_a", "turns_t", "turns_s"))
        zrow = st.sb("zrow", [P, 2 * D])
        block = st.block()

        @block.gpsimd
        def _(pool):
            nc.gpsimd.memset(zrow[:, :], 0.0).then_inc(zeroed, 1)

        @block.vector
        def _(v):
            def norm(i, s):
                nc.vector.tensor_scalar(t[s][:, :], cols(m.X, i * D, D), cols(m.mean, i, 1), cols(m.rstd, i, 1),
                                        ALU.subtract, ALU.mult)
                v.drain()
                nc.vector.tensor_tensor(t2[s][:, :], t[s][:, :], m.gammar[:, :], ALU.mult)
                if reused(i):
                    v.wait_ge(turned, i - 1)
                    v.wait_ge(out_xm[s], dma_count_before(i, s))
                    held(v, tv)
                v.drain()
                nc.vector.tensor_tensor(xm[s][:, :], t2[s][:, :], m.betar[:, :], ALU.add).then_inc(xm_made, 1)

            def tile(i, s, rows):
                if isinstance(i, int) and i == 0:
                    norm(0, 0)
                if not (isinstance(i, int) and i == TILES - 1):
                    norm(i + 1, 1 - s)
                v.wait_ge(l_ps, i + 1)
                held(v, tv)
                nc.vector.tensor_tensor(cols(m.L, i * EXPERTS, EXPERTS), pl[s][:, 0:EXPERTS], m.rbr[:, :], ALU.add).then_inc(l_read, 1)

            over_tiles(v, tile)

        @block.scalar
        def _(act):
            def tile(i, s, rows):
                act.wait_ge(turned, i + 1)
                if reused(i):
                    act.wait_ge(l_ps, i - 1)
                held(act, ta)
                nc.scalar.copy(xt[s][:, :], pt[s][:, 0:D]).then_inc(xt_made, 1)

            over_tiles(act, tile)

        @block.tensor
        def _(pe):
            def turn(i, s):
                pe.wait_ge(xm_made, i + 1)
                if reused(i):
                    pe.wait_ge(xt_made, i - 1)
                held(pe, tt)
                for c in range(2):
                    tr = nc.tensor.transpose(pt[s][:, c * P:c * P + P], xm[s][:, c * P:c * P + P], m.ident[:, :])
                tr.then_inc(turned, 1)

            def tile(i, s, rows):
                if isinstance(i, int) and i == 0:
                    turn(0, 0)
                if not (isinstance(i, int) and i == TILES - 1):
                    turn(i + 1, 1 - s)
                pe.wait_ge(xt_made, i + 1)
                if reused(i):
                    pe.wait_ge(l_read, i - 1)
                held(pe, tt)
                for c in range(2):
                    mm = nc.tensor.matmul(pl[s][:, 0:EXPERTS], xt[s][:, c * P:c * P + P], m.rWs[:, c, :], start=(c == 0), stop=(c == 1))
                mm.then_inc(l_ps, 1)

            over_tiles(pe, tile)

        @block.sync
        def _(sp):
            sp.wait_ge(zeroed, 1)
            rows = m.expert_in.rearrange("(t p a) d -> t p (a d)", p=P, a=2)
            for k in range(EX_TILES // 2):
                sp.dma_start(rows[k], zrow[:, :]).then_inc(zero_out, 16)

            def tile(i, s, n):
                sp.wait_ge(xm_made, i + 1)
                held(sp, ts)
                sp.dma_start(m.xm[bass.ds(i * P, P), :], xm[s][:, :]).then_inc(out_xm[s], 16)

            over_tiles(sp, tile)
            for s in range(2):
                sp.wait_ge(out_xm[s], dma_count(TILES - 1 - s, s))
            sp.wait_ge(zero_out, 16 * (EX_TILES // 2))


def stage_route(nc, m):
    with Stage(nc, "route") as st:
        T8 = [P, TILES, EXPERTS]
        l3 = m.L[:, :].rearrange("p (i e) -> p i e", e=EXPERTS)
        cand, oh1, oh2, both, pre, scan, other, l2 = (st.sb(n, T8) for n in ("cand", "oh1", "oh2", "both", "pre", "scan", "other", "l2"))
        m1, m2, i1, pr = (st.sb(n, [P, TILES]) for n in ("m1", "m2", "i1", "pr"))
        valid = st.sb("valid", [P, 1])
        cnt, nt, te, tx, sp8 = (st.sb(n, [P, EXPERTS]) for n in ("cnt", "nt", "te", "tx", "sp8"))
        ni = st.sb("ni", [P, EXPERTS], I32)
        cmp = st.sb("cmp", [1, P, EXPERTS])
        exf = st.sb("exf", [1, P])
        pre_ps, tot_ps = st.ps("pre_ps"), st.ps("tot_ps")
        diff, powed, oh_made, counted = (st.sem(n) for n in ("diff", "powed", "oh_made", "counted"))
        block = st.block()
        f = lambda t: t[:, :, :].rearrange("p i e -> p (i e)")
        over = lambda t: t.unsqueeze(2).broadcast_to(T8)
        exps = m.iota_row[:, 0:EXPERTS].unsqueeze(1).broadcast_to(T8)

        @block.vector
        def _(v):
            def pick(logits, best, chosen):
                nc.vector.tensor_reduce(best[:, :], logits, X_AXIS, ALU.max)
                v.drain()
                nc.vector.tensor_tensor(cand[:, :, :], logits, over(best[:, :]), ALU.is_equal)
                v.drain()
                nc.vector.tensor_scalar(cand[:, :, :], cand[:, :, :], -float(EXPERTS), float(EXPERTS), ALU.mult, ALU.add)
                v.drain()
                nc.vector.tensor_tensor(cand[:, :, :], cand[:, :, :], exps, ALU.add)
                v.drain()
                nc.vector.tensor_reduce(i1[:, :], cand[:, :, :], X_AXIS, ALU.min)
                v.drain()
                nc.vector.tensor_tensor(chosen[:, :, :], exps, over(i1[:, :]), ALU.is_equal)
                v.drain()

            pick(l3, m1, oh1)
            nc.vector.scalar_tensor_tensor(out=l2[:, :, :], in0=oh1[:, :, :], scalar=-3.0e38, in1=l3, op0=ALU.mult, op1=ALU.add)
            v.drain()
            pick(l2[:, :, :], m2, oh2)
            nc.vector.tensor_tensor(pr[:, :], m2[:, :], m1[:, :], ALU.subtract)
            v.drain().then_inc(diff, 1)
            nc.vector.tensor_scalar(valid[:, :], m.slot_no[:, 0:1], float(TAIL), None, ALU.is_lt)
            nc.vector.tensor_tensor(both[:, :, :], oh1[:, :, :], oh2[:, :, :], ALU.add)
            v.drain()
            nc.vector.tensor_scalar(both[:, TILES - 1, :], both[:, TILES - 1, :], valid[:, :], None, ALU.mult)
            v.drain().then_inc(oh_made, 1)
            v.wait_ge(powed, 1)
            nc.vector.tensor_scalar(m1[:, :], pr[:, :], 1.0, None, ALU.add)
            v.drain()
            nc.vector.reciprocal(m.gate[:, 0, :], m1[:, :])
            v.drain()
            nc.vector.tensor_tensor(m.gate[:, 1, :], m.gate[:, 0, :], pr[:, :], ALU.mult)
            v.wait_ge(counted, 1)
            nc.vector.tensor_copy(f(pre), pre_ps[:, 0:TILES * EXPERTS])
            nc.vector.tensor_copy(f(scan), tot_ps[:, 0:TILES * EXPERTS])
            v.drain()
            nc.vector.tensor_tensor(f(pre), f(pre), f(scan), ALU.subtract)
            a, b, w = scan, other, 1
            while w < TILES:
                v.drain()
                nc.vector.tensor_tensor(b[:, w:TILES, :], a[:, w:TILES, :], a[:, 0:TILES - w, :], ALU.add)
                nc.vector.tensor_copy(b[:, 0:w, :], a[:, 0:w, :])
                a, b, w = b, a, 2 * w
            v.drain()
            nc.vector.tensor_scalar(cnt[:, :], a[:, TILES - 1, :], float(P - 1), None, ALU.add)
            nc.vector.tensor_tensor(pre[:, :, :], pre[:, :, :], a[:, :, :], ALU.add)
            v.drain()
            nc.vector.tensor_copy(ni[:, :], cnt[:, :])
            v.drain()
            nc.vector.tensor_scalar(ni[:, :], ni[:, :], 7, None, ALU.logical_shift_right)
            v.drain()
            nc.vector.tensor_copy(nt[:, :], ni[:, :])
            nc.vector.tensor_copy(te[:, :], ni[:, :])
            x, y, w = te, tx, 1
            while w < EXPERTS:
                v.drain()
                nc.vector.tensor_tensor(y[:, w:EXPERTS], x[:, w:EXPERTS], x[:, 0:EXPERTS - w], ALU.add)
                nc.vector.tensor_copy(y[:, 0:w], x[:, 0:w])
                x, y, w = y, x, 2 * w
            v.drain()
            nc.vector.tensor_tensor(sp8[:, :], x[:, :], nt[:, :], ALU.subtract)
            nc.vector.tensor_tensor(cmp[:, :, :], x[0:1, :].unsqueeze(1).broadcast_to([1, P, EXPERTS]),
                                    m.iota_row[0:1, :].unsqueeze(2).broadcast_to([1, P, EXPERTS]), ALU.is_le)
            v.drain()
            nc.vector.tensor_reduce(exf[:, :], cmp[:, :, :], X_AXIS, ALU.add)
            nc.vector.tensor_scalar(sp8[:, :], sp8[:, :], float(P), None, ALU.mult)
            v.drain()
            nc.vector.tensor_scalar(exf[:, :], exf[:, :], float(EXPERTS - 1), None, ALU.min)
            nc.vector.tensor_tensor(pre[:, :, :], pre[:, :, :], sp8[:, :].unsqueeze(1).broadcast_to(T8), ALU.add)
            v.drain()
            nc.vector.tensor_copy(m.exp_row[:, :], exf[:, :])
            for k, oh in enumerate((oh1, oh2)):
                nc.vector.tensor_tensor(cand[:, :, :], pre[:, :, :], oh[:, :, :], ALU.mult)
                v.drain()
                nc.vector.tensor_reduce(i1[:, :], cand[:, :, :], X_AXIS, ALU.add)
                v.drain()
                nc.vector.tensor_copy(m.pos_i[:, k, :], i1[:, :])
                v.drain()

        @block.scalar
        def _(act):
            act.wait_ge(diff, 1)
            nc.scalar.activation(pr[:, :], pr[:, :], ACT.Exp).then_inc(powed, 1)

        @block.tensor
        def _(pe):
            pe.wait_ge(oh_made, 1)
            nc.tensor.matmul(pre_ps[:, 0:TILES * EXPERTS], m.tri[:, :], f(both), start=True, stop=True)
            nc.tensor.matmul(tot_ps[:, 0:TILES * EXPERTS], m.ones[:, :], f(both), start=True, stop=True)
            pe.drain().then_inc(counted, 1)


def stage_dispatch(nc, m):
    with Stage(nc, "dispatch") as st:
        xm = [st.sb(f"xm{s}", [P, D]) for s in range(2)]
        at = [st.sb(f"at{s}", [P, 2], I32) for s in range(2)]
        xm_in, at_made, sent, w_in = st.sems("xm_in"), st.sem("at_made"), st.sems("sent"), st.sem("w_in")
        ta, tp, ts = (st.sem(n) for n in ("turns_a", "turns_p", "turns_s"))
        block = st.block()

        @block.sync
        def _(sp):
            def load(i, s, rows):
                if reused(i):
                    sp.wait_ge(sent[s], 2 * dma_count_before(i, s))
                    held(sp, ts)
                sp.dma_start(xm[s][:, :], m.xm[bass.ds(i * P, P), :]).then_inc(xm_in[s], 16)

            over_tiles(sp, load)
            n = 0
            for e in range(EXPERTS):
                for t, w, width in ((m.W1E, m.eW1, 2 * HID), (m.W2E, m.eW2, 4 * D)):
                    c = width // w.shape[2]
                    sp.dma_start(t[:, e * width:(e + 1) * width].rearrange("p (c n) -> p c n", c=c),
                                 w[e].rearrange("(c p) n -> p c n", p=P)).then_inc(w_in, 16)
                    n += 16
            sp.dma_start(m.B1E[:, :], row_to_all(m.eb1.rearrange("e n -> (e n)"))).then_inc(w_in, 16)
            sp.dma_start(m.B2E[:, :], row_to_all(m.eb2.rearrange("e n -> (e n)"))).then_inc(w_in, 16)
            sp.wait_ge(w_in, n + 32)

        @block.scalar
        def _(act):
            def tile(i, s, rows):
                if reused(i):
                    act.wait_ge(sent[s], 2 * dma_count_before(i, s))
                    held(act, ta)
                nc.scalar.copy(at[s][:, 0:1], cols(m.pos_i[:, 0, :], i, 1))
                nc.scalar.copy(at[s][:, 1:2], cols(m.pos_i[:, 1, :], i, 1))
                act.drain().then_inc(at_made, 1)

            over_tiles(act, tile)

        @block.gpsimd
        def _(pool):
            def tile(i, s, rows):
                pool.wait_ge(at_made, i + 1)
                pool.wait_ge(xm_in[s], dma_count(i, s))
                held(pool, tp)
                for k in range(2):
                    pool.indirect_dma_start(m.expert_in, bass.IndirectOffsetOnAxis(ap=at[s][0:rows, k:k + 1], axis=0),
                                            xm[s][0:rows, :], None).then_inc(sent[s], 16)

            over_tiles(pool, tile)
            for s in range(2):
                pool.wait_ge(sent[s], 2 * dma_count(TILES - 1 - s, s))


def stage_experts(nc, m):
    with Stage(nc, "experts") as st:
        two = lambda n, w: [st.sb(f"{n}{s}", [P, w]) for s in range(2)]
        xe, xt, hb, hg, ht, y = two("xe", D), two("xt", D), two("hb", HID), two("hg", HID), two("ht", HID), two("y", D)
        pt, ph, pg, po = ([st.ps(f"{n}{s}") for s in range(2)] for n in ("pt", "ph", "pg", "po"))
        x_in, turned, xt_made, h_ps, hb_made, hg_made, h_turned, ht_made, y_ps, y_made, stored = (
            st.sems("x_in"), *(st.sem(n) for n in ("turned", "xt_made", "h_ps", "hb_made", "hg_made", "h_turned",
                                                   "ht_made", "y_ps", "y_made")), st.sems("stored"))
        tv, ta, tt, ts = (st.sem(n) for n in ("turns_v", "turns_a", "turns_t", "turns_s"))
        block = st.block()
        first = lambda t: isinstance(t, int) and t == 0

        def expert(eng, t):
            return eng.value_load(m.exp_row[0:1, bass.ds(t, 1)], min_val=0, max_val=EXPERTS - 1)

        @block.sync
        def _(sp):
            def store(t, s):
                sp.wait_ge(y_made, t + 1)
                held(sp, ts)
                sp.dma_start(m.expert_out[bass.ds(t * P, P), :], y[s][:, :]).then_inc(stored[s], 16)

            def tile(t, s):
                if reused(t):
                    sp.wait_ge(turned, t - 1)
                    held(sp, ts)
                sp.dma_start(xe[s][:, :], m.expert_in[bass.ds(t * P, P), :]).then_inc(x_in[s], 16)
                if reused(t):
                    store(t - 2, s)

            in_twos(sp, EX_TILES, tile)
            store(EX_TILES - 2, 0)
            store(EX_TILES - 1, 1)
            for s in range(2):
                sp.wait_ge(stored[s], EX_TILES * 8)

        @block.tensor
        def _(pe):
            def second(t, s):
                pe.wait_ge(hg_made, t + 1)
                if reused(t):
                    pe.wait_ge(ht_made, t - 1)
                held(pe, tt)
                for c in range(4):
                    tr = nc.tensor.transpose(pg[s][:, c * P:c * P + P], hg[s][:, c * P:c * P + P], m.ident[:, :])
                tr.then_inc(h_turned, 1)

            def third(t, s):
                e = expert(pe, t)
                pe.wait_ge(ht_made, t + 1)
                if reused(t):
                    pe.wait_ge(y_made, t - 1)
                held(pe, tt)
                for c in range(4):
                    mm = nc.tensor.matmul(po[s][:, 0:D], ht[s][:, c * P:c * P + P], cols(m.W2E, e * (4 * D) + c * D, D),
                                          start=(c == 0), stop=(c == 3))
                mm.then_inc(y_ps, 1)

            def tile(t, s):
                pe.wait_ge(x_in[s], dma_count(t, s))
                if reused(t):
                    pe.wait_ge(xt_made, t - 1)
                held(pe, tt)
                for c in range(2):
                    tr = nc.tensor.transpose(pt[s][:, c * P:c * P + P], xe[s][:, c * P:c * P + P], m.ident[:, :])
                tr.then_inc(turned, 1)
                if not first(t):
                    second(t - 1, 1 - s)
                e = expert(pe, t)
                pe.wait_ge(xt_made, t + 1)
                if reused(t):
                    pe.wait_ge(hb_made, t - 1)
                held(pe, tt)
                for c in range(2):
                    mm = nc.tensor.matmul(ph[s][:, :], xt[s][:, c * P:c * P + P], cols(m.W1E, e * (2 * HID) + c * HID, HID),
                                          start=(c == 0), stop=(c == 1))
                mm.then_inc(h_ps, 1)
                if not first(t):
                    third(t - 1, 1 - s)

            in_twos(pe, EX_TILES, tile)
            second(EX_TILES - 1, 1)
            third(EX_TILES - 1, 1)

        @block.scalar
        def _(act):
            def turned_h(t, s):
                act.wait_ge(h_turned, t + 1)
                if reused(t):
                    act.wait_ge(y_ps, t - 1)
                held(act, ta)
                nc.scalar.copy(ht[s][:, :], pg[s][:, :]).then_inc(ht_made, 1)

            def tile(t, s):
                act.wait_ge(turned, t + 1)
                if reused(t):
                    act.wait_ge(h_ps, t - 1)
                held(act, ta)
                nc.scalar.copy(xt[s][:, :], pt[s][:, 0:D]).then_inc(xt_made, 1)
                if not first(t):
                    turned_h(t - 1, 1 - s)
                act.wait_ge(hb_made, t + 1)
                if reused(t):
                    act.wait_ge(h_turned, t - 1)
                held(act, ta)
                nc.scalar.activation(hg[s][:, :], hb[s][:, :], ACT.Gelu).then_inc(hg_made, 1)

            in_twos(act, EX_TILES, tile)
            turned_h(EX_TILES - 1, 1)

        @block.vector
        def _(v):
            def out(t, s):
                e = expert(v, t)
                v.wait_ge(y_ps, t + 1)
                if reused(t):
                    v.wait_ge(stored[s], dma_count_before(t, s))
                held(v, tv)
                nc.vector.tensor_tensor(y[s][:, :], po[s][:, 0:D], cols(m.B2E, e * D, D), ALU.add).then_inc(y_made, 1)

            def tile(t, s):
                e = expert(v, t)
                v.wait_ge(h_ps, t + 1)
                if reused(t):
                    v.wait_ge(hg_made, t - 1)
                held(v, tv)
                nc.vector.tensor_tensor(hb[s][:, :], ph[s][:, :], cols(m.B1E, e * HID, HID), ALU.add).then_inc(hb_made, 1)
                if not first(t):
                    out(t - 1, 1 - s)

            in_twos(v, EX_TILES, tile)
            out(EX_TILES - 1, 1)


def stage_combine(nc, m):
    with Stage(nc, "combine") as st:
        y1, y2, o = ([st.sb(f"{n}{s}", [P, D]) for s in range(2)] for n in ("y1", "y2", "o"))
        at = [st.sb(f"at{s}", [P, 2], I32) for s in range(2)]
        at_made, got, out_made, stored = st.sem("at_made"), st.sems("got"), st.sem("out_made"), st.sems("stored")
        tv, ta, tp, ts = (st.sem(n) for n in ("turns_v", "turns_a", "turns_p", "turns_s"))
        block = st.block()

        @block.scalar
        def _(act):
            def tile(i, s, rows):
                if reused(i):
                    act.wait_ge(out_made, i - 1)
                    held(act, ta)
                nc.scalar.copy(at[s][:, 0:1], cols(m.pos_i[:, 0, :], i, 1))
                nc.scalar.copy(at[s][:, 1:2], cols(m.pos_i[:, 1, :], i, 1))
                act.drain().then_inc(at_made, 1)

            over_tiles(act, tile)

        @block.gpsimd
        def _(pool):
            def tile(i, s, rows):
                pool.wait_ge(at_made, i + 1)
                if reused(i):
                    pool.wait_ge(out_made, i - 1)
                held(pool, tp)
                for k, y in enumerate((y1, y2)):
                    pool.indirect_dma_start(y[s][0:rows, :], None, m.expert_out,
                                            bass.IndirectOffsetOnAxis(ap=at[s][0:rows, k:k + 1], axis=0)).then_inc(got[s], 16)

            over_tiles(pool, tile)

        @block.vector
        def _(v):
            def tile(i, s, rows):
                v.wait_ge(got[s], 2 * dma_count(i, s))
                if reused(i):
                    v.wait_ge(stored[s], dma_count_before(i, s))
                held(v, tv)
                x = m.X[0:rows, bass.ds(i * D, D)]
                nc.vector.scalar_tensor_tensor(out=y1[s][0:rows, :], in0=y1[s][0:rows, :], scalar=m.gate[0:rows, 0, bass.ds(i, 1)],
                                               in1=x, op0=ALU.mult, op1=ALU.add)
                v.drain()
                nc.vector.scalar_tensor_tensor(out=o[s][0:rows, :], in0=y2[s][0:rows, :], scalar=m.gate[0:rows, 1, bass.ds(i, 1)],
                                               in1=y1[s][0:rows, :], op0=ALU.mult, op1=ALU.add).then_inc(out_made, 1)

            over_tiles(v, tile)

        @block.sync
        def _(sp):
            def tile(i, s, rows):
                sp.wait_ge(out_made, i + 1)
                held(sp, ts)
                sp.dma_start(m.out[bass.ds(i * P, rows), :], o[s][0:rows, :]).then_inc(stored[s], 16)

            over_tiles(sp, tile)
            for s in range(2):
                sp.wait_ge(stored[s], dma_count(TILES - 1 - s, s))


class Memory:
    pass


def stages(nc, m):
    with ExitStack() as graph:
        def sb(name, shape, dt=F32):
            return graph.enter_context(nc.sbuf_tensor(name, shape, dt))

        m.src_i, m.dst_i, m.packed = (
            sb(n, [LANES, COLS], I32) for n in ("src_i", "dst_i", "packed"))
        m.pad_dst = sb("pad_dst", [1, EDGE_ROOM - E], I32)
        m.pad_src = sb("pad_src", [1, EDGE_ROOM - E], I32)
        m.GI = sb("GI", [P, SC * P], I32)
        m.LOC = sb("LOC", [P, SC * P])
        m.bin_row = sb("bin_row", [1, SC * P], I32)
        m.ACC = sb("ACC", [P, TILES * AW])
        m.EL = sb("EL", [P, TILES * 4])
        m.kvbd = sb("kvbd", [P, 2, P + 4])
        m.wqs, m.woT, m.fT, m.w11s, m.w12s, m.w21s, m.w22s, m.wouts, m.mixM = (
            sb(n, [P, 2, D]) for n in ("wqs", "woT", "fT", "w11s", "w12s", "w21s", "w22s", "wouts", "mixM"))
        m.wkvT = sb("wkvT", [P, 2, 2 * D])
        m.wqkvs = sb("wqkvs", [P, 2, 3 * D])
        m.gWs = sb("gWs", [P, 2, 64])
        m.gcat = sb("gcat", [P, 2, 72])
        m.b11s, m.b21s = (
            sb(n, [P, 2]) for n in ("b11s", "b21s"))
        m.b12r, m.b22r, m.bor, m.fbr, m.boutr, m.mw2r = (
            sb(n, [P, D]) for n in ("b12r", "b22r", "bor", "fbr", "boutr", "mw2r"))
        m.gbr = sb("gbr", [P, 64])
        m.kgp = sb("kgp", [P, 1])
        m.kbp = sb("kbp", [P, 1])
        m.vgr = sb("vgr", [P, P])
        m.vbr = sb("vbr", [P, P])

        stage_load(nc, m)
        stage_stats(nc, m, "stats0", 1e-5)
        stage_norm_kv(nc, m)
        stage_rank(nc, m, m.dst_i, 0)
        stage_conv(nc, m, "conv1", m.relu_xn_table)
        stage_mlp(nc, m, "mlp1", m.w11s, m.b11s, m.w12s, m.b12r, False)
        stage_conv(nc, m, "conv2", m.conv1_table)
        stage_mlp(nc, m, "mlp2", m.w21s, m.b21s, m.w22s, m.b22r, True)
        stage_stats(nc, m, "stats1", 1e-5)
        stage_ffn(nc, m)
        stage_stats(nc, m, "stats2", 1e-5, with_rms=True)
        stage_attn_kv(nc, m)
        stage_attn_q(nc, m)
        stage_attn_add(nc, m)
        stage_rank(nc, m, m.src_i, 1)
        stage_gat(nc, m)
        stage_stats(nc, m, "stats3", 1e-5)
    with ExitStack() as experts:
        def sb(name, shape, dt=F32):
            return experts.enter_context(nc.sbuf_tensor(name, shape, dt))

        m.L = sb("L", [P, TILES * EXPERTS])
        m.pos_i = sb("pos_i", [P, 2, TILES], I32)
        m.gate = sb("gate", [P, 2, TILES])
        m.exp_row = sb("exp_row", [1, P], I32)
        m.W1E = sb("W1E", [P, EXPERTS * 2 * HID])
        m.W2E = sb("W2E", [P, EXPERTS * 4 * D])
        m.B1E = sb("B1E", [P, EXPERTS * HID])
        m.B2E = sb("B2E", [P, EXPERTS * D])
        stage_router(nc, m)
        stage_route(nc, m)
        stage_dispatch(nc, m)
        stage_experts(nc, m)
        stage_combine(nc, m)



def gps_program(nc, args, out):
    with ExitStack() as ctx:
        m = Memory()
        (m.x, m.src, m.dst, m.w11, m.b11, m.w12, m.b12, m.w21, m.b21, m.w22, m.b22, m.wq, m.wk, m.wv, m.wo, m.bo,
         m.kg, m.kb, m.vg, m.vb, m.fw, m.fb, m.gW, m.gWl, m.gWr, m.gb, m.mw1, m.wqkv, m.wout, m.bout, m.mw2, m.gamma,
         m.beta, m.rW, m.rb, m.eW1, m.eb1, m.eW2, m.eb2, m.out) = (*args, out)

        def sb(name, shape, dt=F32):
            return ctx.enter_context(nc.sbuf_tensor(name, shape, dt))

        def dram(name, shape, dt=F32):
            return nc.dram_tensor(name, shape, dt).ap()

        m.relu_xn_table = dram("relu_xn_table", [NPAD, D])
        m.conv1_table = dram("conv1_table", [NPAD, D])
        m.attn_table = dram("attn_table", [NPAD, GW])
        m.xnT = dram("xnT", [NPAD, D])
        m.xrT = dram("xrT", [NPAD, D])
        m.xm = dram("xm", [NPAD, D])
        m.expert_in = dram("expert_in", [EX_TILES * P, D])
        m.expert_out = dram("expert_out", [EX_TILES * P, D])
        m.edges = [nc.dram_tensor(f"edges_by_{e}", [EDGE_ROOM], I32).ap() for e in ("dst", "src")]
        m.bin_dram = [nc.dram_tensor(f"bins_by_{e}", [SC * P], I32).ap() for e in ("dst", "src")]

        m.X = sb("X", [P, TILES * D])
        m.ident = sb("ident", [P, P])
        m.iota_row = sb("iota_row", [P, P])
        m.slot_no = sb("slot_no", [P, SC])
        m.tri = sb("tri", [P, P])
        m.ones = sb("ones", [P, P])
        m.zeros = sb("zeros", [P, 2 * AW])
        m.mask64 = sb("mask64", [P, P])
        m.mask32 = sb("mask32", [P, P])
        m.tri_bf, m.rest_bf, m.ones_bf = (
            sb(n, [P, P], BF16) for n in ("tri_bf", "rest_bf", "ones_bf"))
        m.zeros_bf = sb("zeros_bf", [P, 512], BF16)
        m.gammar, m.betar = (
            sb(n, [P, D]) for n in ("gammar", "betar"))
        m.rbr = sb("rbr", [P, EXPERTS])
        m.rWs = sb("rWs", [P, 2, EXPERTS])
        m.mean, m.rstd, m.rms_in, m.rms_out = (
            sb(n, [P, TILES]) for n in ("mean", "rstd", "rms_in", "rms_out"))

        stages(nc, m)


_INS = ['x', 'src', 'dst', 'L0_gnn_w11', 'L0_gnn_b11', 'L0_gnn_w12', 'L0_gnn_b12', 'L0_gnn_w21', 'L0_gnn_b21',
        'L0_gnn_w22', 'L0_gnn_b22', 'L0_mix_wq', 'L0_mix_wk', 'L0_mix_wv', 'L0_mix_wo', 'L0_mix_bo', 'L0_mix_ln_k_g',
        'L0_mix_ln_k_b', 'L0_mix_ln_v_g', 'L0_mix_ln_v_b', 'L0_ffn_weight', 'L0_ffn_bias', 'L1_gnn_W', 'L1_gnn_Wl',
        'L1_gnn_Wr', 'L1_gnn_b', 'L1_mix_w_norm1', 'L1_mix_w_qkv', 'L1_mix_w_out', 'L1_mix_b_out', 'L1_mix_w_norm2',
        'L1_ffn_gamma', 'L1_ffn_beta', 'L1_ffn_Wr', 'L1_ffn_br', 'L1_ffn_W1', 'L1_ffn_b1', 'L1_ffn_W2', 'L1_ffn_b2']


def kernel(**inputs):
    import numpy as _np
    import concourse.bacc as _bacc
    from concourse import mybir as _mybir
    from concourse.bass_utils import run_bass_kernel_spmd as _run

    nc = _bacc.Bacc("TRN2", target_bir_lowering=False, num_devices=1)
    arrays, args = {}, []
    for name in _INS:
        a = _np.ascontiguousarray(inputs[name])
        arrays[f"in_{name}_dram"] = a
        args.append(nc.dram_tensor(f"in_{name}_dram", a.shape, _mybir.dt.from_np(a.dtype), kind="ExternalInput").ap())
    out = nc.dram_tensor("out_0_dram", (N, D), F32, kind="ExternalOutput").ap()
    gps_program(nc, args, out)
    r = _run(nc, [arrays], core_ids=[0])
    return r.results[0]["out_0_dram"]
```

```python
from contextlib import ExitStack

import concourse.bass as bass
from concourse import mybir

P = 128
N, D = 6250, 256
E = 100000
EDGE_ROOM = (E + 2 * P - 1) // P * P
TILES = (N + P - 1) // P
TAIL = N - (TILES - 1) * P
NPAD = TILES * P
LANES = 125
COLS = E // LANES
CH = 10
CT = CH * TILES
BITS = 13
NOWHERE = (1 << BITS) - 1
SLOT_TILES = ((E + TILES * (P - 1)) // P + 7) // 8 * 8
SC = (SLOT_TILES + P - 1) // P
AW = 260
GW = 68
EXPERTS, HID = 8, 512
EX_TILES = ((2 * N + EXPERTS * (P - 1)) // P + 1) // 2 * 2
RING = 8

F32 = mybir.dt.float32
I32 = mybir.dt.int32
BF16 = mybir.dt.bfloat16
ALU = mybir.AluOpType
ACT = mybir.ActivationFunctionType
PE, DVE = mybir.EngineType.PE, mybir.EngineType.DVE
X_AXIS = mybir.AxisListType.X


class Stage:

    def __init__(self, nc, name):
        self.nc, self.name, self.ctx, self.taken = nc, name, ExitStack(), []

    def __enter__(self):
        return self

    def __exit__(self, *a):
        self.ctx.__exit__(*a)
        self.nc.clear_and_free_semaphores(self.taken)
        self.nc.all_engine_barrier()

    def sb(self, name, shape, dt=F32):
        return self.ctx.enter_context(self.nc.sbuf_tensor(f"{self.name}_{name}", shape, dt))

    def ps(self, name, shape=(P, 512), dt=F32):
        return self.ctx.enter_context(self.nc.psum_tensor(f"{self.name}_{name}", list(shape), dt))

    def sem(self, name):
        self.taken.append(self.nc.alloc_semaphore(f"{self.name}_{name}"))
        return self.taken[-1]

    def sems(self, name, n=2):
        return [self.sem(f"{name}{k}") for k in range(n)]

    def block(self):
        return self.ctx.enter_context(self.nc.Block())


def in_twos(eng, count, body):
    body(0, 0)
    body(1, 1)
    with eng.Fori(1, count // 2) as q:
        body(q * 2, 0)
        body(q * 2 + 1, 1)


def over_tiles(eng, body):
    in_twos(eng, TILES - 1, lambda i, s: body(i, s, P))
    body(TILES - 1, 0, TAIL)


def skewed(eng, behind, step):
    first = 2 + behind + behind % 2
    for i in range(-1, first):
        step(i, i % 2)
    with eng.Fori(first // 2, (TILES - 1) // 2) as q:
        step(q * 2, 0)
        step(q * 2 + 1, 1)
    for i in range(TILES - 1, TILES + behind):
        step(i, i % 2)


def there(i):
    return not isinstance(i, int) or 0 <= i < TILES


def reused(i):
    return not (isinstance(i, int) and i < 2)


def dma_count(i, s):
    return i * 8 + (16 - 8 * s)


def dma_count_before(i, s):
    return i * 8 - 8 * s


def held(eng, turns):
    eng.sem_inc(turns, 1)


def cols(t, start, width):
    return t[:, bass.ds(start, width)]


def bins_of_round(nc, m, engine, r):
    return nc.values_load_multi_w_load_instructions(m.bin_row[0:1, bass.ds(r * RING, RING)], engines=(engine,),
                                                    min_val=0, max_val=TILES - 1,
                                                    skip_runtime_bounds_check_because="bins are clamped on the chip")[1]


def row_to_all(ap, parts=P):
    return ap.partition_broadcast(parts)


def stage_load(nc, m):
    with Stage(nc, "load") as st:
        nat = [st.sb(f"nat{k}", [P, 2, D]) for k in range(4)]
        gWs = st.sb("gWs", [P, 2, 64])
        gWlr = st.sb("gWlr", [8, 64])
        gWT = st.sb("gWT", [64, D])
        gWlrT = st.sb("gWlrT", [64, 8])
        mw1p = st.sb("mw1p", [P, 2])
        pad_dst, pad_src = (st.sb(n, [1, EDGE_ROOM - E], I32) for n in ("pad_dst", "pad_src"))
        ps = [st.ps(f"ps{k}") for k in range(4)]
        loaded, x_in, x_clear, consts, steps = (st.sem(s) for s in ("loaded", "x_in", "x_clear", "consts", "steps"))
        turned, copied = st.sem("turned"), st.sem("copied")
        pads, pads_out, next_set = st.sem("pads"), st.sem("pads_out"), st.sem("next_set")
        block = st.block()
        chunks = lambda w: w.rearrange("(c p) n -> p c n", p=P)
        count = [0]

        @block.sync
        def _(sp):
            def load(to, frm, **kw):
                sp.dma_start(to, frm, **kw).then_inc(loaded, 16)
                count[0] += 16

            load(m.src_i[:, :], m.src.rearrange("(p c) -> p c", p=LANES))
            load(m.dst_i[:, :], m.dst.rearrange("(p c) -> p c", p=LANES))
            sp.wait_ge(next_set, 1)
            load(m.next_i[0:LANES - 1, :], m.dst[COLS:E].rearrange("(p c) -> p c", c=COLS)[:, 0:1], allow_slow_non_contiguous=True)
            for k, w in enumerate((m.wk, m.wv, m.wo, m.fw)):
                load(nat[k][:, :, :], chunks(w))
            load(gWlr[0:4, :], m.gWr)
            load(gWlr[4:8, :], m.gWl)
            load(gWs[:, :, :], chunks(m.gW))
            load(mw1p[:, :], m.mw1.rearrange("(c p) -> p c", p=P), allow_slow_non_contiguous=True)
            load(m.wqkvs[:, :, :], chunks(m.wqkv))
            for to, frm in ((m.wqs, m.wq), (m.w11s, m.w11), (m.w12s, m.w12), (m.w21s, m.w21), (m.w22s, m.w22),
                            (m.wouts, m.wout), (m.rWs, m.rW)):
                load(to[:, :, :], chunks(frm))
            for to, frm in ((m.b11s, m.b11), (m.b21s, m.b21)):
                load(to[:, :], frm.rearrange("(c p) -> p c", p=P), allow_slow_non_contiguous=True)
            for to, frm in ((m.b12r, m.b12), (m.b22r, m.b22), (m.bor, m.bo), (m.fbr, m.fb), (m.boutr, m.bout),
                            (m.mw2r, m.mw2), (m.gammar, m.gamma), (m.betar, m.beta), (m.gbr, m.gb), (m.rbr, m.rb)):
                load(to[:, :], row_to_all(frm))
            for half in range(2):
                lo = 64 * half
                load(m.kgp[lo:lo + 64, :], m.kg.rearrange("(p a) -> p a", a=1))
                load(m.kbp[lo:lo + 64, :], m.kb.rearrange("(p a) -> p a", a=1))
                load(m.vgr[:, lo:lo + 64], row_to_all(m.vg))
                load(m.vbr[:, lo:lo + 64], row_to_all(m.vb))
            whole = (TILES - 1) * P
            for g in range(4):
                sp.dma_start(m.X[:, g * 12 * D:(g + 1) * 12 * D].rearrange("p (i d) -> p i d", d=D),
                             m.x[g * 12 * P:(g + 1) * 12 * P, :].rearrange("(i p) d -> p i d", p=P)).then_inc(x_in, 16)
            sp.wait_ge(x_clear, 1)
            sp.dma_start(m.X[0:TAIL, (TILES - 1) * D:TILES * D], m.x[whole:N, :]).then_inc(x_in, 16)
            sp.wait_ge(x_in, 80)
            sp.wait_ge(pads, 1)
            sp.dma_start(m.edges[0][E:EDGE_ROOM].rearrange("(a b) -> a b", a=1), pad_dst[:, :]).then_inc(pads_out, 16)
            sp.dma_start(m.edges[1][E:EDGE_ROOM].rearrange("(a b) -> a b", a=1), pad_src[:, :]).then_inc(pads_out, 16)
            sp.wait_ge(pads_out, 32)
            sp.wait_ge(loaded, count[0])

        @block.gpsimd
        def _(pool):
            nc.gpsimd.memset(m.next_i[:, :], NOWHERE).then_inc(next_set, 1)
            nc.gpsimd.memset(m.X[:, (TILES - 1) * D:TILES * D], 0.0).then_inc(x_clear, 1)
            for t, v in ((m.ident, 0.0), (m.tri, 1.0), (m.ones, 1.0), (m.zeros, 0.0), (m.mask64, 1.0), (m.mask32, 1.0)):
                nc.gpsimd.memset(t[:, :], v)
            nc.gpsimd.memset(pad_dst[:, :], NOWHERE)
            nc.gpsimd.memset(pad_src[:, :], NOWHERE << BITS)
            pool.drain().then_inc(pads, 1)
            nc.gpsimd.affine_select(out=m.ident[:, :], in_=m.ident[:, :], compare_op=ALU.not_equal, fill=1.0, base=0,
                                    pattern=[[-1, P]], channel_multiplier=1)
            nc.gpsimd.affine_select(out=m.tri[:, :], in_=m.tri[:, :], compare_op=ALU.is_ge, fill=0.0, base=-1,
                                    pattern=[[1, P]], channel_multiplier=-1)
            for t, w in ((m.mask64, 64), (m.mask32, 32)):
                v = t[:, :].rearrange("p (g j) -> p g j", j=w)
                nc.gpsimd.affine_select(out=v, in_=v, compare_op=ALU.is_ge, fill=0.0, base=0,
                                        pattern=[[-w, P // w], [0, w]], channel_multiplier=1)
                pool.drain()
                nc.gpsimd.affine_select(out=v, in_=v, compare_op=ALU.is_ge, fill=0.0, base=w - 1,
                                        pattern=[[w, P // w], [0, w]], channel_multiplier=-1)
            nc.gpsimd.iota(m.iota_row[:, :], [[1, P]], base=0, channel_multiplier=0, allow_small_or_imprecise_dtypes=True)
            nc.gpsimd.iota(m.slot_no[:, :], [[P, SC]], base=0, channel_multiplier=1, allow_small_or_imprecise_dtypes=True)
            pool.drain().then_inc(consts, 1)

        @block.tensor
        def _(pe):
            pe.wait_ge(consts, 1)
            pe.wait_ge(loaded, count[0])
            for k in range(4):
                for oc in range(2):
                    for kc in range(2):
                        nc.tensor.transpose(ps[k][:, kc * D + oc * P:kc * D + oc * P + P], nat[k][:, oc, kc * P:kc * P + P],
                                            m.ident[:, :])
            pe.drain().then_inc(turned, 1)
            pe.wait_ge(copied, 1)
            for kc in range(2):
                nc.tensor.transpose(ps[0][0:64, kc * P:kc * P + P], gWs[:, kc, :], m.ident[:, :])
            nc.tensor.transpose(ps[1][0:64, 0:8], gWlr[:, :], m.ident[0:8, 0:8])
            pe.drain().then_inc(turned, 1)
            pe.wait_ge(copied, 2)
            for kc in range(2):
                nc.tensor.matmul(ps[2][:, 8 * kc:8 * kc + 8], gWT[:, kc * P:kc * P + P], gWlrT[:, :], start=True, stop=True)
            pe.drain().then_inc(turned, 1)

        @block.scalar
        def _(act):
            act.wait_ge(consts, 1)
            nc.scalar.copy(m.tri_bf[:, :], m.tri[:, :])
            nc.scalar.copy(m.ident_bf[:, :], m.ident[:, :])
            nc.scalar.copy(m.iota_bf[:, :], m.iota_row[:, :])
            nc.scalar.copy(m.ones_bf[:, :], m.ones[:, :])
            nc.scalar.copy(m.zeros_bf[:, :], m.zeros[:, 0:512])
            nc.scalar.activation(m.rest_bf[:, :], m.tri[:, :], ACT.Copy, bias=1.0, scale=-1.0)
            act.wait_ge(turned, 1)
            for k, (t, at) in enumerate(((m.wkvT, 0), (m.wkvT, D), (m.woT, 0), (m.fT, 0))):
                nc.scalar.copy(t[:, :, at:at + D], ps[k][:, :].rearrange("p (c n) -> p c n", c=2))
            act.drain().then_inc(copied, 1)
            act.wait_ge(turned, 2)
            nc.scalar.copy(gWT[:, :], ps[0][0:64, 0:D])
            nc.scalar.copy(gWlrT[:, :], ps[1][0:64, 0:8])
            nc.scalar.copy(m.gcat[:, :, 0:64], gWs[:, :, :])
            act.drain().then_inc(copied, 1)
            act.wait_ge(turned, 3)
            nc.scalar.copy(m.gcat[:, :, 64:72], ps[2][:, 0:16].rearrange("p (c n) -> p c n", c=2))

        @block.vector
        def _(v):
            v.wait_ge(loaded, count[0])
            for kc in range(2):
                nc.vector.tensor_scalar(m.wqkvs[:, kc, :], m.wqkvs[:, kc, :], mw1p[:, kc:kc + 1], None, ALU.mult)
            nc.vector.tensor_scalar(m.packed[:, :], m.src_i[:, :], BITS, None, ALU.logical_shift_left)
            v.drain()
            nc.vector.tensor_tensor(m.packed[:, :], m.packed[:, :], m.dst_i[:, :], ALU.bitwise_or)


def stage_stats(nc, m, name, eps, with_rms=False):
    with Stage(nc, name) as st:
        parts = st.sb("parts", [P, TILES, 6])
        a, b = st.sb("a", [P, TILES]), st.sb("b", [P, TILES])
        var_done, root_done = st.sem("var_done"), st.sem("root_done")
        block = st.block()

        @block.vector
        def _(v):
            flat = parts[:, :, :].rearrange("p i s -> p (i s)")
            with v.Fori(0, TILES // 7) as q:
                for k in range(7):
                    nc.vector.bn_stats(flat[:, bass.ds(q * 42 + k * 6, 6)], cols(m.X, q * (7 * D) + k * D, D))
            v.drain()
            f = lambda k: parts[:, :, k]
            nc.vector.tensor_tensor(a[:, :], f(1), f(4), ALU.add)
            nc.vector.tensor_tensor(b[:, :], f(1), f(4), ALU.subtract)
            nc.vector.tensor_tensor(m.rms_out[:, :], f(2), f(5), ALU.add)
            v.drain()
            nc.vector.tensor_scalar(m.mean[:, :], a[:, :], 0.5, None, ALU.mult)
            nc.vector.scalar_tensor_tensor(out=b[:, :], in0=b[:, :], scalar=0.25, in1=b[:, :], op0=ALU.mult, op1=ALU.mult)
            v.drain()
            nc.vector.scalar_tensor_tensor(out=b[:, :], in0=m.rms_out[:, :], scalar=1.0 / D, in1=b[:, :],
                                           op0=ALU.mult, op1=ALU.add)
            v.drain()
            nc.vector.tensor_scalar(a[:, :], b[:, :], eps, None, ALU.add)
            v.drain().then_inc(var_done, 1)
            v.wait_ge(root_done, 1)
            nc.vector.reciprocal(m.rstd[:, :], m.rms_out[:, :])
            if with_rms:
                v.drain()
                nc.vector.tensor_tensor(a[:, :], m.rstd[:, :], m.rstd[:, :], ALU.mult)
                v.drain()
                nc.vector.tensor_tensor(a[:, :], a[:, :], b[:, :], ALU.mult)
                v.drain()
                nc.vector.tensor_scalar(a[:, :], a[:, :], 1e-6, None, ALU.add)
                v.drain().then_inc(var_done, 1)
                v.wait_ge(root_done, 2)
                nc.vector.reciprocal(b[:, :], m.rms_out[:, :])
                v.drain()
                nc.vector.tensor_tensor(m.rms_in[:, :], b[:, :], m.rstd[:, :], ALU.mult)

        @block.scalar
        def _(act):
            act.wait_ge(var_done, 1)
            nc.scalar.activation(m.rms_out[:, :], a[:, :], ACT.Sqrt).then_inc(root_done, 1)
            if with_rms:
                act.wait_ge(var_done, 2)
                nc.scalar.activation(m.rms_out[:, :], a[:, :], ACT.Sqrt).then_inc(root_done, 1)


def stage_norm(nc, m):
    with Stage(nc, "norm") as st:
        xn = [st.sb(f"xn{s}", [P, D]) for s in range(2)]
        rx = [st.sb(f"rx{s}", [P, D]) for s in range(2)]
        xt = [st.sb(f"xt{s}", [P, D]) for s in range(2)]
        pt = [st.ps(f"pt{s}") for s in range(2)]
        xn_made, xn_turned, xt_made, rx_made = (st.sem(n) for n in ("xn_made", "xn_turned", "xt_made", "rx_made"))
        out_rx, out_xt = st.sems("out_rx"), st.sems("out_xt")
        tv, ta, tt, ts = (st.sem(n) for n in ("turns_v", "turns_a", "turns_t", "turns_s"))
        block = st.block()

        @block.vector
        def _(v):
            def norm(i, s, rows):
                if reused(i):
                    v.wait_ge(xn_turned, i - 1)
                    v.wait_ge(rx_made, i - 1)
                    held(v, tv)
                nc.vector.tensor_scalar(xn[s][:, :], cols(m.X, i * D, D), cols(m.mean, i, 1), cols(m.rstd, i, 1),
                                        ALU.subtract, ALU.mult).then_inc(xn_made, 1)
                nc.vector.tensor_scalar(cols(m.ACC, i * AW, D), cols(m.X, i * D, D), cols(m.mean, i, 1), cols(m.rstd, i, 1),
                                        ALU.subtract, ALU.mult)

            over_tiles(v, norm)

        @block.tensor
        def _(pe):
            def turn(i, s, rows):
                pe.wait_ge(xn_made, i + 1)
                if reused(i):
                    pe.wait_ge(xt_made, i - 1)
                held(pe, tt)
                for c in range(2):
                    tr = nc.tensor.transpose(pt[s][:, c * P:c * P + P], xn[s][:, c * P:c * P + P], m.ident[:, :])
                tr.then_inc(xn_turned, 1)

            over_tiles(pe, turn)

        @block.scalar
        def _(act):
            def tile(i, s, rows):
                act.wait_ge(xn_made, i + 1)
                if reused(i):
                    act.wait_ge(out_rx[s], dma_count_before(i, s))
                held(act, ta)
                nc.scalar.activation(rx[s][:, :], xn[s][:, :], ACT.Relu).then_inc(rx_made, 1)
                act.wait_ge(xn_turned, i + 1)
                if reused(i):
                    act.wait_ge(out_xt[s], dma_count_before(i, s))
                held(act, ta)
                nc.scalar.copy(xt[s][:, :], pt[s][:, 0:D]).then_inc(xt_made, 1)

            over_tiles(act, tile)

        @block.sync
        def _(sp):
            def tile(i, s, rows):
                sp.wait_ge(rx_made, i + 1)
                held(sp, ts)
                sp.dma_start(m.relu_xn_table[bass.ds(i * P, P), :], rx[s][:, :]).then_inc(out_rx[s], 16)
                sp.wait_ge(xt_made, i + 1)
                held(sp, ts)
                sp.dma_start(m.xnT[bass.ds(i * P, P), :], xt[s][:, :]).then_inc(out_xt[s], 16)

            over_tiles(sp, tile)
            for s in range(2):
                sp.wait_ge(out_rx[s], dma_count(TILES - 1 - s, s))
                sp.wait_ge(out_xt[s], dma_count(TILES - 1 - s, s))


class KeyValueSums:

    W2 = P + 1

    def __init__(self, nc, m, st):
        self.nc, self.m = nc, m
        self.xt, self.cen, self.vn = st.sb("xt", [P, D]), st.sb("cen", [P, 2 * D]), st.sb("vn", [P, 2, P + 1])
        self.sq = st.sb("sq", [P, 2 * D])
        self.s1, self.s2, self.mu, self.va, self.rt = (st.sb(n, [P, 8]) for n in ("s1", "s2", "mu", "va", "rt"))
        self.pkv, self.psum_kv, self.psum_v = st.ps("pkv"), st.ps("kv"), st.ps("v")
        (self.xt_in, self.projected, self.squared, self.root_in, self.rooted, self.kn_made, self.kn_used, self.sums_done) = (
            st.sem(n) for n in ("xt_in", "projected", "squared", "root_in", "rooted", "kn_made", "kn_used", "sums_done"))

    def groups(self, t):
        return t.rearrange("p (g j) -> p g j", j=64)

    def sp_load(self, sp, turns, i):
        if not (isinstance(i, int) and i == 0):
            sp.wait_ge(self.projected, i)
            held(sp, turns)
        sp.dma_start(self.xt[:, :], self.m.xnT[bass.ds(i * P, P), :]).then_inc(self.xt_in, 16)

    def pe_begin(self):
        for bank in (self.psum_kv, self.psum_v):
            self.nc.tensor.matmul(bank[:, 0:2 * self.W2], self.m.ones[:, :], self.m.zeros[:, 0:2 * self.W2], start=True,
                                  stop=False, skip_group_check=True)

    def pe_project(self, pe, turns, i):
        pe.wait_ge(self.xt_in, i * 16 + 16)
        if not (isinstance(i, int) and i == 0):
            pe.wait_ge(self.kn_made, i)
        held(pe, turns)
        for c in range(2):
            mm = self.nc.tensor.matmul(self.pkv[:, :], self.xt[:, c * P:c * P + P], self.m.wkvT[:, c, :], start=(c == 0),
                                       stop=(c == 1))
        mm.then_inc(self.projected, 1)

    def act_square(self, act, turns, i):
        act.wait_ge(self.projected, i + 1)
        held(act, turns)
        self.nc.scalar.activation(self.sq[:, :], self.pkv[:, :], ACT.Square).then_inc(self.squared, 1)

    def dve_center(self, v, turns, i):
        nc = self.nc
        v.wait_ge(self.squared, i + 1)
        held(v, turns)
        kv = self.groups(self.pkv[:, :])
        nc.vector.tensor_reduce(self.s1[:, :], kv, X_AXIS, ALU.add)
        nc.vector.tensor_reduce(self.s2[:, :], self.groups(self.sq[:, :]), X_AXIS, ALU.add)
        v.drain()
        nc.vector.tensor_scalar(self.mu[:, :], self.s1[:, :], 1.0 / 64, None, ALU.mult)
        v.drain()
        nc.vector.tensor_tensor(self.va[:, :], self.mu[:, :], self.mu[:, :], ALU.mult)
        nc.vector.tensor_tensor(self.groups(self.cen[:, :]), kv, self.mu[:, :].unsqueeze(2).broadcast_to([P, 8, 64]),
                                ALU.subtract)
        v.drain()
        nc.vector.scalar_tensor_tensor(out=self.s2[:, :], in0=self.s2[:, :], scalar=1.0 / 64, in1=self.va[:, :],
                                       op0=ALU.mult, op1=ALU.subtract)
        v.drain()
        nc.vector.tensor_scalar(self.va[:, :], self.s2[:, :], 0.0, 1e-5, ALU.max, ALU.add).then_inc(self.root_in, 1)

    def act_root(self, act, turns, i):
        act.wait_ge(self.root_in, i + 1)
        held(act, turns)
        self.nc.scalar.activation(self.rt[:, :], self.va[:, :], ACT.Sqrt).then_inc(self.rooted, 1)

    def dve_norm(self, v, turns, i):
        nc = self.nc
        v.wait_ge(self.rooted, i + 1)
        if not (isinstance(i, int) and i == 0):
            v.wait_ge(self.kn_used, i)
        held(v, turns)
        nc.vector.reciprocal(self.s1[:, :], self.rt[:, :])
        v.drain()
        r = self.s1[:, :].unsqueeze(2).broadcast_to([P, 8, 64])
        nc.vector.tensor_tensor(self.groups(self.sq[:, 0:D]), self.groups(self.cen[:, 0:D]), r[:, 0:4, :], ALU.mult)
        for c in range(2):
            last = nc.vector.tensor_tensor(self.groups(self.vn[:, c, 0:P]), self.groups(self.cen[:, D + c * P:D + c * P + P]),
                                           r[:, 4 + 2 * c:6 + 2 * c, :], ALU.mult)
        last.then_inc(self.kn_made, 1)

    def pe_sums(self, pe, turns, i):
        nc, W2 = self.nc, self.W2
        pe.wait_ge(self.kn_made, i + 1)
        held(pe, turns)
        for c in range(2):
            nc.tensor.matmul(self.psum_kv[:, c * W2:c * W2 + W2], self.sq[:, c * P:c * P + P], self.vn[:, c, :],
                             start=False, stop=False, skip_group_check=True)
        nc.tensor.matmul(self.psum_v[:, 0:2 * W2], self.m.ones[:, :], self.vn[:, :, :].rearrange("p c n -> p (c n)"),
                         start=False, stop=False, skip_group_check=True).then_inc(self.kn_used, 1)

    def pe_end(self):
        for bank in (self.psum_kv, self.psum_v):
            mm = self.nc.tensor.matmul(bank[:, 0:2 * self.W2], self.m.ones[:, :], self.m.zeros[:, 0:2 * self.W2], start=False,
                                       stop=True, skip_group_check=True)
        mm.then_inc(self.sums_done, 1)

    def dve_end(self, v):
        v.wait_ge(self.sums_done, 1)
        self.nc.vector.tensor_copy(self.m.kv_sum[:, :], self.psum_kv[:, 0:2 * self.W2])
        self.nc.vector.tensor_copy(self.m.v_sum[:, :], self.psum_v[:, 0:2 * self.W2])


def stage_mix(nc, m):
    with Stage(nc, "mix") as st:
        w = [st.sb(f"w{k}", [P, P]) for k in range(3)]
        bd = st.sb("bd", [P, 2, P])
        kgs, kbs = st.sb("kgs", [P, 1]), st.sb("kbs", [P, 1])
        u = st.sb("u", [P, 2, D])
        pu, pm = [st.ps(f"pu{k}") for k in range(2)], [st.ps(f"pm{k}") for k in range(2)]
        bd_made, u_done, u_kept, m_done = (st.sem(n) for n in ("bd_made", "u_done", "u_kept", "m_done"))
        block = st.block()
        kv_sum, v_sum = m.kv_sum, m.v_sum
        W2 = P + 1

        @block.vector
        def _(v):
            nc.vector.tensor_scalar(kgs[:, :], m.kgp[:, :], 1.0 / N, None, ALU.mult)
            nc.vector.tensor_scalar(kbs[:, :], m.kbp[:, :], 1.0 / N, None, ALU.mult)
            v.drain()
            for c in range(2):
                lo = c * W2
                nc.vector.tensor_tensor(w[0][:, :], kv_sum[:, lo:lo + P], m.vgr[:, :], ALU.mult)
                nc.vector.tensor_tensor(w[1][:, :], v_sum[:, lo:lo + P], m.vgr[:, :], ALU.mult)
                v.drain()
                nc.vector.scalar_tensor_tensor(out=w[0][:, :], in0=m.vbr[:, :], scalar=kv_sum[:, lo + P:lo + P + 1],
                                               in1=w[0][:, :], op0=ALU.mult, op1=ALU.add)
                nc.vector.scalar_tensor_tensor(out=w[1][:, :], in0=m.vbr[:, :], scalar=float(N),
                                               in1=w[1][:, :], op0=ALU.mult, op1=ALU.add)
                v.drain()
                nc.vector.tensor_scalar(w[0][:, :], w[0][:, :], kgs[:, :], None, ALU.mult)
                v.drain()
                nc.vector.scalar_tensor_tensor(out=w[2][:, :], in0=w[1][:, :], scalar=kbs[:, :], in1=w[0][:, :],
                                               op0=ALU.mult, op1=ALU.add)
                v.drain()
                nc.vector.tensor_tensor(bd[:, c, :], w[2][:, :], m.mask64[:, :], ALU.mult)
            v.drain().then_inc(bd_made, 1)

        @block.tensor
        def _(pe):
            pe.wait_ge(bd_made, 1)
            for c in range(2):
                mm = nc.tensor.matmul(pu[c][:, 0:D], bd[:, c, :], m.wqs[:, c, :], start=True, stop=True)
            mm.then_inc(u_done, 1)
            pe.wait_ge(u_kept, 1)
            for k in range(2):
                for c in range(2):
                    mm = nc.tensor.matmul(pm[k][:, 0:D], u[:, c, k * P:k * P + P], m.woT[:, c, :], start=(c == 0), stop=(c == 1))
            mm.then_inc(m_done, 1)

        @block.scalar
        def _(act):
            act.wait_ge(u_done, 1)
            for c in range(2):
                cp = nc.scalar.copy(u[:, c, :], pu[c][:, 0:D])
            cp.then_inc(u_kept, 1)
            act.wait_ge(m_done, 1)
            for k in range(2):
                nc.scalar.copy(m.mixM[:, k, :], pm[k][:, 0:D])


def stage_count(nc, m, key_in, which):
    with Stage(nc, f"rank{which}") as st:
        key_i = st.sb("key_i", [LANES, COLS], I32)
        oh = [st.sb(f"oh{s}", [LANES, CH, TILES], BF16) for s in range(2)]
        tot = st.sb("tot", [P, TILES])
        a, b, start, below = (st.sb(n, [P, TILES]) for n in ("a", "b", "start", "below"))
        ti = st.sb("ti", [P, TILES], I32)
        cmp = st.sb("cmp", [P, SC, TILES])
        off, bin_i = st.sb("off", [P, SC]), st.sb("bin_i", [P, SC], I32)
        down, wrong = st.sb("down", [LANES, COLS]), st.sb("wrong", [LANES, 4])
        hist, count = st.ps("hist"), st.ps("count")
        oh_made, oh_used, hist_done, wrong_made, wrong_sum = (
            st.sem(s) for s in ("oh_made", "oh_used", "hist_done", "wrong_made", "wrong_sum"))
        bin_out, bin_back, as_is = st.sem("bin_out"), st.sem("bin_back"), st.sem("as_is")
        t_v, t_t = st.sem("turns_v"), st.sem("turns_t")
        block = st.block()
        key, base, bin_f, off_i = m.key, m.base, m.bin_f, m.off_i

        def f2(t):
            return t[:, :, :].rearrange("p c b -> p (c b)")

        @block.vector
        def _(v):
            nc.vector.tensor_scalar(key_i[:, :], key_in[:, :], 7, None, ALU.logical_shift_right)
            v.drain()
            nc.vector.tensor_copy(key[:, :], key_i[:, :])
            v.drain()

            def count_chunk(c, s):
                if reused(c):
                    v.wait_ge(oh_used, c - 1)
                    held(v, t_v)
                one_hot_of_chunk(nc, m, oh[s], c).then_inc(oh_made, 1)

            in_twos(v, COLS // CH, count_chunk)
            if which == 0:
                nc.vector.tensor_scalar(m.next_i[:, :], m.next_i[:, :], 7, None, ALU.logical_shift_right)
                nc.vector.tensor_tensor(down[:, 0:COLS - 1], key[:, 0:COLS - 1], key[:, 1:COLS], ALU.is_gt)
                v.drain()
                nc.vector.tensor_copy(wrong[:, 0:1], m.next_i[:, :])
                nc.vector.tensor_reduce(wrong[:, 1:2], down[:, 0:COLS - 1], X_AXIS, ALU.add)
                v.drain()
                nc.vector.tensor_tensor(wrong[:, 2:3], key[:, COLS - 1:COLS], wrong[:, 0:1], ALU.is_gt)
                v.drain()
                nc.vector.tensor_tensor(wrong[:, 3:4], wrong[:, 1:2], wrong[:, 2:3], ALU.add)
                v.drain().then_inc(wrong_made, 1)
                v.wait_ge(wrong_sum, 1)
                nc.vector.tensor_scalar(off[0:1, 0:1], count[0:1, 0:1], 1.0, None, ALU.min)
                v.drain()
                nc.vector.tensor_copy(m.unsorted[:, :], off[0:1, 0:1])
                v.drain()
            v.wait_ge(hist_done, 1)
            nc.vector.tensor_copy(f2(base), hist[:, 0:CT])
            v.drain()
            nc.vector.tensor_reduce(tot[:, :], base[:, :, :].rearrange("p c b -> p b c"), X_AXIS, ALU.add)
            v.drain()

            def prefix(x, y):
                w = 1
                while w < TILES:
                    nc.vector.tensor_tensor(y[:, w:TILES], x[:, w:TILES], x[:, 0:TILES - w], ALU.add)
                    nc.vector.tensor_copy(y[:, 0:w], x[:, 0:w])
                    v.drain()
                    x, y, w = y, x, 2 * w
                return x, y

            nc.vector.tensor_copy(a[:, :], tot[:, :])
            v.drain()
            ends, spare = prefix(a, b)
            nc.vector.tensor_tensor(start[:, :], ends[:, :], tot[:, :], ALU.subtract)
            v.drain()
            nc.vector.tensor_copy(below[:, :], start[:, :])
            v.drain()
            for j in range(CH):
                nc.vector.tensor_copy(spare[:, :], base[:, j, :])
                v.drain()
                nc.vector.tensor_copy(base[:, j, :], below[:, :])
                v.drain()
                nc.vector.tensor_tensor(below[:, :], below[:, :], spare[:, :], ALU.add)
                v.drain()
            nc.vector.tensor_scalar(a[:, :], tot[:, :], float(P - 1), None, ALU.add)
            v.drain()
            nc.vector.tensor_copy(ti[:, :], a[:, :])
            v.drain()
            nc.vector.tensor_scalar(ti[:, :], ti[:, :], 7, None, ALU.logical_shift_right)
            v.drain()
            nc.vector.tensor_copy(a[:, :], ti[:, :])
            nc.vector.tensor_copy(tot[:, :], ti[:, :])
            v.drain()
            tile_ends, spare = prefix(a, b)
            nc.vector.tensor_tensor(tot[:, :], tile_ends[:, :], tot[:, :], ALU.subtract)
            v.drain()
            nc.vector.scalar_tensor_tensor(out=spare[:, :], in0=tot[:, :], scalar=-float(P), in1=start[:, :], op0=ALU.mult,
                                           op1=ALU.add)
            slots = m.slot_no[:, :].unsqueeze(2).broadcast_to([P, SC, TILES])
            over = lambda t: t.unsqueeze(1).broadcast_to([P, SC, TILES])
            nc.vector.tensor_tensor(cmp[:, :, :], over(tile_ends[:, :]), slots, ALU.is_le)
            v.drain()
            nc.vector.tensor_reduce(bin_f[:, :], cmp[:, :, :], X_AXIS, ALU.add)
            v.drain()
            nc.vector.tensor_tensor(cmp[:, :, :], over(m.iota_row[:, 0:TILES]),
                                    bin_f[:, :].unsqueeze(2).broadcast_to([P, SC, TILES]), ALU.is_equal)
            nc.vector.tensor_scalar(off[:, :], bin_f[:, :], float(TILES - 1), None, ALU.min)
            v.drain()
            nc.vector.tensor_copy(bin_i[:, :], off[:, :]).then_inc(bin_out, 1)
            nc.vector.tensor_tensor(cmp[:, :, :], cmp[:, :, :], over(spare[:, :]), ALU.mult)
            v.drain()
            nc.vector.tensor_reduce(off[:, :], cmp[:, :, :], X_AXIS, ALU.add)
            v.drain()
            nc.vector.scalar_tensor_tensor(out=off[:, :], in0=m.slot_no[:, :], scalar=float(P), in1=off[:, :],
                                           op0=ALU.mult, op1=ALU.add)
            v.drain()
            nc.vector.tensor_scalar(off[:, :], off[:, :], float(E), None, ALU.min)
            v.drain()
            nc.vector.tensor_copy(off_i[:, :], off[:, :])

        @block.tensor
        def _(pe):
            nc.tensor.matmul(hist[:, 0:CT], m.ones_bf[0:LANES, :], m.zeros_bf[0:LANES, 0:CT], start=True, stop=False,
                             skip_group_check=True)

            def count_chunk(c, s):
                pe.wait_ge(oh_made, c + 1)
                held(pe, t_t)
                nc.tensor.matmul(hist[:, 0:CT], m.ones_bf[0:LANES, :], f2(oh[s]), start=False, stop=False,
                                 skip_group_check=True).then_inc(oh_used, 1)

            in_twos(pe, COLS // CH, count_chunk)
            nc.tensor.matmul(hist[:, 0:CT], m.ones_bf[0:LANES, :], m.zeros_bf[0:LANES, 0:CT], start=False, stop=True,
                             skip_group_check=True).then_inc(hist_done, 1)
            if which == 0:
                pe.wait_ge(wrong_made, 1)
                nc.tensor.matmul(count[:, 0:1], m.ones[0:LANES, :], wrong[:, 3:4], start=True, stop=True).then_inc(wrong_sum, 1)

        @block.sync
        def _(sp):
            if which == 0:
                sp.dma_start(m.edges[0][0:E].rearrange("(p c) -> p c", p=LANES), m.packed[:, :]).then_inc(as_is, 16)
                sp.wait_ge(as_is, 16)
            sp.wait_ge(bin_out, 1)
            sp.dma_start(m.bin_dram[which].rearrange("(c p) -> p c", p=P), bin_i[:, :],
                         allow_slow_non_contiguous=True).then_inc(bin_back, 16)
            sp.wait_ge(bin_back, 16)


def one_hot_of_chunk(nc, m, to, c):
    bins = m.iota_row[0:LANES, 0:TILES].unsqueeze(1).broadcast_to([LANES, CH, TILES])
    k = cols(m.key, c * CH, CH).unsqueeze(2).broadcast_to([LANES, CH, TILES])
    return nc.vector.tensor_tensor(to[:, :, :], k, bins, ALU.is_equal)


class Ranking:

    def __init__(self, nc, m, st):
        self.nc, self.m = nc, m
        self.oh = [st.sb(f"oh{s}", [LANES, CH, TILES], BF16) for s in range(2)]
        self.at = st.sb("at", [LANES, CH, TILES])
        self.run = st.ps("run")
        self.oh_made, self.before, self.counted, self.after = (
            st.sem(s) for s in ("oh_made", "before", "counted", "after"))

    def flat(self, t):
        return t[:, :, :].rearrange("p c b -> p (c b)")

    def pe_sum(self, weights, rhs, start=False, stop=False):
        return self.nc.tensor.matmul(self.run[:, 0:CT], weights[0:LANES, :], rhs, start=start, stop=stop, skip_group_check=True)

    def pe_begin(self, pe, turns):
        self.pe_sum(self.m.ones_bf, self.m.zeros_bf[0:LANES, 0:CT], start=True)
        self.pe_lanes_above(pe, turns, 0, 0)

    def pe_lanes_above(self, pe, turns, c, s):
        pe.wait_ge(self.oh_made, c + 1)
        held(pe, turns)
        self.pe_sum(self.m.tri_bf, self.flat(self.oh[s])).then_inc(self.before, 1)

    def pe_rest(self, pe, turns, c, s):
        pe.wait_ge(self.counted, c + 1)
        held(pe, turns)
        self.pe_sum(self.m.rest_bf, self.flat(self.oh[s])).then_inc(self.after, 1)

    def pe_end(self):
        self.pe_sum(self.m.ones_bf, self.m.zeros_bf[0:LANES, 0:CT], stop=True)

    def dve_one_hot(self, v, turns, c, s):
        if reused(c):
            v.wait_ge(self.after, c - 1)
            held(v, turns)
        one_hot_of_chunk(self.nc, self.m, self.oh[s], c).then_inc(self.oh_made, 1)

    def dve_read(self, v, turns, c):
        v.wait_ge(self.before, c + 1)
        held(v, turns)
        self.nc.vector.tensor_tensor(self.flat(self.at), self.run[0:LANES, 0:CT], self.flat(self.m.base)[0:LANES, :],
                                     ALU.add).then_inc(self.counted, 1)

    def dve_rank(self, v, c, s):
        v.drain()
        self.nc.vector.tensor_tensor(self.flat(self.at), self.flat(self.at), self.flat(self.oh[s]), ALU.mult)
        v.drain()
        self.nc.vector.tensor_reduce(cols(self.m.key, c * CH, CH), self.at[:, :, :], X_AXIS, ALU.add)
        v.drain()


class Scatter:

    def __init__(self, nc, m, st, which):
        self.nc, self.m, self.which = nc, m, which
        self.idx, self.pay = st.sb("lanes_idx", [LANES, 2, 8], I32), st.sb("lanes_pay", [LANES, 2, 8], I32)
        self.copied, self.sent, self.turns = st.sem("copied"), st.sems("sent"), st.sem("turns_sc")

    def columns(self, pool, first, count):
        def batch(c, s):
            if reused(c):
                pool.wait_ge(self.sent[s], (c - s) * 64)
                held(pool, self.turns)
            self.nc.gpsimd.tensor_copy(self.idx[:, s, :], cols(self.m.rank_i, c * 8 + first, 8)).then_inc(self.copied, 1)
            self.nc.gpsimd.tensor_copy(self.pay[:, s, :], cols(self.m.packed, c * 8 + first, 8)).then_inc(self.copied, 1)
            pool.wait_ge(self.copied, c * 2 + 2)
            held(pool, self.turns)
            for k in range(8):
                pool.indirect_dma_start(self.m.edges[self.which].rearrange("(e a) -> e a", a=1),
                                        bass.IndirectOffsetOnAxis(ap=self.idx[:, s, k:k + 1], axis=0),
                                        self.pay[:, s, k:k + 1], None).then_inc(self.sent[s], 16)

        in_twos(pool, count // 8, batch)
        for s in range(2):
            pool.wait_ge(self.sent[s], count * 8)


def stage_sort_if_unsorted(nc, m):
    with Stage(nc, "sort") as st:
        ranking, scatter = Ranking(nc, m, st), Scatter(nc, m, st, 0)
        ranked, t_v, t_t = st.sem("ranked"), st.sem("turns_v"), st.sem("turns_t")
        block = st.block()

        @block.vector
        def _(v):
            with v.If(v.value_load(m.unsorted[0:1, 0:1], min_val=0, max_val=1) != 0):
                ranking.dve_one_hot(v, t_v, 0, 0)

                def chunk(c, s):
                    ranking.dve_read(v, t_v, c)
                    ranking.dve_rank(v, c, s)
                    if not (isinstance(c, int) and c == COLS // CH - 1):
                        ranking.dve_one_hot(v, t_v, c + 1, 1 - s)

                chunk(0, 0)
                chunk(1, 1)
                with v.Fori(1, COLS // CH // 2 - 1) as q:
                    chunk(q * 2, 0)
                    chunk(q * 2 + 1, 1)
                chunk(COLS // CH - 2, 0)
                chunk(COLS // CH - 1, 1)
                nc.vector.tensor_copy(m.rank_i[:, :], m.key[:, :]).then_inc(ranked, 1)

        @block.tensor
        def _(pe):
            with pe.If(pe.value_load(m.unsorted[0:1, 0:1], min_val=0, max_val=1) != 0):
                ranking.pe_begin(pe, t_t)

                def chunk(c, s):
                    ranking.pe_rest(pe, t_t, c, s)
                    if not (isinstance(c, int) and c == COLS // CH - 1):
                        ranking.pe_lanes_above(pe, t_t, c + 1, 1 - s)

                chunk(0, 0)
                chunk(1, 1)
                with pe.Fori(1, COLS // CH // 2 - 1) as q:
                    chunk(q * 2, 0)
                    chunk(q * 2 + 1, 1)
                chunk(COLS // CH - 2, 0)
                chunk(COLS // CH - 1, 1)
                ranking.pe_end()

        @block.gpsimd
        def _(pool):
            with pool.If(pool.value_load(m.unsorted[0:1, 0:1], min_val=0, max_val=1) != 0):
                pool.wait_ge(ranked, 1)
                scatter.columns(pool, 0, COLS)


def stage_slots(nc, m, which):
    with Stage(nc, f"slots{which}") as st:
        raw = st.sb("raw", [P, SC, P], I32)
        part = st.sb("part", [P, SC, P], I32)
        loc, nbr = st.sb("loc", [P, SC, P]), st.sb("nbr", [P, SC, P])
        bin_f2 = st.sb("bin_f2", [P, SC])
        pt = [st.ps(f"pt{k}") for k in range(4)]
        sorted_in, slots_ready, turned, bin_in = (st.sem(s) for s in ("sorted_in", "slots_ready", "turned", "bin_in"))
        block = st.block()

        @block.gpsimd
        def _(pool):
            for c in range(SC):
                pool.indirect_dma_start(raw[:, c, :], None, m.edges[which].rearrange("(r c) -> r c", c=P),
                                        bass.IndirectOffsetOnAxis(ap=m.off_i[:, c:c + 1], axis=1)).then_inc(sorted_in, 16)
            pool.wait_ge(sorted_in, 16 * SC)

        @block.sync
        def _(sp):
            sp.dma_start(m.bin_row[:, :], m.bin_dram[which].rearrange("(a c) -> a c", a=1)).then_inc(bin_in, 16)
            sp.wait_ge(bin_in, 16)

        @block.vector
        def _(v):
            nc.vector.tensor_scalar(bin_f2[:, :], m.bin_f[:, :], -float(P), None, ALU.mult)
            v.wait_ge(sorted_in, 16 * SC)
            shift, keep = (ALU.logical_shift_right, BITS), (ALU.bitwise_and, NOWHERE)
            own, other = (keep, shift) if which == 0 else (shift, keep)
            nc.vector.tensor_scalar(part[:, :, :], raw[:, :, :], own[1], None, own[0])
            v.drain()
            nc.vector.tensor_copy(loc[:, :, :], part[:, :, :])
            v.drain()
            nc.vector.tensor_scalar(part[:, :, :], raw[:, :, :], other[1], None, other[0])
            for c in range(SC):
                nc.vector.tensor_scalar(loc[:, c, :], loc[:, c, :], bin_f2[:, c:c + 1], None, ALU.add)
            v.drain()
            nc.vector.tensor_copy(nbr[:, :, :], part[:, :, :])
            v.drain().then_inc(slots_ready, 1)
            v.wait_ge(turned, 1)
            for k, t in enumerate((m.LOC, m.GI)):
                nc.vector.tensor_copy(t[:, 0:512], pt[2 * k][:, :])
                nc.vector.tensor_copy(t[:, 512:SC * P], pt[2 * k + 1][:, 0:SC * P - 512])

        @block.tensor
        def _(pe):
            pe.wait_ge(slots_ready, 1)
            for k, t in enumerate((loc, nbr)):
                for c in range(SC):
                    nc.tensor.transpose(pt[2 * k + c // 4][:, (c % 4) * P:(c % 4 + 1) * P], t[:, c, :], m.ident[:, :])
            pe.drain().then_inc(turned, 1)


def stage_conv(nc, m, name, table, rank_sources, sum_keys):
    with Stage(nc, name) as st:
        NB = 4
        idx = st.sb("idx", [P, 2, RING], I32)
        msg = st.sb("msg", [P, 2 * RING, D])
        S = st.sb("S", [P, 2, RING, P])
        ps = [st.ps(f"ps{k}") for k in range(NB)]
        ranking = Ranking(nc, m, st) if rank_sources else None
        kv = KeyValueSums(nc, m, st) if sum_keys else None
        idx_ready, got = st.sem("idx_ready"), st.sems("got")
        s_made, summed, added = st.sem("s_made"), st.sem("summed"), st.sem("added")
        tv, tt, tp, ta = (st.sem(n) for n in ("turns_v", "turns_t", "turns_p", "turns_a"))
        ts = st.sem("turns_s")
        block = st.block()
        ROUNDS, CHUNKS = SLOT_TILES // RING, COLS // CH

        def in_rounds(eng, body):
            beside = CHUNKS // 2 if rank_sources else TILES if sum_keys else 1

            def pair(q, more):
                for h in range(2):
                    body(q * 2 + h, h, q * 2 + h if more and rank_sources else None, q if more and sum_keys else None)

            pair(0, True)
            if beside > 1:
                with eng.Fori(1, beside - 1) as q:
                    pair(q, True)
                pair(beside - 1, True)
            with eng.Fori(beside, ROUNDS // 2 - 1) as q:
                pair(q, False)
            pair(ROUNDS // 2 - 1, False)

        last_chunk = lambda r: isinstance(r, int) and r == CHUNKS - 1

        @block.gpsimd
        def _(pool):
            def gathers(r, h):
                pool.wait_ge(idx_ready, r + 1)
                if reused(r):
                    pool.wait_ge(summed, (r - 1) * RING)
                held(pool, tp)
                for k in range(RING):
                    pool.indirect_dma_start(msg[:, h * RING + k, :], None, table,
                                            bass.IndirectOffsetOnAxis(ap=idx[:, h, k:k + 1], axis=0)).then_inc(got[h], 16)

            in_twos(pool, ROUNDS, gathers)

        @block.scalar
        def _(act):
            def indices(r, h):
                if reused(r):
                    act.wait_ge(got[h], (r - h) * (8 * RING))
                    held(act, ta)
                nc.scalar.copy(idx[:, h, :], cols(m.GI, r * RING, RING)).then_inc(idx_ready, 1)

            def ahead(r, h, chunk, tile):
                if tile is not None and h == 0:
                    kv.act_square(act, ta, tile)
                if tile is not None and h == 1:
                    kv.act_root(act, ta, tile)
                if not (isinstance(r, int) and r >= ROUNDS - 2):
                    indices(r + 2, h)

            indices(0, 0)
            indices(1, 1)
            in_rounds(act, ahead)

        if sum_keys:
            @block.sync
            def _(sp):
                in_twos(sp, TILES - 1, lambda i, s: kv.sp_load(sp, ts, i))
                kv.sp_load(sp, ts, TILES - 1)
                sp.wait_ge(kv.xt_in, TILES * 16)

        @block.vector
        def _(v):
            def one_hots(r, h):
                for k in range(RING):
                    last = nc.vector.tensor_scalar(S[:, h, k, :], m.iota_row[:, :], cols(m.LOC, r * RING + k, 1), None,
                                                   ALU.is_equal)
                last.then_inc(s_made, 1)

            def tile(r, h, chunk, keys):
                if chunk is not None:
                    ranking.dve_read(v, tv, r)
                    if not last_chunk(r):
                        ranking.dve_one_hot(v, tv, r + 1, 1 - h)
                if not (isinstance(r, int) and r == ROUNDS - 1):
                    if not (isinstance(r, int) and r == 0):
                        v.wait_ge(summed, r * RING)
                        held(v, tv)
                    one_hots(r + 1, 1 - h)
                if keys is not None and h == 1:
                    kv.dve_norm(v, tv, keys)
                starts = [v.snap(b * AW) for b in bins_of_round(nc, m, DVE, r)]
                for k in range(RING):
                    v.drain()
                    v.wait_ge(summed, r * RING + k + 1)
                    acc = cols(m.ACC, starts[k], D)
                    nc.vector.tensor_tensor(acc, acc, ps[k % NB][:, 0:D], ALU.add).then_inc(added, 1)
                if keys is not None and h == 0:
                    kv.dve_center(v, tv, keys)
                if chunk is not None:
                    ranking.dve_rank(v, r, h)

            if sum_keys:
                nc.vector.memset(kv.vn[:, :, :], 1.0)
            if rank_sources:
                ranking.dve_one_hot(v, tv, 0, 0)
            one_hots(0, 0)
            in_rounds(v, tile)
            if sum_keys:
                kv.dve_end(v)
            if rank_sources:
                nc.vector.tensor_copy(m.rank_i[:, :], m.key[:, :])

        @block.tensor
        def _(pe):
            def sums(r, h, chunk, keys):
                if keys is not None and h == 0:
                    kv.pe_project(pe, tt, keys)
                pe.wait_ge(got[h], (r - h) * (8 * RING) + 16 * RING)
                pe.wait_ge(s_made, r + 1)
                held(pe, tt)
                for k in range(RING):
                    if k % 2 == 0 and (k >= NB or not (isinstance(r, int) and r == 0)):
                        pe.wait_ge(added, r * RING + k - 2)
                        held(pe, tt)
                    nc.tensor.matmul(ps[k % NB][:, 0:D], S[:, h, k, :], msg[:, h * RING + k, :], start=True,
                                     stop=True).then_inc(summed, 1)
                if keys is not None and h == 1:
                    kv.pe_sums(pe, tt, keys)
                if chunk is not None:
                    ranking.pe_rest(pe, tt, r, h)
                if chunk is not None and not last_chunk(r):
                    ranking.pe_lanes_above(pe, tt, r + 1, 1 - h)

            if rank_sources:
                ranking.pe_begin(pe, tt)
            if sum_keys:
                kv.pe_begin()
            in_rounds(pe, sums)
            if rank_sources:
                ranking.pe_end()
            if sum_keys:
                kv.pe_end()


def stage_mlp(nc, m, name, w1, b1, w2, b2, last, columns):
    with Stage(nc, name) as st:
        two = lambda n, w: [st.sb(f"{n}{s}", [P, w]) for s in range(2)]
        hs, ht, h1, a, b, xt = two("hs", D), two("ht", D), two("h1", D), two("a", D), two("b", D), two("xt", D)
        pt, ph, po = ([st.ps(f"{n}{s}") for s in range(2)] for n in ("pt", "ph", "po"))
        scatter = Scatter(nc, m, st, 1)
        taken, turned, ht_made, h1_ps, h1_made, out_ps, out_made = (
            st.sem(n) for n in ("taken", "turned", "ht_made", "h1_ps", "h1_made", "out_ps", "out_made"))
        stored, xt_in = st.sems("stored"), st.sems("xt_in")
        tv, ta, tt, tp, ts = (st.sem(n) for n in ("turns_v", "turns_a", "turns_t", "turns_p", "turns_s"))
        block = st.block()

        @block.scalar
        def _(act):
            def first(i, s):
                if reused(i):
                    act.wait_ge(turned, i - 1)
                    held(act, ta)
                nc.scalar.copy(hs[s][:, :], cols(m.ACC, i * AW, D)).then_inc(taken, 1)

            def tile(i, s, rows):
                if isinstance(i, int) and i == 0:
                    first(0, 0)
                if not (isinstance(i, int) and i == TILES - 1):
                    first(i + 1, 1 - s)
                act.wait_ge(turned, i + 1)
                if reused(i):
                    act.wait_ge(h1_ps, i - 1)
                held(act, ta)
                nc.scalar.copy(ht[s][:, :], pt[s][:, 0:D]).then_inc(ht_made, 1)
                act.wait_ge(h1_ps, i + 1)
                if reused(i):
                    act.wait_ge(out_ps, i - 1)
                held(act, ta)
                for c in range(2):
                    nc.scalar.activation(h1[s][:, c * P:c * P + P], ph[s][:, c * P:c * P + P], ACT.Relu, bias=b1[:, c:c + 1])
                act.drain().then_inc(h1_made, 1)

            over_tiles(act, tile)

        @block.tensor
        def _(pe):
            def turn(i, s):
                pe.wait_ge(taken, i + 1)
                if reused(i):
                    pe.wait_ge(ht_made, i - 1)
                held(pe, tt)
                for c in range(2):
                    tr = nc.tensor.transpose(pt[s][:, c * P:c * P + P], hs[s][:, c * P:c * P + P], m.ident[:, :])
                tr.then_inc(turned, 1)

            def second(i, s):
                pe.wait_ge(h1_made, i + 1)
                if reused(i):
                    pe.wait_ge(out_made, i - 1)
                if last:
                    pe.wait_ge(xt_in[s], dma_count(i, s))
                held(pe, tt)
                if last:
                    for c in range(2):
                        nc.tensor.matmul(po[s][:, D:2 * D], xt[s][:, c * P:c * P + P], m.mixM[:, c, :],
                                         start=(c == 0), stop=(c == 1))
                for c in range(2):
                    mm = nc.tensor.matmul(po[s][:, 0:D], h1[s][:, c * P:c * P + P], w2[:, c, :], start=(c == 0), stop=(c == 1))
                mm.then_inc(out_ps, 1)

            def tile(i, s, rows):
                if isinstance(i, int) and i == 0:
                    turn(0, 0)
                pe.wait_ge(ht_made, i + 1)
                if reused(i):
                    pe.wait_ge(h1_made, i - 1)
                held(pe, tt)
                for k in range(2):
                    for c in range(2):
                        mm = nc.tensor.matmul(ph[s][:, k * P:k * P + P], w1[:, c, k * P:k * P + P], ht[s][:, c * P:c * P + P],
                                              start=(c == 0), stop=(c == 1))
                mm.then_inc(h1_ps, 1)
                if not (isinstance(i, int) and i == TILES - 1):
                    turn(i + 1, 1 - s)
                if not (isinstance(i, int) and i == 0):
                    second(i - 1, 1 - s)

            over_tiles(pe, tile)
            second(TILES - 1, 0)

        @block.vector
        def _(v):
            def tile(i, s, rows):
                v.wait_ge(out_ps, i + 1)
                if reused(i) and not last:
                    v.wait_ge(stored[s], dma_count_before(i, s))
                held(v, tv)
                nc.vector.tensor_tensor(b[s][:, :], po[s][:, 0:D], b2[:, :], ALU.add)
                if not last:
                    v.drain()
                    nc.vector.tensor_scalar(a[s][:, :], b[s][:, :], 0.0, None, ALU.max).then_inc(out_made, 1)
                    nc.vector.tensor_scalar(cols(m.ACC, i * AW, D), b[s][:, :], 0.0, None, ALU.max)
                    return
                nc.vector.tensor_tensor(a[s][:, :], po[s][:, D:2 * D], m.bor[:, :], ALU.add)
                v.drain().then_inc(out_made, 1)
                x = cols(m.X, i * D, D)
                nc.vector.tensor_scalar(b[s][:, :], b[s][:, :], 0.0, 2.0, ALU.max, ALU.mult)
                nc.vector.tensor_tensor(x, x, a[s][:, :], ALU.add)
                v.drain()
                nc.vector.tensor_tensor(x, x, b[s][:, :], ALU.add)

            over_tiles(v, tile)

        @block.gpsimd
        def _(pool):
            scatter.columns(pool, *columns)

        @block.sync
        def _(sp):
            def store(i, s, rows):
                sp.wait_ge(out_made, i + 1)
                held(sp, ts)
                sp.dma_start(m.conv1_table[bass.ds(i * P, P), :], a[s][:, :]).then_inc(stored[s], 16)

            def load(i, s, rows):
                if reused(i):
                    sp.wait_ge(out_ps, i - 1)
                    held(sp, ts)
                sp.dma_start(xt[s][:, :], m.xnT[bass.ds(i * P, P), :]).then_inc(xt_in[s], 16)

            over_tiles(sp, load if last else store)
            for s in range(2):
                sp.wait_ge((xt_in if last else stored)[s], dma_count(TILES - 1 - s, s))


def stage_ffn(nc, m, columns):
    with Stage(nc, "ffn") as st:
        scatter = Scatter(nc, m, st, 1)
        two = lambda n, w: [st.sb(f"{n}{s}", [P, w]) for s in range(2)]
        xn, xt, a = two("xn", D), two("xt", D), two("a", D)
        pt, po = ([st.ps(f"{n}{s}") for s in range(2)] for n in ("pt", "po"))
        xn_made, turned, xt_made, out_ps, out_read = (st.sem(n) for n in ("xn_made", "turned", "xt_made", "out_ps", "out_read"))
        tv, ta, tt = (st.sem(n) for n in ("turns_v", "turns_a", "turns_t"))
        block = st.block()

        @block.gpsimd
        def _(pool):
            scatter.columns(pool, *columns)

        @block.vector
        def _(v):
            def norm(i, s):
                if reused(i):
                    v.wait_ge(turned, i - 1)
                    held(v, tv)
                nc.vector.tensor_scalar(xn[s][:, :], cols(m.X, i * D, D), cols(m.mean, i, 1), cols(m.rstd, i, 1),
                                        ALU.subtract, ALU.mult).then_inc(xn_made, 1)

            def added(i, s):
                v.wait_ge(out_ps, i + 1)
                held(v, tv)
                nc.vector.tensor_tensor(a[s][:, :], po[s][:, 0:D], m.fbr[:, :], ALU.add)
                v.drain().then_inc(out_read, 1)
                x = cols(m.X, i * D, D)
                nc.vector.tensor_tensor(x, x, a[s][:, :], ALU.add)

            def step(i, s):
                if there(i + 1):
                    norm(i + 1, 1 - s)
                if there(i - 1):
                    added(i - 1, 1 - s)

            skewed(v, 1, step)

        @block.scalar
        def _(act):
            def tile(i, s, rows):
                act.wait_ge(turned, i + 1)
                if reused(i):
                    act.wait_ge(out_ps, i - 1)
                held(act, ta)
                nc.scalar.copy(xt[s][:, :], pt[s][:, 0:D]).then_inc(xt_made, 1)

            over_tiles(act, tile)

        @block.tensor
        def _(pe):
            def turn(i, s):
                pe.wait_ge(xn_made, i + 1)
                if reused(i):
                    pe.wait_ge(xt_made, i - 1)
                held(pe, tt)
                for c in range(2):
                    tr = nc.tensor.transpose(pt[s][:, c * P:c * P + P], xn[s][:, c * P:c * P + P], m.ident[:, :])
                tr.then_inc(turned, 1)

            def tile(i, s, rows):
                if isinstance(i, int) and i == 0:
                    turn(0, 0)
                if not (isinstance(i, int) and i == TILES - 1):
                    turn(i + 1, 1 - s)
                pe.wait_ge(xt_made, i + 1)
                if reused(i):
                    pe.wait_ge(out_read, i - 1)
                held(pe, tt)
                for c in range(2):
                    mm = nc.tensor.matmul(po[s][:, 0:D], xt[s][:, c * P:c * P + P], m.fT[:, c, :], start=(c == 0), stop=(c == 1))
                mm.then_inc(out_ps, 1)

            over_tiles(pe, tile)


def stage_attn_kv(nc, m, columns):
    W2 = P + 1
    with Stage(nc, "akv") as st:
        scatter = Scatter(nc, m, st, 1)
        two = lambda n, w: [st.sb(f"{n}{s}", [P, w]) for s in range(2)]
        xr, xt, g, low, ex, kp = two("xr", D), two("xt", D), two("g", 72), two("low", D), two("ex", D), two("kp", D)
        vp = [st.sb(f"vp{s}", [P, 2, W2]) for s in range(2)]
        kv_sum = st.sb("kv_sum", [P, 2 * W2])
        pt, pk, pg = ([st.ps(f"{n}{s}") for s in range(2)] for n in ("pt", "pk", "pg"))
        psum_kv = st.ps("kv")
        xr_made, turned, xt_made, projected, low_made, ex_made, kp_made, vp_made, g_made, used, vones, sums = (
            st.sem(n) for n in ("xr_made", "turned", "xt_made", "projected", "low_made", "ex_made", "kp_made", "vp_made",
                                "g_made", "used", "vones", "sums"))
        out_xt, out_g = st.sems("out_xt"), st.sems("out_g")
        tv, ta, tt, tp, ts = (st.sem(n) for n in ("turns_v", "turns_a", "turns_t", "turns_p", "turns_s"))
        block = st.block()

        @block.vector
        def _(v):
            for s in range(2):
                nc.vector.memset(vp[s][:, :, :], 1.0)
            v.drain().then_inc(vones, 1)

            def norm(i, s):
                if reused(i):
                    v.wait_ge(turned, i - 1)
                    held(v, tv)
                nc.vector.tensor_scalar(xr[s][:, :], cols(m.X, i * D, D), cols(m.mean, i, 1), cols(m.rms_in, i, 1),
                                        ALU.subtract, ALU.mult).then_inc(xr_made, 1)

            def keys(i, s):
                v.wait_ge(projected, i + 1)
                if reused(i):
                    v.wait_ge(ex_made, i - 1)
                held(v, tv)
                nc.vector.tensor_scalar(low[s][:, :], pk[s][:, 0:D], 0.0, None, ALU.min).then_inc(low_made, 1)
                v.wait_ge(ex_made, i + 1)
                if reused(i):
                    v.wait_ge(used, i - 1)
                held(v, tv)
                nc.vector.scalar_tensor_tensor(out=kp[s][:, :], in0=pk[s][:, 0:D], scalar=0.0, in1=ex[s][:, :],
                                               op0=ALU.max, op1=ALU.add).then_inc(kp_made, 1)

            def step(i, s):
                if there(i + 1):
                    norm(i + 1, 1 - s)
                if there(i - 1):
                    keys(i - 1, 1 - s)

            skewed(v, 1, step)
            v.wait_ge(sums, 1)
            nc.vector.tensor_copy(kv_sum[:, :], psum_kv[:, 0:2 * W2])
            v.drain()
            for c in range(2):
                lo = c * W2
                nc.vector.tensor_tensor(m.kvbd[:, c, 0:P], kv_sum[:, lo:lo + P], m.mask32[:, :], ALU.mult)
                nc.vector.tensor_scalar(m.kvbd[:, c, P:P + 4], m.mask32[:, 0:P:32], kv_sum[:, lo + P:lo + P + 1], None, ALU.mult)

        @block.scalar
        def _(act):
            act.wait_ge(vones, 1)

            def turned_out(i, s):
                act.wait_ge(turned, i + 1)
                if reused(i):
                    act.wait_ge(projected, i - 1)
                    act.wait_ge(out_xt[s], dma_count_before(i, s))
                held(act, ta)
                nc.scalar.copy(xt[s][:, :], pt[s][:, 0:D]).then_inc(xt_made, 1)

            def tile(i, s, rows):
                if isinstance(i, int) and i == 0:
                    turned_out(0, 0)
                if not (isinstance(i, int) and i == TILES - 1):
                    turned_out(i + 1, 1 - s)
                act.wait_ge(projected, i + 1)
                if reused(i):
                    act.wait_ge(out_g[s], dma_count_before(i, s))
                    act.wait_ge(used, i - 1)
                held(act, ta)
                nc.scalar.activation(g[s][:, :], pg[s][:, 0:72], ACT.Copy, scale=cols(m.rms_out, i, 1)).then_inc(g_made, 1)
                nc.scalar.activation(cols(m.EL, i * 4, 4), pg[s][:, 68:72], ACT.Copy, scale=cols(m.rms_out, i, 1))
                nc.scalar.copy(vp[s][:, :, 0:P], pg[s][:, D:2 * D].rearrange("p (c n) -> p c n", c=2)).then_inc(vp_made, 1)
                act.wait_ge(low_made, i + 1)
                if reused(i):
                    act.wait_ge(kp_made, i - 1)
                held(act, ta)
                nc.scalar.activation(ex[s][:, :], low[s][:, :], ACT.Exp).then_inc(ex_made, 1)

            over_tiles(act, tile)

        @block.tensor
        def _(pe):
            nc.tensor.matmul(psum_kv[:, 0:2 * W2], m.ones[:, :], m.zeros[:, 0:2 * W2], start=True, stop=False, skip_group_check=True)

            def turn(i, s):
                pe.wait_ge(xr_made, i + 1)
                if reused(i):
                    pe.wait_ge(xt_made, i - 1)
                held(pe, tt)
                for c in range(2):
                    tr = nc.tensor.transpose(pt[s][:, c * P:c * P + P], xr[s][:, c * P:c * P + P], m.ident[:, :])
                tr.then_inc(turned, 1)

            def gather_sums(i, s, rows):
                pe.wait_ge(kp_made, i + 1)
                pe.wait_ge(vp_made, i + 1)
                held(pe, tt)
                for c in range(2):
                    mm = nc.tensor.matmul(psum_kv[:, c * W2:c * W2 + W2], kp[s][0:rows, c * P:c * P + P], vp[s][0:rows, c, :],
                                          start=False, stop=False, skip_group_check=True)
                mm.then_inc(used, 1)

            def tile(i, s, rows):
                if isinstance(i, int) and i == 0:
                    turn(0, 0)
                if not (isinstance(i, int) and i == TILES - 1):
                    turn(i + 1, 1 - s)
                pe.wait_ge(xt_made, i + 1)
                if reused(i):
                    pe.wait_ge(kp_made, i - 1)
                    pe.wait_ge(vp_made, i - 1)
                    pe.wait_ge(g_made, i - 1)
                held(pe, tt)
                for c in range(2):
                    nc.tensor.matmul(pg[s][:, 0:72], xt[s][:, c * P:c * P + P], m.gcat[:, c, :], start=(c == 0), stop=(c == 1))
                for c in range(2):
                    nc.tensor.matmul(pg[s][:, D:2 * D], xt[s][:, c * P:c * P + P], m.wqkvs[:, c, 2 * D:3 * D], start=(c == 0), stop=(c == 1))
                for c in range(2):
                    mm = nc.tensor.matmul(pk[s][:, 0:D], xt[s][:, c * P:c * P + P], m.wqkvs[:, c, D:2 * D], start=(c == 0), stop=(c == 1))
                mm.then_inc(projected, 1)
                if not (isinstance(i, int) and i == 0):
                    gather_sums(i - 1, 1 - s, P)

            over_tiles(pe, tile)
            gather_sums(TILES - 1, 0, TAIL)
            nc.tensor.matmul(psum_kv[:, 0:2 * W2], m.ones[:, :], m.zeros[:, 0:2 * W2], start=False, stop=True,
                             skip_group_check=True).then_inc(sums, 1)

        @block.gpsimd
        def _(pool):
            scatter.columns(pool, *columns)

        @block.sync
        def _(sp):
            def tile(i, s, rows):
                sp.wait_ge(xt_made, i + 1)
                held(sp, ts)
                sp.dma_start(m.xrT[bass.ds(i * P, P), :], xt[s][:, :]).then_inc(out_xt[s], 16)
                sp.wait_ge(g_made, i + 1)
                held(sp, ts)
                sp.dma_start(m.attn_table[bass.ds(i * P, P), :], g[s][:, 0:GW]).then_inc(out_g[s], 16)

            over_tiles(sp, tile)
            for s in range(2):
                sp.wait_ge(out_xt[s], dma_count(TILES - 1 - s, s))
                sp.wait_ge(out_g[s], dma_count(TILES - 1 - s, s))


def stage_attn_q(nc, m, columns):
    with Stage(nc, "aq") as st:
        scatter = Scatter(nc, m, st, 1)
        two = lambda n, w: [st.sb(f"{n}{s}", [P, w]) for s in range(2)]
        xt, low, ex, qp, o, ot = (two(n, D) for n in ("xt", "low", "ex", "qp", "o", "ot"))
        den = st.sb("den", [P, 2, 4])
        z = st.sb("z", [P, 2, 4])
        pq, pn, pt, po = ([st.ps(f"{n}{s}") for s in range(2)] for n in ("pq", "pn", "pt", "po"))
        q_ps, low_made, ex_made, qp_made, n_ps, o_made, turned, ot_made, out_ps, h_made = (
            st.sem(n) for n in ("q_ps", "low_made", "ex_made", "qp_made", "n_ps", "o_made", "turned", "ot_made",
                                "out_ps", "h_made"))
        xt_in = st.sems("xt_in")
        tv, ta, tt, ts = (st.sem(n) for n in ("turns_v", "turns_a", "turns_t", "turns_s"))
        block = st.block()
        W = P + 4

        @block.sync
        def _(sp):
            def load(i, s, rows):
                if reused(i):
                    sp.wait_ge(q_ps, i - 1)
                    held(sp, ts)
                sp.dma_start(xt[s][:, :], m.xrT[bass.ds(i * P, P), :]).then_inc(xt_in[s], 16)

            over_tiles(sp, load)

        @block.tensor
        def _(pe):
            def queries(i, s):
                pe.wait_ge(xt_in[s], dma_count(i, s))
                if reused(i):
                    pe.wait_ge(qp_made, i - 1)
                held(pe, tt)
                for k in range(2):
                    for c in range(2):
                        mm = nc.tensor.matmul(pq[s][:, k * P:k * P + P], m.wqkvs[:, c, k * P:k * P + P], xt[s][:, c * P:c * P + P],
                                              start=(c == 0), stop=(c == 1))
                mm.then_inc(q_ps, 1)

            def products(i, s):
                pe.wait_ge(qp_made, i + 1)
                if reused(i):
                    pe.wait_ge(o_made, i - 1)
                held(pe, tt)
                for c in range(2):
                    mm = nc.tensor.matmul(pn[s][:, c * W:c * W + W], qp[s][:, c * P:c * P + P], m.kvbd[:, c, :], start=True, stop=True)
                mm.then_inc(n_ps, 1)

            def turn(i, s):
                pe.wait_ge(o_made, i + 1)
                if reused(i):
                    pe.wait_ge(ot_made, i - 1)
                held(pe, tt)
                for c in range(2):
                    tr = nc.tensor.transpose(pt[s][:, c * P:c * P + P], o[s][:, c * P:c * P + P], m.ident[:, :])
                tr.then_inc(turned, 1)

            def project_out(i, s):
                pe.wait_ge(ot_made, i + 1)
                if reused(i):
                    pe.wait_ge(h_made, i - 1)
                held(pe, tt)
                for c in range(2):
                    mm = nc.tensor.matmul(po[s][:, 0:D], ot[s][:, c * P:c * P + P], m.wouts[:, c, :], start=(c == 0), stop=(c == 1))
                mm.then_inc(out_ps, 1)

            def step(i, s):
                if there(i + 1):
                    queries(i + 1, 1 - s)
                if there(i):
                    products(i, s)
                if there(i - 1):
                    turn(i - 1, 1 - s)
                if there(i - 2):
                    project_out(i - 2, s)

            skewed(pe, 2, step)

        @block.scalar
        def _(act):
            def exps(i, s):
                act.wait_ge(low_made, i + 1)
                if reused(i):
                    act.wait_ge(qp_made, i - 1)
                held(act, ta)
                nc.scalar.activation(ex[s][:, :], low[s][:, :], ACT.Exp).then_inc(ex_made, 1)

            def turned_out(i, s):
                act.wait_ge(turned, i + 1)
                if reused(i):
                    act.wait_ge(out_ps, i - 1)
                held(act, ta)
                nc.scalar.copy(ot[s][:, :], pt[s][:, 0:D]).then_inc(ot_made, 1)

            def step(i, s):
                if there(i + 1):
                    exps(i + 1, 1 - s)
                if there(i - 1):
                    turned_out(i - 1, 1 - s)

            skewed(act, 2, step)

        @block.gpsimd
        def _(pool):
            scatter.columns(pool, *columns)

        @block.vector
        def _(v):
            def low_of(i, s):
                v.wait_ge(q_ps, i + 1)
                if reused(i):
                    v.wait_ge(ex_made, i - 1)
                held(v, tv)
                nc.vector.tensor_scalar(low[s][:, :], pq[s][:, 0:D], 0.0, None, ALU.min).then_inc(low_made, 1)

            def queries(i, s):
                v.wait_ge(ex_made, i + 1)
                if reused(i):
                    v.wait_ge(n_ps, i - 1)
                held(v, tv)
                nc.vector.scalar_tensor_tensor(out=qp[s][:, :], in0=pq[s][:, 0:D], scalar=0.0, in1=ex[s][:, :],
                                               op0=ALU.max, op1=ALU.add).then_inc(qp_made, 1)
                nc.vector.tensor_scalar(cols(m.ACC, i * AW, D), cols(m.X, i * D, D), cols(m.mean, i, 1), cols(m.rstd, i, 1),
                                        ALU.subtract, ALU.mult)

            def divided(i, s):
                v.wait_ge(n_ps, i + 1)
                if reused(i):
                    v.wait_ge(turned, i - 1)
                held(v, tv)
                n3 = pn[s][:, 0:2 * W].rearrange("p (c n) -> p c n", c=2)
                nc.vector.tensor_scalar(den[:, :, :], n3[:, :, P:W], 1e-6, None, ALU.add)
                v.drain()
                nc.vector.reciprocal(z[:, :, :], den[:, :, :])
                acc = cols(m.ACC, i * AW, D)
                nc.vector.tensor_tensor(acc, acc, m.boutr[:, :], ALU.add)
                v.drain()
                for c in range(2):
                    op = nc.vector.tensor_tensor(o[s][:, c * P:c * P + P].rearrange("p (g j) -> p g j", j=32),
                                                 n3[:, c, 0:P].rearrange("p (g j) -> p g j", j=32),
                                                 z[:, c, :].unsqueeze(2).broadcast_to([P, 4, 32]), ALU.mult)
                op.then_inc(o_made, 1)

            def out_added(i, s):
                v.wait_ge(out_ps, i + 1)
                held(v, tv)
                acc = cols(m.ACC, i * AW, D)
                nc.vector.tensor_tensor(acc, acc, po[s][:, 0:D], ALU.add).then_inc(h_made, 1)

            def step(i, s):
                if there(i):
                    queries(i, s)
                if there(i + 1):
                    low_of(i + 1, 1 - s)
                if there(i):
                    divided(i, s)
                if there(i - 2):
                    out_added(i - 2, s)

            skewed(v, 2, step)


def stage_attn_add(nc, m):
    with Stage(nc, "aadd") as st:
        parts = st.sb("parts", [P, TILES * 6])
        a, b, r = (st.sb(n, [P, TILES]) for n in ("a", "b", "r"))
        t = [st.sb(f"t{s}", [P, D]) for s in range(2)]
        ready, rooted = st.sem("ready"), st.sem("rooted")
        block = st.block()

        @block.vector
        def _(v):
            with v.Fori(0, TILES // 7) as q:
                for k in range(7):
                    nc.vector.bn_stats(parts[:, bass.ds(q * 42 + k * 6, 6)], cols(m.ACC, q * (7 * AW) + k * AW, D))
            v.drain()
            f = lambda k: parts[:, :].rearrange("p (i s) -> p i s", s=6)[:, :, k]
            nc.vector.tensor_tensor(r[:, :], f(2), f(5), ALU.add)
            nc.vector.tensor_tensor(a[:, :], f(1), f(1), ALU.mult)
            nc.vector.tensor_tensor(b[:, :], f(4), f(4), ALU.mult)
            v.drain()
            nc.vector.tensor_tensor(a[:, :], a[:, :], b[:, :], ALU.add)
            nc.vector.tensor_scalar(r[:, :], r[:, :], 1.0 / D, 1e-6, ALU.mult, ALU.add)
            v.drain()
            nc.vector.scalar_tensor_tensor(out=b[:, :], in0=a[:, :], scalar=0.5, in1=r[:, :], op0=ALU.mult, op1=ALU.add)
            v.drain().then_inc(ready, 1)
            v.wait_ge(rooted, 1)
            nc.vector.reciprocal(r[:, :], a[:, :])
            v.drain()

            def tile(i, s, rows):
                h, x = cols(m.ACC, i * AW, D), cols(m.X, i * D, D)
                nc.vector.tensor_tensor(t[s][:, :], h, m.mw2r[:, :], ALU.mult)
                v.drain()
                nc.vector.scalar_tensor_tensor(out=t[s][:, :], in0=t[s][:, :], scalar=cols(r, i, 1), in1=h, op0=ALU.mult, op1=ALU.add)
                v.drain()
                nc.vector.tensor_tensor(x, x, t[s][:, :], ALU.add)

            over_tiles(v, tile)

        @block.scalar
        def _(act):
            act.wait_ge(ready, 1)
            nc.scalar.activation(a[:, :], b[:, :], ACT.Sqrt).then_inc(rooted, 1)


def stage_gat(nc, m):
    with Stage(nc, "gat") as st:
        idx = st.sb("idx", [P, 2, RING], I32)
        msg = st.sb("msg", [P, 2 * RING, GW])
        SB = st.sb("SB", [P, 2, RING, P], BF16)
        S = st.sb("S", [P, 2, RING, P])
        ST = st.sb("ST", [P, 2, RING, P], BF16)
        M = st.sb("M", [P, 2 * RING, AW])
        el3 = st.sb("el3", [P, TILES, 3, 4], BF16)
        rest = st.sb("rest", [P, TILES, 4])
        zz, lk = (st.sb(n, [P, 2, RING, 4]) for n in ("zz", "lk"))
        pst = st.ps("pst", (P, RING * P), BF16)
        pel = [st.ps(f"pel{k}") for k in range(2)]
        NB = 4
        ps = [st.ps(f"ps{k}") for k in range(NB)]
        idx_ready, got = st.sem("idx_ready"), st.sems("got", 2)
        sb_made, turned, st_made, s_made, el_made, lk_made, e_made, m_made, summed, added, el_cut = (
            st.sem(n) for n in ("sb_made", "turned", "st_made", "s_made", "el_made", "lk_made", "e_made", "m_made",
                                "summed", "added", "el_cut"))
        tv, tt, tp, ta = (st.sem(n) for n in ("turns_v", "turns_t", "turns_p", "turns_a"))
        block = st.block()
        ROUNDS = SLOT_TILES // RING
        flat = lambda t, h: t[:, h, :, :].rearrange("p k n -> p (k n)")

        def staggered(eng, step):
            for r in (-2, -1, 0, 1):
                step(r, r % 2)
            with eng.Fori(1, (ROUNDS - 2) // 2) as q:
                step(q * 2, 0)
                step(q * 2 + 1, 1)
            for r in (ROUNDS - 2, ROUNDS - 1):
                step(r, r % 2)

        there = lambda r: not isinstance(r, int) or 0 <= r < ROUNDS
        later = lambda r, n: not isinstance(r, int) or r >= n

        @block.gpsimd
        def _(pool):
            def gathers(r, h):
                pool.wait_ge(idx_ready, r + 1)
                if reused(r):
                    pool.wait_ge(m_made, r - 1)
                held(pool, tp)
                for k in range(RING):
                    pool.indirect_dma_start(msg[:, h * RING + k, :], None, m.attn_table,
                                            bass.IndirectOffsetOnAxis(ap=idx[:, h, k:k + 1], axis=0)).then_inc(got[h], 16)

            in_twos(pool, ROUNDS, gathers)

        @block.scalar
        def _(act):
            def indices(r, h):
                nc.scalar.copy(idx[:, h, :], cols(m.GI, r * RING, RING)).then_inc(idx_ready, 1)

            indices(0, 0)
            indices(1, 1)

            def step(r, h):
                if there(r + 1):
                    act.wait_ge(lk_made, r + 2)
                    if later(r, 1):
                        act.wait_ge(summed, r * RING)
                    held(act, ta)
                    nc.scalar.activation(M[:, (1 - h) * RING:(2 - h) * RING, D:AW], lk[:, 1 - h, :, :], ACT.Exp
                                         ).then_inc(e_made, 1)
                    if there(r + 3):
                        indices(r + 3, 1 - h)
                if there(r + 2):
                    act.wait_ge(turned, r + 3)
                    if later(r, 0):
                        act.wait_ge(el_made, r + 1)
                    held(act, ta)
                    nc.scalar.copy(flat(ST, h), pst[:, :]).then_inc(st_made, 1)
                if there(r + 1):
                    nc.scalar.copy(flat(S, 1 - h), flat(SB, 1 - h)).then_inc(s_made, 1)

            staggered(act, step)

        @block.tensor
        def _(pe):
            pe.wait_ge(el_cut, 1)

            def sums(r, h, k, bank):
                t = r * RING + k
                if k == 0:
                    pe.wait_ge(m_made, r + 1)
                    pe.wait_ge(s_made, r + 1)
                if later(r, 1) or k >= NB:
                    pe.wait_ge(added, t - NB + 1)
                held(pe, tt)
                nc.tensor.matmul(bank[:, 0:AW], S[:, h, k, :], M[:, h * RING + k, :], start=True, stop=True).then_inc(summed, 1)

            def step(r, h):
                if there(r):
                    for k in range(NB):
                        sums(r, h, k, ps[k])
                if there(r + 2):
                    starts = [pe.snap(b * 12) for b in bins_of_round(nc, m, PE, r + 2)]
                    pe.wait_ge(sb_made, r + 3)
                    if later(r, -1):
                        pe.wait_ge(st_made, r + 2)
                    held(pe, tt)
                    for k in range(RING):
                        tr = nc.tensor.transpose(pst[:, k * P:k * P + P], SB[:, h, k, :], m.ident_bf[:, :])
                    tr.then_inc(turned, 1)
                    pe.wait_ge(st_made, r + 3)
                    if later(r, 0):
                        pe.wait_ge(lk_made, r + 1)
                    held(pe, tt)
                    for j in range(RING):
                        mm = nc.tensor.matmul(pel[h][:, j * 12:j * 12 + 12], ST[:, h, j, :],
                                              cols(el3[:, :, :, :].rearrange("p i c q -> p (i c q)"), starts[j], 12),
                                              start=True, stop=True)
                    mm.then_inc(el_made, 1)
                if there(r):
                    for k in range(NB, RING):
                        sums(r, h, k, ps[k - NB])

            staggered(pe, step)

        @block.vector
        def _(v):
            el = m.EL[:, :].rearrange("p (i q) -> p i q", q=4)
            nc.vector.tensor_copy(el3[:, :, 0, :], el)
            nc.vector.memset(m.ACC[:, :], 0.0)
            v.drain()
            nc.vector.tensor_tensor(rest[:, :, :], el, el3[:, :, 0, :], ALU.subtract)
            v.drain()
            nc.vector.tensor_copy(el3[:, :, 1, :], rest[:, :, :])
            v.drain()
            nc.vector.tensor_tensor(rest[:, :, :], rest[:, :, :], el3[:, :, 1, :], ALU.subtract)
            v.drain()
            nc.vector.tensor_copy(el3[:, :, 2, :], rest[:, :, :])
            v.drain().then_inc(el_cut, 1)

            def add(r, k, bank, start):
                v.drain()
                v.wait_ge(summed, r * RING + k + 1)
                acc = cols(m.ACC, start, AW)
                nc.vector.tensor_tensor(acc, acc, bank[:, 0:AW], ALU.add).then_inc(added, 1)

            def step(r, h):
                if there(r + 2):
                    if later(r, 0):
                        v.wait_ge(s_made, r + 1)
                        v.wait_ge(turned, r + 1)
                        held(v, tv)
                    for k in range(RING):
                        sbk = nc.vector.tensor_scalar(SB[:, h, k, :], m.iota_bf[:, :], cols(m.LOC, (r + 2) * RING + k, 1), None,
                                                      ALU.is_equal)
                    sbk.then_inc(sb_made, 1)
                if there(r + 1):
                    g = 1 - h
                    v.wait_ge(el_made, r + 2)
                    v.wait_ge(got[g], (r + 1 - g) * (8 * RING) + 16 * RING)
                    if later(r, 1):
                        v.wait_ge(e_made, r)
                    held(v, tv)
                    rows = msg[:, g * RING:(g + 1) * RING, :]
                    nc.vector.tensor_reduce(zz[:, g, :, :], pel[g][:, 0:12 * RING].rearrange("p (k c q) -> p k q c", c=3, q=4),
                                            X_AXIS, ALU.add)
                    v.drain()
                    nc.vector.tensor_tensor(zz[:, g, :, :], zz[:, g, :, :], rows[:, :, 64:GW], ALU.add)
                    v.drain()
                    nc.vector.scalar_tensor_tensor(out=lk[:, g, :, :], in0=zz[:, g, :, :], scalar=0.2, in1=zz[:, g, :, :],
                                                   op0=ALU.mult, op1=ALU.max).then_inc(lk_made, 1)
                    v.wait_ge(e_made, r + 2)
                    held(v, tv)
                    Mg = M[:, g * RING:(g + 1) * RING, :]
                    for q in range(4):
                        last = nc.vector.tensor_tensor(Mg[:, :, 64 * q:64 * q + 64], rows[:, :, 0:64],
                                                      Mg[:, :, D + q:D + q + 1].broadcast_to([P, RING, 64]), ALU.mult)
                    last.then_inc(m_made, 1)
                if there(r):
                    starts = [v.snap(b * AW) for b in bins_of_round(nc, m, DVE, r)]
                    for k in range(RING):
                        add(r, k, ps[k % NB], starts[k])

            staggered(v, step)


def stage_heads(nc, m):
    with Stage(nc, "heads") as st:
        rs, o, ex = ([st.sb(f"{n}{s}", [P, w]) for s in range(2)] for n, w in (("rs", 4), ("o", D), ("ex", D)))
        low_made, ex_made, tv, ta = (st.sem(n) for n in ("low_made", "ex_made", "turns_v", "turns_a"))
        block = st.block()

        @block.scalar
        def _(act):
            def exp_tile(i, s, rows):
                act.wait_ge(low_made, i + 1)
                held(act, ta)
                nc.scalar.activation(ex[s][:, :], ex[s][:, :], ACT.Exp).then_inc(ex_made, 1)

            over_tiles(act, exp_tile)

        @block.vector
        def _(v):
            def heads(i, s):
                acc = cols(m.ACC, i * AW, D)
                nc.vector.tensor_scalar(rs[s][:, :], cols(m.ACC, i * AW + D, 4), 1e-12, None, ALU.max)
                v.drain()
                nc.vector.reciprocal(rs[s][:, :], rs[s][:, :])
                v.drain()
                o3 = o[s][:, :].rearrange("p (g j) -> p g j", j=64)
                nc.vector.tensor_tensor(o3, acc.rearrange("p (g j) -> p g j", j=64),
                                        rs[s][:, :].unsqueeze(2).broadcast_to([P, 4, 64]), ALU.mult)
                v.drain()
                nc.vector.tensor_tensor(o3, o3, m.gbr[:, :].unsqueeze(1).broadcast_to([P, 4, 64]), ALU.add)
                v.drain()
                nc.vector.tensor_scalar(ex[s][:, :], o[s][:, :], 0.0, None, ALU.min).then_inc(low_made, 1)

            def finish(i, s):
                v.wait_ge(ex_made, i + 1)
                held(v, tv)
                x = cols(m.X, i * D, D)
                nc.vector.scalar_tensor_tensor(out=o[s][:, :], in0=o[s][:, :], scalar=0.0, in1=ex[s][:, :], op0=ALU.max, op1=ALU.add)
                v.drain()
                nc.vector.scalar_tensor_tensor(out=x, in0=o[s][:, :], scalar=-1.0, in1=x, op0=ALU.add, op1=ALU.add)
                v.drain()

            def out_tile(i, s, rows):
                heads(i, s)
                if not (isinstance(i, int) and i == 0):
                    finish(i - 1, 1 - s)

            over_tiles(v, out_tile)
            finish(TILES - 1, 0)


def stage_router(nc, m):
    with Stage(nc, "router") as st:
        two = lambda n, w: [st.sb(f"{n}{s}", [P, w]) for s in range(2)]
        t, t2, xm, xt = (two(n, D) for n in ("t", "u", "xm", "xt"))
        pt, pl = ([st.ps(f"{n}{s}") for s in range(2)] for n in ("pt", "pl"))
        xm_made, turned, xt_made, l_ps, l_read, zeroed = (
            st.sem(n) for n in ("xm_made", "turned", "xt_made", "l_ps", "l_read", "zeroed"))
        out_xm, zero_out = st.sems("out_xm"), st.sem("zero_out")
        tv, ta, tt, ts = (st.sem(n) for n in ("turns_v", "turns_a", "turns_t", "turns_s"))
        zrow = st.sb("zrow", [P, 2 * D])
        block = st.block()

        @block.gpsimd
        def _(pool):
            nc.gpsimd.memset(zrow[:, :], 0.0).then_inc(zeroed, 1)

        @block.vector
        def _(v):
            def norm(i, s):
                nc.vector.tensor_scalar(t[s][:, :], cols(m.X, i * D, D), cols(m.mean, i, 1), cols(m.rstd, i, 1),
                                        ALU.subtract, ALU.mult)
                v.drain()
                nc.vector.tensor_tensor(t2[s][:, :], t[s][:, :], m.gammar[:, :], ALU.mult)
                if reused(i):
                    v.wait_ge(turned, i - 1)
                    v.wait_ge(out_xm[s], dma_count_before(i, s))
                    held(v, tv)
                v.drain()
                nc.vector.tensor_tensor(xm[s][:, :], t2[s][:, :], m.betar[:, :], ALU.add).then_inc(xm_made, 1)

            def logits(i, s):
                v.wait_ge(l_ps, i + 1)
                held(v, tv)
                nc.vector.tensor_tensor(cols(m.L, i * EXPERTS, EXPERTS), pl[s][:, 0:EXPERTS], m.rbr[:, :], ALU.add).then_inc(l_read, 1)

            def step(i, s):
                if there(i + 1):
                    norm(i + 1, 1 - s)
                if there(i - 1):
                    logits(i - 1, 1 - s)

            skewed(v, 1, step)

        @block.scalar
        def _(act):
            def tile(i, s, rows):
                act.wait_ge(turned, i + 1)
                if reused(i):
                    act.wait_ge(l_ps, i - 1)
                held(act, ta)
                nc.scalar.copy(xt[s][:, :], pt[s][:, 0:D]).then_inc(xt_made, 1)

            over_tiles(act, tile)

        @block.tensor
        def _(pe):
            def turn(i, s):
                pe.wait_ge(xm_made, i + 1)
                if reused(i):
                    pe.wait_ge(xt_made, i - 1)
                held(pe, tt)
                for c in range(2):
                    tr = nc.tensor.transpose(pt[s][:, c * P:c * P + P], xm[s][:, c * P:c * P + P], m.ident[:, :])
                tr.then_inc(turned, 1)

            def tile(i, s, rows):
                if isinstance(i, int) and i == 0:
                    turn(0, 0)
                if not (isinstance(i, int) and i == TILES - 1):
                    turn(i + 1, 1 - s)
                pe.wait_ge(xt_made, i + 1)
                if reused(i):
                    pe.wait_ge(l_read, i - 1)
                held(pe, tt)
                for c in range(2):
                    mm = nc.tensor.matmul(pl[s][:, 0:EXPERTS], xt[s][:, c * P:c * P + P], m.rWs[:, c, :], start=(c == 0), stop=(c == 1))
                mm.then_inc(l_ps, 1)

            over_tiles(pe, tile)

        @block.sync
        def _(sp):
            sp.wait_ge(zeroed, 1)
            rows = m.expert_in.rearrange("(t p a) d -> t p (a d)", p=P, a=2)
            for k in range(EX_TILES // 2):
                sp.dma_start(rows[k], zrow[:, :]).then_inc(zero_out, 16)

            def tile(i, s, n):
                sp.wait_ge(xm_made, i + 1)
                held(sp, ts)
                sp.dma_start(m.xm[bass.ds(i * P, P), :], xm[s][:, :]).then_inc(out_xm[s], 16)

            over_tiles(sp, tile)
            for s in range(2):
                sp.wait_ge(out_xm[s], dma_count(TILES - 1 - s, s))
            sp.wait_ge(zero_out, 16 * (EX_TILES // 2))


def stage_route(nc, m):
    with Stage(nc, "route") as st:
        T8 = [P, TILES, EXPERTS]
        l3 = m.L[:, :].rearrange("p (i e) -> p i e", e=EXPERTS)
        cand, oh1, oh2, both, pre, scan, other, l2 = (st.sb(n, T8) for n in ("cand", "oh1", "oh2", "both", "pre", "scan", "other", "l2"))
        m1, m2, i1, pr = (st.sb(n, [P, TILES]) for n in ("m1", "m2", "i1", "pr"))
        valid = st.sb("valid", [P, 1])
        cnt, nt, te, tx, sp8 = (st.sb(n, [P, EXPERTS]) for n in ("cnt", "nt", "te", "tx", "sp8"))
        ni = st.sb("ni", [P, EXPERTS], I32)
        cmp = st.sb("cmp", [1, P, EXPERTS])
        exf = st.sb("exf", [1, P])
        pre_ps, tot_ps = st.ps("pre_ps"), st.ps("tot_ps")
        diff, powed, oh_made, counted = (st.sem(n) for n in ("diff", "powed", "oh_made", "counted"))
        block = st.block()
        f = lambda t: t[:, :, :].rearrange("p i e -> p (i e)")
        over = lambda t: t.unsqueeze(2).broadcast_to(T8)
        exps = m.iota_row[:, 0:EXPERTS].unsqueeze(1).broadcast_to(T8)

        @block.vector
        def _(v):
            def pick(logits, best, chosen):
                nc.vector.tensor_reduce(best[:, :], logits, X_AXIS, ALU.max)
                v.drain()
                nc.vector.tensor_tensor(cand[:, :, :], logits, over(best[:, :]), ALU.is_equal)
                v.drain()
                nc.vector.tensor_scalar(cand[:, :, :], cand[:, :, :], -float(EXPERTS), float(EXPERTS), ALU.mult, ALU.add)
                v.drain()
                nc.vector.tensor_tensor(cand[:, :, :], cand[:, :, :], exps, ALU.add)
                v.drain()
                nc.vector.tensor_reduce(i1[:, :], cand[:, :, :], X_AXIS, ALU.min)
                v.drain()
                nc.vector.tensor_tensor(chosen[:, :, :], exps, over(i1[:, :]), ALU.is_equal)
                v.drain()

            pick(l3, m1, oh1)
            nc.vector.scalar_tensor_tensor(out=l2[:, :, :], in0=oh1[:, :, :], scalar=-3.0e38, in1=l3, op0=ALU.mult, op1=ALU.add)
            v.drain()
            pick(l2[:, :, :], m2, oh2)
            nc.vector.tensor_tensor(pr[:, :], m2[:, :], m1[:, :], ALU.subtract)
            v.drain().then_inc(diff, 1)
            nc.vector.tensor_scalar(valid[:, :], m.slot_no[:, 0:1], float(TAIL), None, ALU.is_lt)
            nc.vector.tensor_tensor(both[:, :, :], oh1[:, :, :], oh2[:, :, :], ALU.add)
            v.drain()
            nc.vector.tensor_scalar(both[:, TILES - 1, :], both[:, TILES - 1, :], valid[:, :], None, ALU.mult)
            v.drain().then_inc(oh_made, 1)
            v.wait_ge(powed, 1)
            nc.vector.tensor_scalar(m1[:, :], pr[:, :], 1.0, None, ALU.add)
            v.drain()
            nc.vector.reciprocal(m.gate[:, 0, :], m1[:, :])
            v.drain()
            nc.vector.tensor_tensor(m.gate[:, 1, :], m.gate[:, 0, :], pr[:, :], ALU.mult)
            v.wait_ge(counted, 1)
            nc.vector.tensor_copy(f(pre), pre_ps[:, 0:TILES * EXPERTS])
            nc.vector.tensor_copy(f(scan), tot_ps[:, 0:TILES * EXPERTS])
            v.drain()
            nc.vector.tensor_tensor(f(pre), f(pre), f(scan), ALU.subtract)
            a, b, w = scan, other, 1
            while w < TILES:
                v.drain()
                nc.vector.tensor_tensor(b[:, w:TILES, :], a[:, w:TILES, :], a[:, 0:TILES - w, :], ALU.add)
                nc.vector.tensor_copy(b[:, 0:w, :], a[:, 0:w, :])
                a, b, w = b, a, 2 * w
            v.drain()
            nc.vector.tensor_scalar(cnt[:, :], a[:, TILES - 1, :], float(P - 1), None, ALU.add)
            nc.vector.tensor_tensor(pre[:, :, :], pre[:, :, :], a[:, :, :], ALU.add)
            v.drain()
            nc.vector.tensor_copy(ni[:, :], cnt[:, :])
            v.drain()
            nc.vector.tensor_scalar(ni[:, :], ni[:, :], 7, None, ALU.logical_shift_right)
            v.drain()
            nc.vector.tensor_copy(nt[:, :], ni[:, :])
            nc.vector.tensor_copy(te[:, :], ni[:, :])
            x, y, w = te, tx, 1
            while w < EXPERTS:
                v.drain()
                nc.vector.tensor_tensor(y[:, w:EXPERTS], x[:, w:EXPERTS], x[:, 0:EXPERTS - w], ALU.add)
                nc.vector.tensor_copy(y[:, 0:w], x[:, 0:w])
                x, y, w = y, x, 2 * w
            v.drain()
            nc.vector.tensor_tensor(sp8[:, :], x[:, :], nt[:, :], ALU.subtract)
            nc.vector.tensor_tensor(cmp[:, :, :], x[0:1, :].unsqueeze(1).broadcast_to([1, P, EXPERTS]),
                                    m.iota_row[0:1, :].unsqueeze(2).broadcast_to([1, P, EXPERTS]), ALU.is_le)
            v.drain()
            nc.vector.tensor_reduce(exf[:, :], cmp[:, :, :], X_AXIS, ALU.add)
            nc.vector.tensor_scalar(sp8[:, :], sp8[:, :], float(P), None, ALU.mult)
            v.drain()
            nc.vector.tensor_scalar(exf[:, :], exf[:, :], float(EXPERTS - 1), None, ALU.min)
            nc.vector.tensor_tensor(pre[:, :, :], pre[:, :, :], sp8[:, :].unsqueeze(1).broadcast_to(T8), ALU.add)
            v.drain()
            nc.vector.tensor_copy(m.exp_row[:, :], exf[:, :])
            for k, oh in enumerate((oh1, oh2)):
                nc.vector.tensor_tensor(cand[:, :, :], pre[:, :, :], oh[:, :, :], ALU.mult)
                v.drain()
                nc.vector.tensor_reduce(i1[:, :], cand[:, :, :], X_AXIS, ALU.add)
                v.drain()
                nc.vector.tensor_copy(m.pos_i[:, k, :], i1[:, :])
                v.drain()

        @block.scalar
        def _(act):
            act.wait_ge(diff, 1)
            nc.scalar.activation(pr[:, :], pr[:, :], ACT.Exp).then_inc(powed, 1)

        @block.tensor
        def _(pe):
            pe.wait_ge(oh_made, 1)
            nc.tensor.matmul(pre_ps[:, 0:TILES * EXPERTS], m.tri[:, :], f(both), start=True, stop=True)
            nc.tensor.matmul(tot_ps[:, 0:TILES * EXPERTS], m.ones[:, :], f(both), start=True, stop=True)
            pe.drain().then_inc(counted, 1)


def stage_dispatch(nc, m):
    with Stage(nc, "dispatch") as st:
        xm = [st.sb(f"xm{s}", [P, D]) for s in range(2)]
        at = [st.sb(f"at{s}", [P, 2], I32) for s in range(2)]
        xm_in, at_made, sent, w_in = st.sems("xm_in"), st.sem("at_made"), st.sems("sent"), st.sem("w_in")
        ta, tp, ts = (st.sem(n) for n in ("turns_a", "turns_p", "turns_s"))
        block = st.block()

        @block.sync
        def _(sp):
            def load(i, s, rows):
                if reused(i):
                    sp.wait_ge(sent[s], 2 * dma_count_before(i, s))
                    held(sp, ts)
                sp.dma_start(xm[s][:, :], m.xm[bass.ds(i * P, P), :]).then_inc(xm_in[s], 16)

            over_tiles(sp, load)
            n = 0
            for e in range(EXPERTS):
                for t, w, width in ((m.W1E, m.eW1, 2 * HID), (m.W2E, m.eW2, 4 * D)):
                    c = width // w.shape[2]
                    sp.dma_start(t[:, e * width:(e + 1) * width].rearrange("p (c n) -> p c n", c=c),
                                 w[e].rearrange("(c p) n -> p c n", p=P)).then_inc(w_in, 16)
                    n += 16
            sp.dma_start(m.B1E[:, :], row_to_all(m.eb1.rearrange("e n -> (e n)"))).then_inc(w_in, 16)
            sp.dma_start(m.B2E[:, :], row_to_all(m.eb2.rearrange("e n -> (e n)"))).then_inc(w_in, 16)
            sp.wait_ge(w_in, n + 32)

        @block.scalar
        def _(act):
            def tile(i, s, rows):
                if reused(i):
                    act.wait_ge(sent[s], 2 * dma_count_before(i, s))
                    held(act, ta)
                nc.scalar.copy(at[s][:, 0:1], cols(m.pos_i[:, 0, :], i, 1))
                nc.scalar.copy(at[s][:, 1:2], cols(m.pos_i[:, 1, :], i, 1))
                act.drain().then_inc(at_made, 1)

            over_tiles(act, tile)

        @block.gpsimd
        def _(pool):
            def tile(i, s, rows):
                pool.wait_ge(at_made, i + 1)
                pool.wait_ge(xm_in[s], dma_count(i, s))
                held(pool, tp)
                for k in range(2):
                    pool.indirect_dma_start(m.expert_in, bass.IndirectOffsetOnAxis(ap=at[s][0:rows, k:k + 1], axis=0),
                                            xm[s][0:rows, :], None).then_inc(sent[s], 16)

            over_tiles(pool, tile)
            for s in range(2):
                pool.wait_ge(sent[s], 2 * dma_count(TILES - 1 - s, s))


def stage_experts(nc, m):
    with Stage(nc, "experts") as st:
        two = lambda n, w: [st.sb(f"{n}{s}", [P, w]) for s in range(2)]
        xe, xt, hb, hg, ht, y = two("xe", D), two("xt", D), two("hb", HID), two("hg", HID), two("ht", HID), two("y", D)
        pt, ph, pg, po = ([st.ps(f"{n}{s}") for s in range(2)] for n in ("pt", "ph", "pg", "po"))
        x_in, turned, xt_made, h_ps, hb_made, hg_made, h_turned, ht_made, y_ps, y_made, stored = (
            st.sems("x_in"), *(st.sem(n) for n in ("turned", "xt_made", "h_ps", "hb_made", "hg_made", "h_turned",
                                                   "ht_made", "y_ps", "y_made")), st.sems("stored"))
        tv, ta, tt, ts = (st.sem(n) for n in ("turns_v", "turns_a", "turns_t", "turns_s"))
        block = st.block()
        first = lambda t: isinstance(t, int) and t == 0

        def expert(eng, t):
            return eng.value_load(m.exp_row[0:1, bass.ds(t, 1)], min_val=0, max_val=EXPERTS - 1)

        @block.sync
        def _(sp):
            def store(t, s):
                sp.wait_ge(y_made, t + 1)
                held(sp, ts)
                sp.dma_start(m.expert_out[bass.ds(t * P, P), :], y[s][:, :]).then_inc(stored[s], 16)

            def tile(t, s):
                if reused(t):
                    sp.wait_ge(turned, t - 1)
                    held(sp, ts)
                sp.dma_start(xe[s][:, :], m.expert_in[bass.ds(t * P, P), :]).then_inc(x_in[s], 16)
                if reused(t):
                    store(t - 2, s)

            in_twos(sp, EX_TILES, tile)
            store(EX_TILES - 2, 0)
            store(EX_TILES - 1, 1)
            for s in range(2):
                sp.wait_ge(stored[s], EX_TILES * 8)

        @block.tensor
        def _(pe):
            def second(t, s):
                pe.wait_ge(hg_made, t + 1)
                if reused(t):
                    pe.wait_ge(ht_made, t - 1)
                held(pe, tt)
                for c in range(4):
                    tr = nc.tensor.transpose(pg[s][:, c * P:c * P + P], hg[s][:, c * P:c * P + P], m.ident[:, :])
                tr.then_inc(h_turned, 1)

            def third(t, s):
                e = expert(pe, t)
                pe.wait_ge(ht_made, t + 1)
                if reused(t):
                    pe.wait_ge(y_made, t - 1)
                held(pe, tt)
                for c in range(4):
                    mm = nc.tensor.matmul(po[s][:, 0:D], ht[s][:, c * P:c * P + P], cols(m.W2E, e * (4 * D) + c * D, D),
                                          start=(c == 0), stop=(c == 3))
                mm.then_inc(y_ps, 1)

            def tile(t, s):
                pe.wait_ge(x_in[s], dma_count(t, s))
                if reused(t):
                    pe.wait_ge(xt_made, t - 1)
                held(pe, tt)
                for c in range(2):
                    tr = nc.tensor.transpose(pt[s][:, c * P:c * P + P], xe[s][:, c * P:c * P + P], m.ident[:, :])
                tr.then_inc(turned, 1)
                if not first(t):
                    second(t - 1, 1 - s)
                e = expert(pe, t)
                pe.wait_ge(xt_made, t + 1)
                if reused(t):
                    pe.wait_ge(hb_made, t - 1)
                held(pe, tt)
                for c in range(2):
                    mm = nc.tensor.matmul(ph[s][:, :], xt[s][:, c * P:c * P + P], cols(m.W1E, e * (2 * HID) + c * HID, HID),
                                          start=(c == 0), stop=(c == 1))
                mm.then_inc(h_ps, 1)
                if not first(t):
                    third(t - 1, 1 - s)

            in_twos(pe, EX_TILES, tile)
            second(EX_TILES - 1, 1)
            third(EX_TILES - 1, 1)

        @block.scalar
        def _(act):
            def turned_h(t, s):
                act.wait_ge(h_turned, t + 1)
                if reused(t):
                    act.wait_ge(y_ps, t - 1)
                held(act, ta)
                nc.scalar.copy(ht[s][:, :], pg[s][:, :]).then_inc(ht_made, 1)

            def tile(t, s):
                act.wait_ge(turned, t + 1)
                if reused(t):
                    act.wait_ge(h_ps, t - 1)
                held(act, ta)
                nc.scalar.copy(xt[s][:, :], pt[s][:, 0:D]).then_inc(xt_made, 1)
                if not first(t):
                    turned_h(t - 1, 1 - s)
                act.wait_ge(hb_made, t + 1)
                if reused(t):
                    act.wait_ge(h_turned, t - 1)
                held(act, ta)
                nc.scalar.activation(hg[s][:, :], hb[s][:, :], ACT.Gelu).then_inc(hg_made, 1)

            in_twos(act, EX_TILES, tile)
            turned_h(EX_TILES - 1, 1)

        @block.vector
        def _(v):
            def out(t, s):
                e = expert(v, t)
                v.wait_ge(y_ps, t + 1)
                if reused(t):
                    v.wait_ge(stored[s], dma_count_before(t, s))
                held(v, tv)
                nc.vector.tensor_tensor(y[s][:, :], po[s][:, 0:D], cols(m.B2E, e * D, D), ALU.add).then_inc(y_made, 1)

            def tile(t, s):
                e = expert(v, t)
                v.wait_ge(h_ps, t + 1)
                if reused(t):
                    v.wait_ge(hg_made, t - 1)
                held(v, tv)
                nc.vector.tensor_tensor(hb[s][:, :], ph[s][:, :], cols(m.B1E, e * HID, HID), ALU.add).then_inc(hb_made, 1)
                if not first(t):
                    out(t - 1, 1 - s)

            in_twos(v, EX_TILES, tile)
            out(EX_TILES - 1, 1)


def stage_combine(nc, m):
    with Stage(nc, "combine") as st:
        y1, y2, o = ([st.sb(f"{n}{s}", [P, D]) for s in range(2)] for n in ("y1", "y2", "o"))
        at = [st.sb(f"at{s}", [P, 2], I32) for s in range(2)]
        at_made, got, out_made, stored = st.sem("at_made"), st.sems("got"), st.sem("out_made"), st.sems("stored")
        tv, ta, tp, ts = (st.sem(n) for n in ("turns_v", "turns_a", "turns_p", "turns_s"))
        block = st.block()

        @block.scalar
        def _(act):
            def tile(i, s, rows):
                if reused(i):
                    act.wait_ge(out_made, i - 1)
                    held(act, ta)
                nc.scalar.copy(at[s][:, 0:1], cols(m.pos_i[:, 0, :], i, 1))
                nc.scalar.copy(at[s][:, 1:2], cols(m.pos_i[:, 1, :], i, 1))
                act.drain().then_inc(at_made, 1)

            over_tiles(act, tile)

        @block.gpsimd
        def _(pool):
            def tile(i, s, rows):
                pool.wait_ge(at_made, i + 1)
                if reused(i):
                    pool.wait_ge(out_made, i - 1)
                held(pool, tp)
                for k, y in enumerate((y1, y2)):
                    pool.indirect_dma_start(y[s][0:rows, :], None, m.expert_out,
                                            bass.IndirectOffsetOnAxis(ap=at[s][0:rows, k:k + 1], axis=0)).then_inc(got[s], 16)

            over_tiles(pool, tile)

        @block.vector
        def _(v):
            def tile(i, s, rows):
                v.wait_ge(got[s], 2 * dma_count(i, s))
                if reused(i):
                    v.wait_ge(stored[s], dma_count_before(i, s))
                held(v, tv)
                x = m.X[0:rows, bass.ds(i * D, D)]
                nc.vector.scalar_tensor_tensor(out=y1[s][0:rows, :], in0=y1[s][0:rows, :], scalar=m.gate[0:rows, 0, bass.ds(i, 1)],
                                               in1=x, op0=ALU.mult, op1=ALU.add)
                v.drain()
                nc.vector.scalar_tensor_tensor(out=o[s][0:rows, :], in0=y2[s][0:rows, :], scalar=m.gate[0:rows, 1, bass.ds(i, 1)],
                                               in1=y1[s][0:rows, :], op0=ALU.mult, op1=ALU.add).then_inc(out_made, 1)

            over_tiles(v, tile)

        @block.sync
        def _(sp):
            def tile(i, s, rows):
                sp.wait_ge(out_made, i + 1)
                held(sp, ts)
                sp.dma_start(m.out[bass.ds(i * P, rows), :], o[s][0:rows, :]).then_inc(stored[s], 16)

            over_tiles(sp, tile)
            for s in range(2):
                sp.wait_ge(stored[s], dma_count(TILES - 1 - s, s))


class Memory:
    pass


def stages_before_attention(nc, m, dense):
    def sb(name, shape, dt=F32):
        return dense.enter_context(nc.sbuf_tensor(name, shape, dt))

    m.next_i = sb("next_i", [LANES, 1], I32)
    m.unsorted = sb("unsorted", [1, 1], I32)
    m.key = sb("key", [LANES, COLS])
    m.rank_i = sb("rank_i", [LANES, COLS], I32)
    m.base = sb("base", [P, CH, TILES])
    m.off_i, m.bin_f = sb("off_i", [P, SC], I32), sb("bin_f", [P, SC])
    m.kvbd = sb("kvbd", [P, 2, P + 4])
    m.wqs, m.woT, m.fT, m.w11s, m.w12s, m.w21s, m.w22s, m.wouts, m.mixM = (
        sb(n, [P, 2, D]) for n in ("wqs", "woT", "fT", "w11s", "w12s", "w21s", "w22s", "wouts", "mixM"))
    m.wkvT = sb("wkvT", [P, 2, 2 * D])
    m.wqkvs = sb("wqkvs", [P, 2, 3 * D])
    m.kv_sum, m.v_sum = sb("kv_sum", [P, 2 * (P + 1)]), sb("v_sum", [P, 2 * (P + 1)])
    m.gcat = sb("gcat", [P, 2, 72])
    m.b11s, m.b21s = (sb(n, [P, 2]) for n in ("b11s", "b21s"))
    m.b12r, m.b22r, m.bor, m.fbr, m.boutr, m.mw2r = (
        sb(n, [P, D]) for n in ("b12r", "b22r", "bor", "fbr", "boutr", "mw2r"))
    m.kgp, m.kbp = sb("kgp", [P, 1]), sb("kbp", [P, 1])
    m.vgr, m.vbr = sb("vgr", [P, P]), sb("vbr", [P, P])

    stage_load(nc, m)
    stage_count(nc, m, m.dst_i, 0)
    stage_sort_if_unsorted(nc, m)
    stage_slots(nc, m, 0)
    stage_count(nc, m, m.src_i, 1)
    stage_stats(nc, m, "stats0", 1e-5)
    stage_norm(nc, m)
    stage_conv(nc, m, "conv1", m.relu_xn_table, True, False)
    stage_mlp(nc, m, "mlp1", m.w11s, m.b11s, m.w12s, m.b12r, False, (0, 144))
    stage_conv(nc, m, "conv2", m.conv1_table, False, True)
    stage_mix(nc, m)
    stage_mlp(nc, m, "mlp2", m.w21s, m.b21s, m.w22s, m.b22r, True, (144, 144))
    stage_stats(nc, m, "stats1", 1e-5)
    stage_ffn(nc, m, (288, 176))
    stage_stats(nc, m, "stats2", 1e-5, with_rms=True)
    stage_attn_kv(nc, m, (464, 176))
    stage_attn_q(nc, m, (640, 160))
    stage_attn_add(nc, m)
    stage_slots(nc, m, 1)


def stages(nc, m):
    with ExitStack() as graph:
        def sb(name, shape, dt=F32):
            return graph.enter_context(nc.sbuf_tensor(name, shape, dt))

        m.src_i, m.dst_i, m.packed = (
            sb(n, [LANES, COLS], I32) for n in ("src_i", "dst_i", "packed"))
        m.GI = sb("GI", [P, SC * P], I32)
        m.LOC = sb("LOC", [P, SC * P])
        m.bin_row = sb("bin_row", [1, SC * P], I32)
        m.ACC = sb("ACC", [P, TILES * AW])
        m.EL = sb("EL", [P, TILES * 4])
        m.gbr = sb("gbr", [P, 64])
        with ExitStack() as dense:
            stages_before_attention(nc, m, dense)
        stage_gat(nc, m)
        stage_heads(nc, m)
        stage_stats(nc, m, "stats3", 1e-5)
    with ExitStack() as experts:
        def sb(name, shape, dt=F32):
            return experts.enter_context(nc.sbuf_tensor(name, shape, dt))

        m.L = sb("L", [P, TILES * EXPERTS])
        m.pos_i = sb("pos_i", [P, 2, TILES], I32)
        m.gate = sb("gate", [P, 2, TILES])
        m.exp_row = sb("exp_row", [1, P], I32)
        m.W1E = sb("W1E", [P, EXPERTS * 2 * HID])
        m.W2E = sb("W2E", [P, EXPERTS * 4 * D])
        m.B1E = sb("B1E", [P, EXPERTS * HID])
        m.B2E = sb("B2E", [P, EXPERTS * D])
        stage_router(nc, m)
        stage_route(nc, m)
        stage_dispatch(nc, m)
        stage_experts(nc, m)
        stage_combine(nc, m)



def gps_program(nc, args, out):
    with ExitStack() as ctx:
        m = Memory()
        (m.x, m.src, m.dst, m.w11, m.b11, m.w12, m.b12, m.w21, m.b21, m.w22, m.b22, m.wq, m.wk, m.wv, m.wo, m.bo,
         m.kg, m.kb, m.vg, m.vb, m.fw, m.fb, m.gW, m.gWl, m.gWr, m.gb, m.mw1, m.wqkv, m.wout, m.bout, m.mw2, m.gamma,
         m.beta, m.rW, m.rb, m.eW1, m.eb1, m.eW2, m.eb2, m.out) = (*args, out)

        def sb(name, shape, dt=F32):
            return ctx.enter_context(nc.sbuf_tensor(name, shape, dt))

        def dram(name, shape, dt=F32):
            return nc.dram_tensor(name, shape, dt).ap()

        m.relu_xn_table = dram("relu_xn_table", [NPAD, D])
        m.conv1_table = dram("conv1_table", [NPAD, D])
        m.attn_table = dram("attn_table", [NPAD, GW])
        m.xnT = dram("xnT", [NPAD, D])
        m.xrT = dram("xrT", [NPAD, D])
        m.xm = dram("xm", [NPAD, D])
        m.expert_in = dram("expert_in", [EX_TILES * P, D])
        m.expert_out = dram("expert_out", [EX_TILES * P, D])
        m.edges = [nc.dram_tensor(f"edges_by_{e}", [EDGE_ROOM], I32).ap() for e in ("dst", "src")]
        m.bin_dram = [nc.dram_tensor(f"bins_by_{e}", [SC * P], I32).ap() for e in ("dst", "src")]

        m.X = sb("X", [P, TILES * D])
        m.ident = sb("ident", [P, P])
        m.iota_row = sb("iota_row", [P, P])
        m.slot_no = sb("slot_no", [P, SC])
        m.tri = sb("tri", [P, P])
        m.ones = sb("ones", [P, P])
        m.zeros = sb("zeros", [P, 2 * AW])
        m.mask64 = sb("mask64", [P, P])
        m.mask32 = sb("mask32", [P, P])
        m.tri_bf, m.rest_bf, m.ones_bf = (
            sb(n, [P, P], BF16) for n in ("tri_bf", "rest_bf", "ones_bf"))
        m.ident_bf, m.iota_bf = (
            sb(n, [P, P], BF16) for n in ("ident_bf", "iota_bf"))
        m.zeros_bf = sb("zeros_bf", [P, 512], BF16)
        m.gammar, m.betar = (
            sb(n, [P, D]) for n in ("gammar", "betar"))
        m.rbr = sb("rbr", [P, EXPERTS])
        m.rWs = sb("rWs", [P, 2, EXPERTS])
        m.mean, m.rstd, m.rms_in, m.rms_out = (
            sb(n, [P, TILES]) for n in ("mean", "rstd", "rms_in", "rms_out"))

        stages(nc, m)


_INS = ['x', 'src', 'dst', 'L0_gnn_w11', 'L0_gnn_b11', 'L0_gnn_w12', 'L0_gnn_b12', 'L0_gnn_w21', 'L0_gnn_b21',
        'L0_gnn_w22', 'L0_gnn_b22', 'L0_mix_wq', 'L0_mix_wk', 'L0_mix_wv', 'L0_mix_wo', 'L0_mix_bo', 'L0_mix_ln_k_g',
        'L0_mix_ln_k_b', 'L0_mix_ln_v_g', 'L0_mix_ln_v_b', 'L0_ffn_weight', 'L0_ffn_bias', 'L1_gnn_W', 'L1_gnn_Wl',
        'L1_gnn_Wr', 'L1_gnn_b', 'L1_mix_w_norm1', 'L1_mix_w_qkv', 'L1_mix_w_out', 'L1_mix_b_out', 'L1_mix_w_norm2',
        'L1_ffn_gamma', 'L1_ffn_beta', 'L1_ffn_Wr', 'L1_ffn_br', 'L1_ffn_W1', 'L1_ffn_b1', 'L1_ffn_W2', 'L1_ffn_b2']


def kernel(**inputs):
    import numpy as _np
    import concourse.bacc as _bacc
    from concourse import mybir as _mybir
    from concourse.bass_utils import run_bass_kernel_spmd as _run

    nc = _bacc.Bacc("TRN2", target_bir_lowering=False, num_devices=1)
    arrays, args = {}, []
    for name in _INS:
        a = _np.ascontiguousarray(inputs[name])
        arrays[f"in_{name}_dram"] = a
        args.append(nc.dram_tensor(f"in_{name}_dram", a.shape, _mybir.dt.from_np(a.dtype), kind="ExternalInput").ap())
    out = nc.dram_tensor("out_0_dram", (N, D), F32, kind="ExternalOutput").ap()
    gps_program(nc, args, out)
    r = _run(nc, [arrays], core_ids=[0])
    return r.results[0]["out_0_dram"]
```
